# Optimizing a Trainium2 kernel written in Bass

```python
import numpy as np
import jax
import jax.numpy as jnp

def _softmax(x, axis=-1):
    return jax.nn.softmax(x, axis=axis)

def _gelu(x):
    return jax.nn.gelu(x, approximate=True)

def _silu(x):
    return jax.nn.silu(x)

def _sigmoid(x):
    return jax.nn.sigmoid(x)

def _layernorm(x, axis=-1, eps=1e-05):
    m = jnp.mean(x, axis=axis, keepdims=True)
    v = jnp.var(x, axis=axis, keepdims=True)
    return (x - m) / jnp.sqrt(v + eps)

def _scatter_add(tgt, idx, src, axis=0):
    return tgt.at[idx].add(src)

def _segment_sum(src, seg, n):
    return jax.ops.segment_sum(src, seg, n)
kernel_name = 'mk_xattn_seq_d2_seqx_r2_9c2c71'

def setup_inputs(seed: int=0):
    np.random.seed(seed)
    _w = jnp.asarray

    def _rec_inputs():
        import jax
        import jax.numpy as jnp
        _rk = jax.random.key(seed)
        x = -0.0002928 + 1 * jax.random.normal(jax.random.fold_in(_rk, 1), (2, 1024, 512), jnp.float32)
        _lenS = 1024 - jax.random.randint(jax.random.fold_in(_rk, 7), (2,), 0, max(1, 1024 // 4) + 1, jnp.int32)
        _lenS2 = 2048 - jax.random.randint(jax.random.fold_in(_rk, 8), (2,), 0, max(1, 2048 // 4) + 1, jnp.int32)
        _ctx_1024P = jax.random.normal(jax.random.fold_in(_rk, 11), (2, 16, 512), jnp.float32)
        _ctx_1024c = jax.random.dirichlet(jax.random.fold_in(_rk, 511), 0.3 * jnp.ones((16,), jnp.float32), (2, 2048))
        _ctx_1024t = jnp.einsum('bsk,bkd->bsd', _ctx_1024c, _ctx_1024P)
        _ctx_1024t = _ctx_1024t * jax.lax.rsqrt(jnp.mean(jnp.square(_ctx_1024t)) + 1e-12) * 0.953939
        ctx_1024 = -1.52775e-05 + 0.999936 * (_ctx_1024t + 0.3 * jax.random.normal(jax.random.fold_in(_rk, 611), (2, 2048, 512), jnp.float32))
        _validS = jnp.arange(1024)[None, :] < _lenS[:, None]
        _validS2 = jnp.arange(2048)[None, :] < _lenS2[:, None]
        _causal = jnp.tril(jnp.ones((1024, 1024), dtype=bool))
        mask_1x1xSxS_ik0 = jnp.where(jnp.broadcast_to(_validS[0:1, None, None, :], (1, 1, 1024, 1024)), 0, 1).astype(jnp.int32)
        return (x, ctx_1024, mask_1x1xSxS_ik0)
    x, ctx_1024, mask_1x1xSxS_ik0 = _rec_inputs()

    def _L0_xattn_setup():
        import jax, jax.numpy as jnp
        import numpy as np
        DIM = 512
        NUM_HEADS = 16
        HEAD_DIM = DIM // NUM_HEADS
        FF = 4 * DIM
        B, T, S = (8, 256, 2048)

        def _perceiver_layer(x, inp, Wq, bq, Wk, bk, Wv, bv, Wo, bo, W1, b1, W2, b2):
            b, t, _ = x.shape
            s = inp.shape[1]
            q = (x @ Wq + bq).reshape(b, t, NUM_HEADS, HEAD_DIM)
            k = (inp @ Wk + bk).reshape(b, s, NUM_HEADS, HEAD_DIM)
            v = (inp @ Wv + bv).reshape(b, s, NUM_HEADS, HEAD_DIM)
            attn = jnp.einsum('bthd,bshd->bhts', q, k)
            attn = jax.nn.softmax(attn / jnp.sqrt(jnp.float32(HEAD_DIM)), axis=-1)
            out = jnp.einsum('bhts,bshd->bthd', attn, v).reshape(b, t, DIM)
            attn_out = out @ Wo + bo
            x = x + attn_out
            h = jax.nn.gelu(x @ W1 + b1, approximate=True)
            x = x + (h @ W2 + b2)
            return x
        key = jax.random.key(seed)
        ks = jax.random.split(key, 14)
        sc = 1.0 / np.sqrt(DIM)
        inp = {'x': jax.random.normal(ks[0], (B, T, DIM), jnp.float32), 'inp': jax.random.normal(ks[1], (B, S, DIM), jnp.float32), 'Wq': jax.random.normal(ks[2], (DIM, DIM), jnp.float32) * sc, 'bq': jnp.zeros((DIM,), jnp.float32), 'Wk': jax.random.normal(ks[3], (DIM, DIM), jnp.float32) * sc, 'bk': jnp.zeros((DIM,), jnp.float32), 'Wv': jax.random.normal(ks[4], (DIM, DIM), jnp.float32) * sc, 'bv': jnp.zeros((DIM,), jnp.float32), 'Wo': jax.random.normal(ks[5], (DIM, DIM), jnp.float32) * sc, 'bo': jnp.zeros((DIM,), jnp.float32), 'W1': jax.random.normal(ks[6], (DIM, FF), jnp.float32) * sc, 'b1': jnp.zeros((FF,), jnp.float32), 'W2': jax.random.normal(ks[7], (FF, DIM), jnp.float32) * (1.0 / np.sqrt(FF)), 'b2': jnp.zeros((DIM,), jnp.float32)}
        return inp
    _L0_xattn_all = _L0_xattn_setup()
    _L0_xattn_in = {k: v for k, v in _L0_xattn_all.items() if k in ('Wq', 'bq', 'Wk', 'bk', 'Wv', 'bv', 'Wo', 'bo', 'W1', 'b1', 'W2', 'b2')}
    del _L0_xattn_all

    def _L1_xattn_setup():
        import jax, jax.numpy as jnp
        import numpy as np
        D_MODEL = 512
        NHEAD = 16
        D_FF = 2048
        B = 2
        S = 1024
        EPS = 1e-05

        def _mha(q_in, k_in, v_in, qw, qb, kw, kb, vw, vb, ow, ob, mask):
            b, sq, d = q_in.shape
            sk = k_in.shape[1]
            hd = d // NHEAD
            q = (q_in @ qw + qb).reshape(b, sq, NHEAD, hd).transpose(0, 2, 1, 3)
            k = (k_in @ kw + kb).reshape(b, sk, NHEAD, hd).transpose(0, 2, 1, 3)
            v = (v_in @ vw + vb).reshape(b, sk, NHEAD, hd).transpose(0, 2, 1, 3)
            scores = jnp.einsum('bhqd,bhkd->bhqk', q, k) / jnp.sqrt(jnp.float32(hd))
            if mask is not None:
                scores = jnp.where(mask == 0, jnp.float32(-1000000000.0), scores)
            attn = jax.nn.softmax(scores, axis=-1)
            out = jnp.einsum('bhqk,bhkd->bhqd', attn, v)
            out = out.transpose(0, 2, 1, 3).reshape(b, sq, d)
            return out @ ow + ob

        def _layernorm(x, g, b):
            mu = jnp.mean(x, axis=-1, keepdims=True)
            var = jnp.var(x, axis=-1, keepdims=True)
            return (x - mu) * jax.lax.rsqrt(var + EPS) * g + b
        key = jax.random.key(seed)
        ks = jax.random.split(key, 16)
        sc = 0.02
        inp = {'tgt': jax.random.normal(ks[0], (B, S, D_MODEL), jnp.float32), 'memory': jax.random.normal(ks[1], (B, S, D_MODEL), jnp.float32), 'tgt_mask': jnp.tril(jnp.ones((S, S), jnp.int32))[None, None, :, :], 'sa_qw': jax.random.normal(ks[2], (D_MODEL, D_MODEL), jnp.float32) * sc, 'sa_qb': jnp.zeros((D_MODEL,), jnp.float32), 'sa_kw': jax.random.normal(ks[3], (D_MODEL, D_MODEL), jnp.float32) * sc, 'sa_kb': jnp.zeros((D_MODEL,), jnp.float32), 'sa_vw': jax.random.normal(ks[4], (D_MODEL, D_MODEL), jnp.float32) * sc, 'sa_vb': jnp.zeros((D_MODEL,), jnp.float32), 'sa_ow': jax.random.normal(ks[5], (D_MODEL, D_MODEL), jnp.float32) * sc, 'sa_ob': jnp.zeros((D_MODEL,), jnp.float32), 'ca_qw': jax.random.normal(ks[6], (D_MODEL, D_MODEL), jnp.float32) * sc, 'ca_qb': jnp.zeros((D_MODEL,), jnp.float32), 'ca_kw': jax.random.normal(ks[7], (D_MODEL, D_MODEL), jnp.float32) * sc, 'ca_kb': jnp.zeros((D_MODEL,), jnp.float32), 'ca_vw': jax.random.normal(ks[8], (D_MODEL, D_MODEL), jnp.float32) * sc, 'ca_vb': jnp.zeros((D_MODEL,), jnp.float32), 'ca_ow': jax.random.normal(ks[9], (D_MODEL, D_MODEL), jnp.float32) * sc, 'ca_ob': jnp.zeros((D_MODEL,), jnp.float32), 'w1': jax.random.normal(ks[10], (D_MODEL, D_FF), jnp.float32) * sc, 'b1': jnp.zeros((D_FF,), jnp.float32), 'w2': jax.random.normal(ks[11], (D_FF, D_MODEL), jnp.float32) * sc, 'b2': jnp.zeros((D_MODEL,), jnp.float32), 'g1': jnp.ones((D_MODEL,), jnp.float32), 'be1': jnp.zeros((D_MODEL,), jnp.float32), 'g2': jnp.ones((D_MODEL,), jnp.float32), 'be2': jnp.zeros((D_MODEL,), jnp.float32), 'g3': jnp.ones((D_MODEL,), jnp.float32), 'be3': jnp.zeros((D_MODEL,), jnp.float32)}
        return inp
    _L1_xattn_all = _L1_xattn_setup()
    _L1_xattn_in = {k: v for k, v in _L1_xattn_all.items() if k in ('sa_qw', 'sa_qb', 'sa_kw', 'sa_kb', 'sa_vw', 'sa_vb', 'sa_ow', 'sa_ob', 'ca_qw', 'ca_qb', 'ca_kw', 'ca_kb', 'ca_vw', 'ca_vb', 'ca_ow', 'ca_ob', 'w1', 'b1', 'w2', 'b2', 'g1', 'be1', 'g2', 'be2', 'g3', 'be3')}
    del _L1_xattn_all
    return {'x': x, 'ctx_1024': ctx_1024, 'mask_1x1xSxS_ik0': mask_1x1xSxS_ik0, 'L0_xattn_Wq': _L0_xattn_in['Wq'], 'L0_xattn_bq': _L0_xattn_in['bq'], 'L0_xattn_Wk': _L0_xattn_in['Wk'], 'L0_xattn_bk': _L0_xattn_in['bk'], 'L0_xattn_Wv': _L0_xattn_in['Wv'], 'L0_xattn_bv': _L0_xattn_in['bv'], 'L0_xattn_Wo': _L0_xattn_in['Wo'], 'L0_xattn_bo': _L0_xattn_in['bo'], 'L0_xattn_W1': _L0_xattn_in['W1'], 'L0_xattn_b1': _L0_xattn_in['b1'], 'L0_xattn_W2': _L0_xattn_in['W2'], 'L0_xattn_b2': _L0_xattn_in['b2'], 'L1_xattn_sa_qw': _L1_xattn_in['sa_qw'], 'L1_xattn_sa_qb': _L1_xattn_in['sa_qb'], 'L1_xattn_sa_kw': _L1_xattn_in['sa_kw'], 'L1_xattn_sa_kb': _L1_xattn_in['sa_kb'], 'L1_xattn_sa_vw': _L1_xattn_in['sa_vw'], 'L1_xattn_sa_vb': _L1_xattn_in['sa_vb'], 'L1_xattn_sa_ow': _L1_xattn_in['sa_ow'], 'L1_xattn_sa_ob': _L1_xattn_in['sa_ob'], 'L1_xattn_ca_qw': _L1_xattn_in['ca_qw'], 'L1_xattn_ca_qb': _L1_xattn_in['ca_qb'], 'L1_xattn_ca_kw': _L1_xattn_in['ca_kw'], 'L1_xattn_ca_kb': _L1_xattn_in['ca_kb'], 'L1_xattn_ca_vw': _L1_xattn_in['ca_vw'], 'L1_xattn_ca_vb': _L1_xattn_in['ca_vb'], 'L1_xattn_ca_ow': _L1_xattn_in['ca_ow'], 'L1_xattn_ca_ob': _L1_xattn_in['ca_ob'], 'L1_xattn_w1': _L1_xattn_in['w1'], 'L1_xattn_b1': _L1_xattn_in['b1'], 'L1_xattn_w2': _L1_xattn_in['w2'], 'L1_xattn_b2': _L1_xattn_in['b2'], 'L1_xattn_g1': _L1_xattn_in['g1'], 'L1_xattn_be1': _L1_xattn_in['be1'], 'L1_xattn_g2': _L1_xattn_in['g2'], 'L1_xattn_be2': _L1_xattn_in['be2'], 'L1_xattn_g3': _L1_xattn_in['g3'], 'L1_xattn_be3': _L1_xattn_in['be3']}

def reference(x, ctx_1024, mask_1x1xSxS_ik0, L0_xattn_Wq, L0_xattn_bq, L0_xattn_Wk, L0_xattn_bk, L0_xattn_Wv, L0_xattn_bv, L0_xattn_Wo, L0_xattn_bo, L0_xattn_W1, L0_xattn_b1, L0_xattn_W2, L0_xattn_b2, L1_xattn_sa_qw, L1_xattn_sa_qb, L1_xattn_sa_kw, L1_xattn_sa_kb, L1_xattn_sa_vw, L1_xattn_sa_vb, L1_xattn_sa_ow, L1_xattn_sa_ob, L1_xattn_ca_qw, L1_xattn_ca_qb, L1_xattn_ca_kw, L1_xattn_ca_kb, L1_xattn_ca_vw, L1_xattn_ca_vb, L1_xattn_ca_ow, L1_xattn_ca_ob, L1_xattn_w1, L1_xattn_b1, L1_xattn_w2, L1_xattn_b2, L1_xattn_g1, L1_xattn_be1, L1_xattn_g2, L1_xattn_be2, L1_xattn_g3, L1_xattn_be3):
    import jax
    import jax.numpy as jnp

    def _L0_xattn_ref(x, inp, Wq, bq, Wk, bk, Wv, bv, Wo, bo, W1, b1, W2, b2):
        import jax, jax.numpy as jnp
        import numpy as np
        DIM = 512
        NUM_HEADS = 16
        HEAD_DIM = DIM // NUM_HEADS
        FF = 4 * DIM
        B, T, S = (8, 256, 2048)

        def _perceiver_layer(x, inp, Wq, bq, Wk, bk, Wv, bv, Wo, bo, W1, b1, W2, b2):
            b, t, _ = x.shape
            s = inp.shape[1]
            q = (x @ Wq + bq).reshape(b, t, NUM_HEADS, HEAD_DIM)
            k = (inp @ Wk + bk).reshape(b, s, NUM_HEADS, HEAD_DIM)
            v = (inp @ Wv + bv).reshape(b, s, NUM_HEADS, HEAD_DIM)
            attn = jnp.einsum('bthd,bshd->bhts', q, k)
            attn = jax.nn.softmax(attn / jnp.sqrt(jnp.float32(HEAD_DIM)), axis=-1)
            out = jnp.einsum('bhts,bshd->bthd', attn, v).reshape(b, t, DIM)
            attn_out = out @ Wo + bo
            x = x + attn_out
            h = jax.nn.gelu(x @ W1 + b1, approximate=True)
            x = x + (h @ W2 + b2)
            return x
        return _perceiver_layer(x, inp, Wq, bq, Wk, bk, Wv, bv, Wo, bo, W1, b1, W2, b2)

    def _L1_xattn_ref(tgt, memory, tgt_mask, sa_qw, sa_qb, sa_kw, sa_kb, sa_vw, sa_vb, sa_ow, sa_ob, ca_qw, ca_qb, ca_kw, ca_kb, ca_vw, ca_vb, ca_ow, ca_ob, w1, b1, w2, b2, g1, be1, g2, be2, g3, be3):
        import jax, jax.numpy as jnp
        import numpy as np
        D_MODEL = 512
        NHEAD = 16
        D_FF = 2048
        B = 2
        S = 1024
        EPS = 1e-05

        def _mha(q_in, k_in, v_in, qw, qb, kw, kb, vw, vb, ow, ob, mask):
            b, sq, d = q_in.shape
            sk = k_in.shape[1]
            hd = d // NHEAD
            q = (q_in @ qw + qb).reshape(b, sq, NHEAD, hd).transpose(0, 2, 1, 3)
            k = (k_in @ kw + kb).reshape(b, sk, NHEAD, hd).transpose(0, 2, 1, 3)
            v = (v_in @ vw + vb).reshape(b, sk, NHEAD, hd).transpose(0, 2, 1, 3)
            scores = jnp.einsum('bhqd,bhkd->bhqk', q, k) / jnp.sqrt(jnp.float32(hd))
            if mask is not None:
                scores = jnp.where(mask == 0, jnp.float32(-1000000000.0), scores)
            attn = jax.nn.softmax(scores, axis=-1)
            out = jnp.einsum('bhqk,bhkd->bhqd', attn, v)
            out = out.transpose(0, 2, 1, 3).reshape(b, sq, d)
            return out @ ow + ob

        def _layernorm(x, g, b):
            mu = jnp.mean(x, axis=-1, keepdims=True)
            var = jnp.var(x, axis=-1, keepdims=True)
            return (x - mu) * jax.lax.rsqrt(var + EPS) * g + b
        x = tgt + _mha(tgt, tgt, tgt, sa_qw, sa_qb, sa_kw, sa_kb, sa_vw, sa_vb, sa_ow, sa_ob, tgt_mask)
        x = _layernorm(x, g1, be1)
        x = x + _mha(x, memory, memory, ca_qw, ca_qb, ca_kw, ca_kb, ca_vw, ca_vb, ca_ow, ca_ob, None)
        x = _layernorm(x, g2, be2)
        x = x + (jax.nn.relu(x @ w1 + b1) @ w2 + b2)
        x = _layernorm(x, g3, be3)
        return x
    x = _L0_xattn_ref(x, ctx_1024, L0_xattn_Wq, L0_xattn_bq, L0_xattn_Wk, L0_xattn_bk, L0_xattn_Wv, L0_xattn_bv, L0_xattn_Wo, L0_xattn_bo, L0_xattn_W1, L0_xattn_b1, L0_xattn_W2, L0_xattn_b2)
    x = _L1_xattn_ref(x, ctx_1024, mask_1x1xSxS_ik0, L1_xattn_sa_qw, L1_xattn_sa_qb, L1_xattn_sa_kw, L1_xattn_sa_kb, L1_xattn_sa_vw, L1_xattn_sa_vb, L1_xattn_sa_ow, L1_xattn_sa_ob, L1_xattn_ca_qw, L1_xattn_ca_qb, L1_xattn_ca_kw, L1_xattn_ca_kb, L1_xattn_ca_vw, L1_xattn_ca_vb, L1_xattn_ca_ow, L1_xattn_ca_ob, L1_xattn_w1, L1_xattn_b1, L1_xattn_w2, L1_xattn_b2, L1_xattn_g1, L1_xattn_be1, L1_xattn_g2, L1_xattn_be2, L1_xattn_g3, L1_xattn_be3)
    return x

_drawn_inputs = setup_inputs


def setup_inputs(seed=0):
    import zlib

    import numpy as np

    out = dict(_drawn_inputs(seed))
    spreads = {'L0_xattn_bq': (0.0, 0.466),
     'L0_xattn_bk': (0.0, 0.8),
     'L0_xattn_bv': (0.0, 0.1),
     'L0_xattn_bo': (0.0, 0.1),
     'L0_xattn_b1': (0.0, 0.1),
     'L0_xattn_b2': (0.0, 0.1),
     'L1_xattn_sa_qb': (0.0, 0.8),
     'L1_xattn_sa_kb': (0.0, 0.8),
     'L1_xattn_sa_vb': (0.0, 0.1),
     'L1_xattn_sa_ob': (0.0, 0.1),
     'L1_xattn_ca_qb': (0.0, 0.8),
     'L1_xattn_ca_kb': (0.0, 0.8),
     'L1_xattn_ca_vb': (0.0, 0.1),
     'L1_xattn_ca_ob': (0.0, 0.1),
     'L1_xattn_b1': (0.0, 0.1),
     'L1_xattn_b2': (0.0, 0.1),
     'L1_xattn_g1': (1.0, 0.2),
     'L1_xattn_be1': (0.0, 0.1),
     'L1_xattn_g2': (1.0, 0.2),
     'L1_xattn_be2': (0.0, 0.1),
     'L1_xattn_g3': (1.0, 0.2),
     'L1_xattn_be3': (0.0, 0.1)}
    factors = {'L1_xattn_sa_qw': 2.674, 'L1_xattn_ca_qw': 7.875, 'L1_xattn_ca_kw': 7.669}
    for name, (base, spread) in spreads.items():
        noise = np.random.default_rng([zlib.crc32(name.encode()), seed]).standard_normal(out[name].shape)
        drawn = base * np.exp(spread * noise) if base else spread * noise
        out[name] = jnp.asarray(drawn.astype(out[name].dtype))
    for name, factor in factors.items():
        out[name] = (out[name] * factor).astype(out[name].dtype)
    return out
```

```python
from contextlib import ExitStack

import concourse.bass as bass
from concourse import mybir

F32 = mybir.dt.float32
F32R = mybir.dt.float32r
BF16 = mybir.dt.bfloat16
I32 = mybir.dt.int32
ALU = mybir.AluOpType
ACT = mybir.ActivationFunctionType
AX = mybir.AxisListType

P = 128
D = 512
KT = D // P
HEADS = 16
HD = D // HEADS
B = 2
SQ = 1024
CH = 512
RT = CH // P
UNITS = B * HEADS
SCALE = float(HD) ** -0.5
EPS = 1e-5
NEG = -1.0e9
LOWEST = -3.0e38


def ds(start, size):
    return bass.ds(start, size)


class Core:

    def __init__(self, nc, stack, tag):
        self.nc, self.stack, self.tag = nc, stack, tag
        self.sems = []
        stack.callback(self.clear)

    def clear(self):
        self.nc.clear_and_free_semaphores(self.sems)
        self.nc.all_engine_barrier()

    def sbuf(self, name, shape, dtype=F32):
        return self.stack.enter_context(self.nc.sbuf_tensor(f"{self.tag}_{name}", shape, dtype))

    def psum(self, name, shape, dtype=F32):
        return self.stack.enter_context(self.nc.psum_tensor(f"{self.tag}_{name}", shape, dtype))

    def sem(self, name):
        self.sems.append(self.nc.alloc_semaphore(f"{self.tag}_{name}"))
        return self.sems[-1]


def row_bias(vector, parts=P):
    return vector.rearrange("(o f) -> o f", o=1).broadcast_to([parts, vector.shape[0]])


def make_identities(nc, const):
    s_memset = nc.alloc_semaphore("id_memset")
    s_identity = nc.alloc_semaphore("id_identity")
    with nc.Block() as block:
        @block.gpsimd
        def _(pool):
            nc.gpsimd.memset(const["ident"][:], 1.0).then_inc(s_memset, 1)
            nc.gpsimd.memset(const["ones"][:], 1.0).then_inc(s_memset, 1)
            pool.wait_ge(s_memset, 1)
            nc.gpsimd.affine_select(out=const["ident"][:], in_=const["ident"][:], compare_op=ALU.is_equal,
                                    fill=0.0, base=0, pattern=[[-1, P]], channel_multiplier=1).then_inc(s_identity, 1)

        @block.vector
        def _(dve):
            dve.wait_ge(s_identity, 1)
            nc.vector.tensor_copy(const["identb"][:], const["ident"][:]).then_inc(s_identity, 1)


def project(nc, const, tag, src, chunks_per_batch, mats):
    CB = chunks_per_batch
    M = len(mats)
    GROUPS = 4 * M
    T_MATS = [m for m in range(M) if mats[m][0] == "T"]
    V_MATS = [m for m in range(M) if mats[m][0] == "V"]
    with ExitStack() as stack:
        core = Core(nc, stack, tag)
        w_stage = core.sbuf("w_stage", [P, M, KT, D])
        w_hi = core.sbuf("w_hi", [P, M, KT, D], F32R)
        w_lo = core.sbuf("w_lo", [P, M, KT, D], F32R)
        b_col = core.sbuf("b_col", [P, M, KT])
        b_row = core.sbuf("b_row", [P, M, D])
        x = core.sbuf("x", [P, 2, RT, D])
        xT_hi = core.sbuf("xT_hi", [P, KT, CH], F32R)
        xT_lo = core.sbuf("xT_lo", [P, KT, CH], F32R)
        t_hi = core.sbuf("t_hi", [P, 4, CH], F32R)
        t_lo = core.sbuf("t_lo", [P, 4, CH], F32R)
        v_out = core.sbuf("v_out", [P, 2, HEADS, RT, HD])
        ps_x = core.psum("ps_x", [P, 2, CH])
        ps_y = core.psum("ps_y", [P, 4, CH])
        w_loaded = [core.sem(f"w_loaded{m}") for m in range(M)]
        x_loaded = [core.sem(f"x_loaded{s}") for s in range(2)]
        w_split = core.sem("w_split")
        w_done = core.sem("w_done")
        x_turned = core.sem("x_turned")
        x_hi_done = core.sem("x_hi_done")
        x_done = core.sem("x_done")
        y_ready = core.sem("y_ready")
        t_hi_done = core.sem("t_hi_done")
        y_done = core.sem("y_done")
        t_stored = [core.sem(f"t_stored{s}") for s in range(4)]
        v_stored = [core.sem(f"v_stored{s}") for s in range(2)]
        TG = 4 * len(T_MATS)
        block = stack.enter_context(nc.Block())

        @block.sync
        def _(sp):
            for g in range(4):
                sp.sem_inc(t_stored[g], 16)
            for v in range(len(V_MATS)):
                sp.sem_inc(v_stored[v], 16)
            for m, mat in enumerate(mats):
                sp.dma_start(w_stage[:, m], mat[1].rearrange("(k p) n -> p k n", p=P)).then_inc(w_loaded[m], 16)
                if mat[0] == "T":
                    with nc.allow_non_contiguous_dma(reason="a bias, one element per partition"):
                        sp.dma_start(b_col[:, m, :], mat[2].rearrange("(k p) -> p k", p=P)).then_inc(w_loaded[m], 16)
                else:
                    sp.dma_start(b_row[:, m, :], row_bias(mat[2])).then_inc(w_loaded[m], 16)
            def load(c):
                sp.dma_start(x[:, c % 2], src[c * CH:(c + 1) * CH, :].rearrange("(r p) d -> p r d", p=P)).then_inc(
                    x_loaded[c % 2], 16)

            load(0)
            load(1)
            for c in range(B * CB):
                b, j = c // CB, c % CB
                for m, mat in enumerate(mats):
                    if mat[0] == "T":
                        for g in range(4):
                            sp.wait_ge(y_done, c * GROUPS + m * 4 + g + 1 + 4)
                            for to, part in ((mat[3], t_hi), (mat[4], t_lo)):
                                sp.dma_start(to[b * D + g * P:b * D + (g + 1) * P, j * CH:(j + 1) * CH],
                                             part[:, g, :].bitcast(F32)).then_inc(t_stored[g], 16)
                    else:
                        v = V_MATS.index(m)
                        sp.wait_ge(y_done, c * GROUPS + m * 4 + 4 + 4)
                        sp.dma_start(mat[3][b * HEADS:(b + 1) * HEADS, :, j * RT * HD:(j + 1) * RT * HD].rearrange("h p f -> p h f"),
                                     v_out[:, v].rearrange("p h r d -> p h (r d)")).then_inc(v_stored[v], 16)
                if c + 2 < B * CB:
                    load(c + 2)
            if T_MATS:
                for g in range(4):
                    sp.wait_ge(t_stored[g], 16 + B * CB * len(T_MATS) * 32)
            for v in range(len(V_MATS)):
                sp.wait_ge(v_stored[v], 16 + B * CB * 16)

        @block.tensor
        def _(pe):
            with pe.Fori(0, B) as b:
                for j in range(CB):
                    c = b * CB + j
                    pe.wait_ge(x_loaded[j % 2], b * (CB // 2 * 16) + 16 * (j // 2 + 1))
                    for k in range(KT):
                        pe.wait_ge(x_done, c * KT + k + 1)
                        for r in range(RT):
                            turn = nc.tensor.transpose(ps_x[:, k % 2, r * P:(r + 1) * P],
                                                       x[:, j % 2, r, k * P:(k + 1) * P], const["ident"][:])
                        turn.then_inc(x_turned, 1)
                    pe.wait_ge(x_done, (c + 1) * KT + 2)
                    for m, mat in enumerate(mats):
                        pe.wait_ge(w_done, m + 1)
                        for g in range(4):
                            n = c * GROUPS + m * 4 + g
                            pe.wait_ge(y_done, n + 1)
                            out = ps_y[:, g, :]
                            for k in range(KT):
                                cols = slice(g * P, (g + 1) * P)
                                if mat[0] == "T":
                                    pairs = ((w_hi[:, m, k, cols], xT_hi[:, k, :]), (w_lo[:, m, k, cols], xT_hi[:, k, :]),
                                             (w_hi[:, m, k, cols], xT_lo[:, k, :]))
                                else:
                                    pairs = ((xT_hi[:, k, cols], w_hi[:, m, k, :]), (xT_hi[:, k, cols], w_lo[:, m, k, :]),
                                             (xT_lo[:, k, cols], w_hi[:, m, k, :]))
                                for i, (stationary, moving) in enumerate(pairs):
                                    mm = nc.tensor.matmul(out, stationary, moving, start=(k == 0 and i == 0),
                                                          stop=(k == KT - 1 and i == 2))
                            mm.then_inc(y_ready, 1)

        @block.scalar
        def _(act):
            for m in range(M):
                act.wait_ge(w_loaded[m], 32)
                nc.scalar.activation(w_hi[:, m], w_stage[:, m], ACT.Copy).then_inc(w_split, 1)
            with act.Fori(0, B) as b:
                for j in range(CB):
                    c = b * CB + j
                    for k in range(KT):
                        act.wait_ge(x_turned, c * KT + k + 1)
                        nc.scalar.activation(xT_hi[:, k, :], ps_x[:, k % 2, :], ACT.Copy).then_inc(x_hi_done, 1)
                    for i, m in enumerate(T_MATS):
                        for g in range(4):
                            act.wait_ge(y_ready, c * GROUPS + m * 4 + g + 1)
                            act.wait_ge(t_stored[g], c * (len(T_MATS) * 32) + (i + 1) * 32 - 16)
                            nc.scalar.activation(t_hi[:, g, :], ps_y[:, g, :], ACT.Identity,
                                                 bias=b_col[:, m, g:g + 1]).then_inc(t_hi_done, 1)

        @block.vector
        def _(dve):
            dve.sem_inc(x_done, 2)
            dve.sem_inc(y_done, 4)
            for m in range(M):
                dve.wait_ge(w_split, m + 1)
                nc.vector.tensor_tensor(w_lo[:, m], w_stage[:, m], w_hi[:, m].bitcast(F32), ALU.subtract).then_inc(w_done, 1)
            with dve.Fori(0, B) as b:
                for j in range(CB):
                    c = b * CB + j
                    for k in range(KT):
                        dve.wait_ge(x_hi_done, c * KT + k + 1)
                        nc.vector.tensor_tensor(xT_lo[:, k, :], ps_x[:, k % 2, :], xT_hi[:, k, :].bitcast(F32),
                                                ALU.subtract).then_inc(x_done, 1)
                    for m, mat in enumerate(mats):
                        for g in range(4):
                            if mat[0] == "T":
                                dve.wait_ge(t_hi_done, c * TG + T_MATS.index(m) * 4 + g + 1)
                                nc.vector.scalar_tensor_tensor(out=t_lo[:, g, :], in0=ps_y[:, g, :], scalar=b_col[:, m, g:g + 1],
                                                               in1=t_hi[:, g, :].bitcast(F32), op0=ALU.add,
                                                               op1=ALU.subtract).then_inc(y_done, 1)
                            else:
                                v = V_MATS.index(m)
                                dve.wait_ge(y_ready, c * GROUPS + m * 4 + g + 1)
                                if g == 0:
                                    dve.wait_ge(v_stored[v], 16 * (c + 1))
                                nc.vector.tensor_tensor(v_out[:, v, :, g, :], ps_y[:, g, :].rearrange("p (h d) -> p h d", h=HEADS),
                                                        b_row[:, m, :].rearrange("p (h d) -> p h d", h=HEADS),
                                                        ALU.add).then_inc(y_done, 1)


def attention(nc, const, tag, k_hi, k_lo, q_hi, q_lo, values, outT, mask=None):
    S = k_hi.shape[1]
    KB = S // P
    QB = SQ // P
    HALVES = S // 1024
    NS = QB * HALVES
    SLOTS = 4
    PR = 4
    ROWS = 3 * HD + 3
    AHEAD = ([1, 1, 2] * 4 + [0] * 4) if KB == 16 else [2, 1, 2, 1, 2, 0, 0, 0]
    TURN = (13, 14) if KB == 16 else (6, 7)
    assert sum(AHEAD) == NS and len(AHEAD) == KB
    LOADS = 7 * 16
    with ExitStack() as stack:
        core = Core(nc, stack, tag)
        k_st = core.sbuf("k_st", [P, SLOTS, S], F32R)
        q_st = core.sbuf("q_st", [P, SLOTS, SQ], F32R)
        v_sb = core.sbuf("v_sb", [P, SLOTS, KB, HD])
        prob = core.sbuf("prob", [P, PR, SQ])
        mx = core.sbuf("mx", [P, NS])
        top = core.sbuf("top", [P, QB])
        rest = core.sbuf("rest", [P, 2, QB])
        parts = core.sbuf("parts", [P, QB, 3], BF16)
        recip = core.sbuf("recip", [P, 2, CH])
        o_sb = core.sbuf("o_sb", [P, 2, CH])
        if mask:
            neg = core.sbuf("neg", [P, QB, S], BF16)
            negT = core.sbuf("negT", [P, KB, SQ], BF16)
            live = core.sbuf("live", [P, SQ])
            junk = core.sbuf("junk", [P, NS, S], BF16)
            pace = core.sbuf("pace", [P, 8])
        ps_s = core.psum("ps_s", [P, 2, 2, CH])
        ps_t = core.psum("ps_t", [P, 2, CH])
        ps_o = core.psum("ps_o", [P, 2, CH])
        loaded = [core.sem(f"loaded{s}") for s in range(SLOTS)]
        mask_loaded = core.sem("mask_loaded")
        minus_ones = core.sem("minus_ones")
        q_live = core.sem("q_live")
        s_ready = core.sem("s_ready")
        s_done = core.sem("s_done")
        top_chain = core.sem("top_chain")
        parts_done = core.sem("parts_done")
        row_ready = core.sem("row_ready")
        row_done = core.sem("row_done")
        t_ready = core.sem("t_ready")
        exp_done = core.sem("exp_done")
        pv_done = core.sem("pv_done")
        recip_done = core.sem("recip_done")
        o_done = core.sem("o_done")
        stored = [core.sem(f"stored{s}") for s in range(2)]
        block = stack.enter_context(nc.Block())

        @block.sync
        def _(sp):
            def load(u, slot, row, free=None):
                rows = ds(row, HD)
                if free is not None:
                    sp.wait_ge(pv_done, free)
                for part, at in ((k_hi, 0), (k_lo, 1), (k_hi, 2)):
                    sp.dma_start(k_st[at * HD:(at + 1) * HD, slot, :].bitcast(F32), part[rows, :]).then_inc(loaded[slot], 16)
                for part, at in ((q_hi, 0), (q_hi, 1), (q_lo, 2)):
                    sp.dma_start(q_st[at * HD:(at + 1) * HD, slot, :].bitcast(F32), part[rows, :]).then_inc(loaded[slot], 16)
                sp.dma_start(v_sb[:, slot].rearrange("p k d -> p (k d)"),
                             values[ds(u, 1)].rearrange("u p f -> (u p) f")).then_inc(loaded[slot], 16)

            def store(row, slot, ready):
                sp.wait_ge(o_done, ready)
                for half in range(2):
                    sp.dma_start(outT[ds(row, HD), half * CH:(half + 1) * CH],
                                 o_sb[half * HD:(half + 1) * HD, slot % 2, :]).then_inc(stored[slot % 2], 16)

            for slot in range(2):
                sp.sem_inc(stored[slot], 32)
            for slot in range(SLOTS):
                load(slot, slot, slot * HD)
                if mask and slot == 0:
                    sp.dma_start(live[:], mask[2]).then_inc(mask_loaded, 16)
                    sp.dma_start(neg[:], mask[0]).then_inc(mask_loaded, 16)
                    sp.dma_start(negT[:], mask[1]).then_inc(mask_loaded, 16)
            with sp.Fori(0, UNITS // SLOTS - 1) as i:
                for slot in range(SLOTS):
                    u = sp.snap(i * SLOTS + slot + SLOTS)
                    row = sp.snap((i * SLOTS + slot + SLOTS) * HD)
                    done = sp.snap((i * SLOTS + slot) * HD)
                    load(u, slot, row, PR + (i * SLOTS + slot + 1) * KB)
                    store(done, slot, i * SLOTS + slot + 1 + 2)
            last = UNITS // SLOTS - 1
            for slot in range(SLOTS):
                store((last * SLOTS + slot) * HD, slot, last * SLOTS + slot + 1 + 2)
            for slot in range(2):
                sp.wait_ge(stored[slot], 32 + UNITS // 2 * 32)

        @block.gpsimd
        def _(pool):
            def wipe(i, slot):
                pool.wait_ge(loaded[slot], (i + 1) * LOADS)
                nc.gpsimd.tensor_tensor(q_st[0:3 * HD, slot, :], q_st[0:3 * HD, slot, :].bitcast(F32), live[0:3 * HD, :],
                                        ALU.mult).then_inc(q_live, 1)

            if mask:
                pool.wait_ge(mask_loaded, 48)
                for slot in range(SLOTS):
                    wipe(0, slot)
                with pool.Fori(0, UNITS // SLOTS - 1) as i:
                    for slot in range(SLOTS):
                        wipe(i + 1, slot)

        @block.tensor
        def _(pe):
            def first_pass(i, slot, n):
                qb, half = n // HALVES, n % HALVES
                if n == 0:
                    pe.wait_ge(loaded[slot], (i + 1) * LOADS)
                    if mask:
                        pe.wait_ge(q_live, i * SLOTS + slot + 1)
                pe.wait_ge(s_done, i * (SLOTS * NS) + slot * NS + n + 1)
                for j in range(2):
                    mm = nc.tensor.matmul(ps_s[:, n % 2, j, :], q_st[0:3 * HD, slot, qb * P:(qb + 1) * P],
                                          k_st[0:3 * HD, slot, half * 1024 + j * CH:half * 1024 + (j + 1) * CH],
                                          start=True, stop=True)
                mm.then_inc(s_ready, 1)

            def turn_maxima(i, slot, half):
                if half == 0:
                    pe.wait_ge(parts_done, i * SLOTS + slot + 1)
                    pe.wait_ge(o_done, i * SLOTS + slot + 1)
                else:
                    pe.wait_ge(row_done, i * (2 * SLOTS) + 2 * slot + 1)
                for q in range(QB // 2):
                    mm = nc.tensor.matmul(ps_o[0:3, slot % 2, q * P:(q + 1) * P], parts[:, half * (QB // 2) + q, :],
                                          const["identb"][:], start=True, stop=True)
                mm.then_inc(row_ready, 1)

            def second_pass(i, slot, k):
                if k == 0:
                    pe.wait_ge(minus_ones, SLOTS)
                    pe.wait_ge(row_done, i * (2 * SLOTS) + 2 * slot + 2)
                    if mask:
                        pe.wait_ge(mask_loaded, 48)
                pe.wait_ge(exp_done, i * (SLOTS * KB) + slot * KB + k + 1)
                for j in range(2):
                    mm = nc.tensor.matmul(ps_t[:, j, :], k_st[0:ROWS, slot, k * P:(k + 1) * P],
                                          q_st[0:ROWS, slot, j * CH:(j + 1) * CH], start=True, stop=not mask)
                    if mask:
                        mm = nc.tensor.matmul(ps_t[:, j, :], const["identb"][:], negT[:, k, j * CH:(j + 1) * CH],
                                              start=False, stop=True)
                mm.then_inc(t_ready, 1)

            def weigh_values(i, slot, k):
                pe.wait_ge(exp_done, i * (SLOTS * KB) + slot * KB + k + 1 + 1)
                if k == 0:
                    pe.wait_ge(o_done, i * SLOTS + slot + 1)
                for tile, (left, half) in enumerate(((v_sb[:, slot, k, :], 0), (v_sb[:, slot, k, :], 1),
                                                     (const["ones"][:], 0), (const["ones"][:], 1))):
                    mm = nc.tensor.matmul(ps_o[tile * HD:(tile + 1) * HD, slot % 2, :], left,
                                          prob[:, k % PR, half * CH:(half + 1) * CH], start=(k == 0), stop=(k == KB - 1))
                mm.then_inc(pv_done, 1)

            def unit(i, slot, before, after):
                nxt = None if not after else (i, slot + 1) if slot + 1 < SLOTS else (i + 1, 0)
                n = 0
                for k in range(KB):
                    for _ in range(AHEAD[k]):
                        if nxt:
                            first_pass(*nxt, n)
                        n += 1
                    second_pass(i, slot, k)
                    if k > 0:
                        weigh_values(i, slot, k - 1)
                    elif before:
                        weigh_values(*before, KB - 1)
                    if nxt and k in TURN:
                        turn_maxima(*nxt, TURN.index(k))

            pe.sem_inc(pv_done, PR)
            for n in range(NS):
                first_pass(0, 0, n)
            turn_maxima(0, 0, 0)
            turn_maxima(0, 0, 1)
            with pe.Fori(0, UNITS // SLOTS - 1) as i:
                for slot in range(SLOTS):
                    unit(i, slot, (i, slot - 1) if slot else None, True)
                weigh_values(i, SLOTS - 1, KB - 1)
            last = UNITS // SLOTS - 1
            for slot in range(SLOTS):
                unit(last, slot, (last, slot - 1) if slot else None, slot + 1 < SLOTS)
            weigh_values(last, SLOTS - 1, KB - 1)

        @block.scalar
        def _(act):
            def exps(i, slot, k):
                act.wait_ge(t_ready, i * (SLOTS * KB) + slot * KB + k + 1)
                act.wait_ge(pv_done, i * (SLOTS * KB) + slot * KB + k + 1)
                nc.scalar.activation(prob[:, k % PR, :], ps_t[:].rearrange("p a b -> p (a b)"), ACT.Exp,
                                     scale=SCALE).then_inc(exp_done, 1)

            def maxima(i, slot, half):
                act.wait_ge(row_ready, i * (2 * SLOTS) + 2 * slot + half + 1)
                nc.scalar.activation(q_st[3 * HD:ROWS, slot, half * CH:(half + 1) * CH], ps_o[0:3, slot % 2, :],
                                     ACT.Copy).then_inc(row_done, 1)

            def unit(i, slot, after):
                nxt = None if not after else (i, slot + 1) if slot + 1 < SLOTS else (i + 1, 0)
                for k in range(KB):
                    exps(i, slot, k)
                    if nxt and k in TURN:
                        maxima(*nxt, TURN.index(k))

            act.sem_inc(exp_done, 1)
            maxima(0, 0, 0)
            maxima(0, 0, 1)
            with act.Fori(0, UNITS // SLOTS - 1) as i:
                for slot in range(SLOTS):
                    unit(i, slot, True)
            for slot in range(SLOTS):
                unit(UNITS // SLOTS - 1, slot, slot + 1 < SLOTS)

        @block.vector
        def _(dve):
            CHAIN = 5

            def tile_max(i, slot, n):
                dve.wait_ge(s_ready, i * (SLOTS * NS) + slot * NS + n + 1)
                tile = ps_s[:, n % 2].rearrange("p a b -> p (a b)")
                if mask:
                    nc.vector.memset(pace[:, n:n + 1], 0.0)
                    nc.vector.tensor_tensor_reduce(out=junk[:, n, :], in0=tile, in1=neg[:, n, :], scale=1.0, scalar=LOWEST,
                                                   op0=ALU.add, op1=ALU.max, accum_out=mx[:, n:n + 1]).then_inc(s_done, 1)
                else:
                    nc.vector.reduce_max(mx[:, n:n + 1], tile, AX.X).then_inc(s_done, 1)

            def split_maxima(i, slot):
                at = i * (SLOTS * CHAIN) + slot * CHAIN
                dve.wait_ge(s_done, i * (SLOTS * NS) + (slot + 1) * NS + 2)
                halves = mx[:].rearrange("p (q h) -> p q h", h=HALVES)
                nc.vector.tensor_tensor(top[:], halves[:, :, 0], halves[:, :, HALVES - 1], ALU.max).then_inc(top_chain, 1)
                dve.wait_ge(top_chain, at + 1)
                nc.vector.tensor_copy(parts[:, :, 0], top[:]).then_inc(top_chain, 1)
                dve.wait_ge(top_chain, at + 2)
                nc.vector.tensor_tensor(rest[:, 0], top[:], parts[:, :, 0], ALU.subtract).then_inc(top_chain, 1)
                dve.wait_ge(top_chain, at + 3)
                nc.vector.tensor_copy(parts[:, :, 1], rest[:, 0]).then_inc(top_chain, 1)
                dve.wait_ge(top_chain, at + 4)
                nc.vector.tensor_tensor(rest[:, 1], rest[:, 0], parts[:, :, 1], ALU.subtract).then_inc(top_chain, 1)
                dve.wait_ge(top_chain, at + 5)
                nc.vector.tensor_copy(parts[:, :, 2], rest[:, 1]).then_inc(parts_done, 1)

            def normalise(i, slot):
                n = i * SLOTS + slot + 1
                dve.wait_ge(pv_done, PR + n * KB)
                nc.vector.reciprocal(recip[0:2 * HD, slot % 2, :], ps_o[2 * HD:4 * HD, slot % 2, :]).then_inc(recip_done, 1)
                dve.wait_ge(recip_done, n)
                dve.wait_ge(stored[slot % 2], i * (SLOTS // 2 * 32) + slot // 2 * 32 + 32)
                nc.vector.tensor_tensor(o_sb[0:2 * HD, slot % 2, :], ps_o[0:2 * HD, slot % 2, :], recip[0:2 * HD, slot % 2, :],
                                        ALU.mult).then_inc(o_done, 1)

            def unit(i, slot, before, after):
                nxt = None if not after else (i, slot + 1) if slot + 1 < SLOTS else (i + 1, 0)
                n = 0
                for k in range(KB):
                    for _ in range(AHEAD[k]):
                        if nxt:
                            tile_max(*nxt, n)
                        n += 1
                    if k == 1 and before:
                        normalise(*before)
                    if nxt and n == NS and AHEAD[k]:
                        split_maxima(*nxt)

            dve.sem_inc(s_done, 2)
            dve.sem_inc(o_done, 2)
            for slot in range(SLOTS):
                nc.vector.memset(k_st[3 * HD:ROWS, slot, :].bitcast(F32), -1.0).then_inc(minus_ones, 1)
            if mask:
                dve.wait_ge(mask_loaded, 48)
            for n in range(NS):
                tile_max(0, 0, n)
            split_maxima(0, 0)
            with dve.Fori(0, UNITS // SLOTS - 1) as i:
                for slot in range(SLOTS):
                    unit(i, slot, (i, slot - 1) if slot else None, True)
                normalise(i, SLOTS - 1)
            last = UNITS // SLOTS - 1
            for slot in range(SLOTS):
                unit(last, slot, (last, slot - 1) if slot else None, slot + 1 < SLOTS)
            normalise(last, SLOTS - 1)


class RowNorm:

    def __init__(self, nc, core, gain, shift, rows_ready, per_chunk, credit):
        self.nc, self.gain, self.shift = nc, gain, shift
        self.rows_ready, self.per_chunk, self.credit = rows_ready, per_chunk, credit
        self.g_row = core.sbuf("g_row", [P, D])
        self.s_row = core.sbuf("s_row", [P, D])
        self.stats = core.sbuf("stats", [P, RT, 6])
        self.mv = core.sbuf("mv", [P, RT, 2])
        self.eps = core.sbuf("eps", [P, 1])
        self.pace = core.sbuf("pace", [P, 8])
        self.std = core.sbuf("std", [P, RT])
        self.rstd = core.sbuf("rstd", [P, RT])
        self.loaded = core.sem("norm_loaded")
        self.eps_set = core.sem("norm_eps_set")
        self.stats_done = core.sem("norm_stats")
        self.var_done = core.sem("norm_var")
        self.std_done = core.sem("norm_std")
        self.rstd_done = core.sem("norm_rstd")
        self.centred = core.sem("norm_centred")
        self.gained = core.sem("norm_gained")
        self.done = core.sem("norm_done")

    def sync_start(self, sp):
        sp.dma_start(self.g_row[:], row_bias(self.gain)).then_inc(self.loaded, 16)
        sp.dma_start(self.s_row[:], row_bias(self.shift)).then_inc(self.loaded, 16)

    def vector_start(self, dve):
        self.nc.vector.memset(self.eps[:], EPS).then_inc(self.eps_set, 1)

    def scalar_start(self, act):
        act.wait_ge(self.eps_set, 1)

    def vector(self, dve, y, c):
        nc = self.nc
        for r in range(RT):
            dve.wait_ge(self.rows_ready, c * self.per_chunk + self.credit + self.per_chunk - RT + r + 1)
            nc.vector.bn_stats(self.stats[:, r, :], y[:, r, :]).then_inc(self.stats_done, 1)
        dve.wait_ge(self.stats_done, (c + 1) * RT)
        nc.vector.memset(self.pace[:], 0.0)
        for r in range(RT):
            nc.vector.bn_aggr(self.mv[:, r, :], self.stats[:, r, :]).then_inc(self.var_done, 1)
        dve.wait_ge(self.std_done, c + 1)
        nc.vector.reciprocal(self.rstd[:], self.std[:]).then_inc(self.rstd_done, 1)
        dve.wait_ge(self.rstd_done, c + 1)
        for r in range(RT):
            nc.vector.tensor_scalar(y[:, r, :], y[:, r, :], self.mv[:, r, 0:1], self.rstd[:, r:r + 1], ALU.subtract,
                                    ALU.mult).then_inc(self.centred, 1)

    def scalar(self, act, c):
        act.wait_ge(self.var_done, c * RT + RT)
        self.nc.scalar.activation(self.std[:], self.mv[:, :, 1], ACT.Sqrt, bias=self.eps[:, 0:1]).then_inc(self.std_done, 1)

    def pool(self, pool, y, c):
        pool.wait_ge(self.loaded, 32)
        for r in range(RT):
            pool.wait_ge(self.centred, c * RT + r + 1)
            self.nc.gpsimd.tensor_tensor(y[:, r, :], y[:, r, :], self.g_row[:], ALU.mult).then_inc(self.gained, 1)
            pool.wait_ge(self.gained, c * RT + r + 1)
            self.nc.gpsimd.tensor_tensor(y[:, r, :], y[:, r, :], self.s_row[:], ALU.add).then_inc(self.done, 1)


def close_attention(nc, const, tag, oT, w, bias, residual, norm, out):
    CB = SQ // CH
    with ExitStack() as stack:
        core = Core(nc, stack, tag)
        w_stage = core.sbuf("w_stage", [P, KT, D])
        w_hi = core.sbuf("w_hi", [P, KT, D], F32R)
        w_lo = core.sbuf("w_lo", [P, KT, D], F32R)
        b_row = core.sbuf("b_row", [P, D])
        o_in = core.sbuf("o_in", [P, 2, KT, CH])
        o_hi = core.sbuf("o_hi", [P, 2, KT, CH], F32R)
        o_lo = core.sbuf("o_lo", [P, 2, KT, CH], F32R)
        y = core.sbuf("y", [P, 2, RT, D])
        ps_y = core.psum("ps_y", [P, 8, CH])
        w_loaded = core.sem("w_loaded")
        b_loaded = core.sem("b_loaded")
        w_hi_done = core.sem("w_hi_done")
        w_done = core.sem("w_done")
        o_loaded = [core.sem(f"o_loaded{s}") for s in range(2)]
        y_loaded = [core.sem(f"y_loaded{s}") for s in range(2)]
        o_hi_done = core.sem("o_hi_done")
        o_done = core.sem("o_done")
        biased = core.sem("biased")
        y_ready = core.sem("y_ready")
        y_done = core.sem("y_done")
        stored = [core.sem(f"stored{s}") for s in range(2)]
        row_norm = RowNorm(nc, core, *norm, y_done, RT, 8) if norm else None
        block = stack.enter_context(nc.Block())

        @block.sync
        def _(sp):
            sp.dma_start(w_stage[:], w.rearrange("(k p) n -> p k n", p=P)).then_inc(w_loaded, 16)
            sp.dma_start(b_row[:], row_bias(bias)).then_inc(b_loaded, 16)
            if norm:
                row_norm.sync_start(sp)
            for b in range(B):
                for j in range(CB):
                    if b > 0:
                        sp.wait_ge(stored[j], b * 16)
                    sp.dma_start(o_in[:, j], oT[b * D:(b + 1) * D, j * CH:(j + 1) * CH].rearrange("(k p) q -> p k q", p=P)).then_inc(
                        o_loaded[j], 16)
                    sp.dma_start(y[:, j], residual[(b * CB + j) * CH:(b * CB + j + 1) * CH, :].rearrange("(r p) d -> p r d", p=P)).then_inc(
                        y_loaded[j], 16)

        @block.tensor
        def _(pe):
            with pe.Fori(0, B) as b:
                for j in range(CB):
                    c = b * CB + j
                    pe.wait_ge(w_done, 1)
                    pe.wait_ge(o_done, c + 1)
                    for r in range(RT):
                        pe.wait_ge(y_done, c * RT + r + 1)
                        rows = slice(r * P, (r + 1) * P)
                        for k in range(KT):
                            for i, (stationary, moving) in enumerate(((o_hi[:, j, k, rows], w_hi[:, k, :]),
                                                                      (o_hi[:, j, k, rows], w_lo[:, k, :]),
                                                                      (o_lo[:, j, k, rows], w_hi[:, k, :]))):
                                mm = nc.tensor.matmul(ps_y[:, j * RT + r, :], stationary, moving, start=(k == 0 and i == 0),
                                                      stop=(k == KT - 1 and i == 2))
                        mm.then_inc(y_ready, 1)

        @block.scalar
        def _(act):
            act.wait_ge(w_loaded, 16)
            nc.scalar.activation(w_hi[:], w_stage[:], ACT.Copy).then_inc(w_hi_done, 1)
            if norm:
                row_norm.scalar_start(act)
            with act.Fori(0, B) as b:
                for j in range(CB):
                    act.wait_ge(o_loaded[j], (b + 1) * 16)
                    nc.scalar.activation(o_hi[:, j], o_in[:, j], ACT.Copy).then_inc(o_hi_done, 1)
                for j in range(CB):
                    if norm:
                        row_norm.scalar(act, b * CB + j)

        @block.vector
        def _(dve):
            dve.sem_inc(y_done, 8)
            if norm:
                row_norm.vector_start(dve)
            dve.wait_ge(w_hi_done, 1)
            nc.vector.tensor_tensor(w_lo[:], w_stage[:], w_hi[:].bitcast(F32), ALU.subtract).then_inc(w_done, 1)
            with dve.Fori(0, B) as b:
                for j in range(CB):
                    dve.wait_ge(o_hi_done, b * CB + j + 1)
                    nc.vector.tensor_tensor(o_lo[:, j], o_in[:, j], o_hi[:, j].bitcast(F32), ALU.subtract).then_inc(o_done, 1)
                for j in range(CB):
                    c = b * CB + j
                    dve.wait_ge(biased, c + 1)
                    for r in range(RT):
                        dve.wait_ge(y_ready, c * RT + r + 1)
                        nc.vector.tensor_tensor(y[:, j, r, :], ps_y[:, j * RT + r, :], y[:, j, r, :], ALU.add).then_inc(y_done, 1)
                    if norm:
                        row_norm.vector(dve, y[:, j], c)

        @block.gpsimd
        def _(pool):
            pool.wait_ge(b_loaded, 16)
            with pool.Fori(0, B) as b:
                for j in range(CB):
                    pool.wait_ge(y_loaded[j], (b + 1) * 16)
                    nc.gpsimd.tensor_tensor(y[:, j], y[:, j], b_row[:].unsqueeze(1).broadcast_to([P, RT, D]), ALU.add).then_inc(
                        biased, 1)
                for j in range(CB):
                    c = b * CB + j
                    if norm:
                        row_norm.pool(pool, y[:, j], c)
                        pool.wait_ge(row_norm.done, (c + 1) * RT)
                    else:
                        pool.wait_ge(y_done, (c + 1) * RT + 8)
                    pool.dma_start(out[ds(pool.snap(c * CH), CH), :].rearrange("(r p) d -> p r d", p=P), y[:, j]).then_inc(stored[j], 16)
            for j in range(CB):
                pool.wait_ge(stored[j], B * 16)


def feed_forward(nc, const, tag, src, w1, b1, w2, b2, function, norm, out):
    CB = SQ // CH
    F = w1.shape[1]
    FT = F // P
    WP = 4
    HR = 3
    with ExitStack() as stack:
        core = Core(nc, stack, tag)
        w_stage = core.sbuf("w_stage", [P, 2, F])
        w1_hi = core.sbuf("w1_hi", [P, KT, F], F32R)
        w1_lo = core.sbuf("w1_lo", [P, KT, F], F32R)
        w2_hi = core.sbuf("w2_hi", [P, FT, D], F32R)
        w2_lo = core.sbuf("w2_lo", [P, FT, D], F32R)
        b1_col = core.sbuf("b1_col", [P, FT])
        b2_row = core.sbuf("b2_row", [P, D])
        y = core.sbuf("y", [P, 2, RT, D])
        xT_hi = core.sbuf("xT_hi", [P, KT, CH], F32R)
        xT_lo = core.sbuf("xT_lo", [P, KT, CH], F32R)
        h = core.sbuf("h", [P, 2, CH])
        h_hi = core.sbuf("h_hi", [P, HR, CH], F32R)
        h_lo = core.sbuf("h_lo", [P, HR, CH], F32R)
        ps_x = core.psum("ps_x", [P, 2, CH])
        ps_h = core.psum("ps_h", [P, 2, CH])
        ps_y = core.psum("ps_y", [P, RT, D])
        w_loaded = [core.sem(f"w_loaded{s}") for s in range(2)]
        b1_loaded = core.sem("b1_loaded")
        b2_loaded = core.sem("b2_loaded")
        w_hi_done = core.sem("w_hi_done")
        w_done = core.sem("w_done")
        x_loaded = [core.sem(f"x_loaded{s}") for s in range(2)]
        x_turned = core.sem("x_turned")
        x_hi_done = core.sem("x_hi_done")
        x_done = core.sem("x_done")
        biased = core.sem("biased")
        h_ready = core.sem("h_ready")
        h_act_done = core.sem("h_act_done")
        h_done = core.sem("h_done")
        h_used = core.sem("h_used")
        y_done = core.sem("y_done")
        stored = [core.sem(f"stored{s}") for s in range(2)]
        row_norm = RowNorm(nc, core, *norm, y_done, RT, RT) if norm else None
        block = stack.enter_context(nc.Block())
        NP = 2 * WP

        def piece(n):
            if n < WP:
                return w1[n * P:(n + 1) * P, :], w1_hi[:, n, :], w1_lo[:, n, :]
            n -= WP
            per = FT // WP
            return (w2[n * per * P:(n + 1) * per * P, :].rearrange("(k p) d -> p k d", p=P),
                    w2_hi[:, n * per:(n + 1) * per, :].rearrange("p k d -> p (k d)"),
                    w2_lo[:, n * per:(n + 1) * per, :].rearrange("p k d -> p (k d)"))

        def hidden_slot(t):
            return t % HR

        @block.sync
        def _(sp):
            with nc.allow_non_contiguous_dma(reason="a bias, one element per partition"):
                sp.dma_start(b1_col[:], b1.rearrange("(t p) -> p t", p=P)).then_inc(b1_loaded, 16)
            sp.dma_start(b2_row[:], row_bias(b2)).then_inc(b2_loaded, 16)
            if norm:
                row_norm.sync_start(sp)

            def load_rows(b, j):
                row = (b * CB + j) * CH
                sp.dma_start(y[:, j], src[row:row + CH, :].rearrange("(r p) d -> p r d", p=P)).then_inc(
                    x_loaded[j], 16)

            for j in range(CB):
                load_rows(0, j)
            for n in range(NP):
                if n >= 2:
                    sp.wait_ge(w_done, n - 1)
                at, _, _ = piece(n)
                to = w_stage[:, n % 2, :] if n < WP else w_stage[:, n % 2, :].rearrange("p (k d) -> p k d", d=D)
                sp.dma_start(to, at).then_inc(w_loaded[n % 2], 16)
            for b in range(1, B):
                for j in range(CB):
                    sp.wait_ge(stored[j], b * 16)
                    load_rows(b, j)

        @block.tensor
        def _(pe):
            with pe.Fori(0, B) as b:
                for j in range(CB):
                    c = b * CB + j
                    pe.wait_ge(x_loaded[j], (b + 1) * 16)
                    for k in range(KT):
                        pe.wait_ge(x_done, c * KT + k + 1)
                        for r in range(RT):
                            turn = nc.tensor.transpose(ps_x[:, k % 2, r * P:(r + 1) * P], y[:, j, r, k * P:(k + 1) * P],
                                                       const["ident"][:])
                        turn.then_inc(x_turned, 1)
                    pe.wait_ge(x_done, (c + 1) * KT + 2)

                    def hidden(t):
                        pe.wait_ge(w_done, WP)
                        pe.wait_ge(h_act_done, c * (2 * FT) + 2 * t + 1)
                        cols = slice(t * P, (t + 1) * P)
                        for k in range(KT):
                            for i, (stationary, moving) in enumerate(((w1_hi[:, k, cols], xT_hi[:, k, :]),
                                                                      (w1_lo[:, k, cols], xT_hi[:, k, :]),
                                                                      (w1_hi[:, k, cols], xT_lo[:, k, :]))):
                                mm = nc.tensor.matmul(ps_h[:, t % 2, :], stationary, moving, start=(k == 0 and i == 0),
                                                      stop=(k == KT - 1 and i == 2))
                        mm.then_inc(h_ready, 1)

                    def output(t):
                        pe.wait_ge(h_done, c * FT + t + 1 + 2)
                        s = hidden_slot(t)
                        for r in range(RT):
                            if t == 0:
                                pe.wait_ge(w_done, NP)
                                pe.wait_ge(y_done, c * RT + r + 1)
                            rows = slice(r * P, (r + 1) * P)
                            for i, (stationary, moving) in enumerate(((h_hi[:, s, rows], w2_hi[:, t, :]),
                                                                      (h_hi[:, s, rows], w2_lo[:, t, :]),
                                                                      (h_lo[:, s, rows], w2_hi[:, t, :]))):
                                mm = nc.tensor.matmul(ps_y[:, r, :], stationary, moving, start=(t == 0 and i == 0),
                                                      stop=(t == FT - 1 and i == 2))
                        mm.then_inc(h_used, 1)

                    for t in range(FT):
                        hidden(t)
                        if t > 0:
                            output(t - 1)
                    output(FT - 1)

        @block.scalar
        def _(act):
            act.sem_inc(h_act_done, 3)
            for n in range(NP):
                act.wait_ge(w_loaded[n % 2], 16 * (n // 2 + 1))
                nc.scalar.activation(piece(n)[1], w_stage[:, n % 2, :], ACT.Copy).then_inc(w_hi_done, 1)
            act.wait_ge(b1_loaded, 16)
            if norm:
                row_norm.scalar_start(act)
            with act.Fori(0, B) as b:
                for j in range(CB):
                    c = b * CB + j
                    for k in range(KT):
                        act.wait_ge(x_turned, c * KT + k + 1)
                        nc.scalar.activation(xT_hi[:, k, :], ps_x[:, k % 2, :], ACT.Copy).then_inc(x_hi_done, 1)
                    for t in range(FT):
                        s = hidden_slot(t)
                        act.wait_ge(h_ready, c * FT + t + 1)
                        act.wait_ge(h_used, c * FT + t + 1)
                        nc.scalar.activation(h_hi[:, s, :], ps_h[:, t % 2, :], function, bias=b1_col[:, t:t + 1]).then_inc(
                            h_act_done, 1)
                        act.wait_ge(h_done, c * FT + t + 1)
                        nc.scalar.activation(h[:, t % 2, :], ps_h[:, t % 2, :], function, bias=b1_col[:, t:t + 1]).then_inc(
                            h_act_done, 1)
                    if norm:
                        row_norm.scalar(act, c)

        @block.vector
        def _(dve):
            dve.sem_inc(x_done, 2)
            dve.sem_inc(y_done, RT)
            dve.sem_inc(h_done, 2)
            if norm:
                row_norm.vector_start(dve)
            for n in range(NP):
                dve.wait_ge(w_hi_done, n + 1)
                _, hi, lo = piece(n)
                nc.vector.tensor_tensor(lo, w_stage[:, n % 2, :], hi.bitcast(F32), ALU.subtract).then_inc(w_done, 1)
            with dve.Fori(0, B) as b:
                for j in range(CB):
                    c = b * CB + j
                    for k in range(KT):
                        dve.wait_ge(x_hi_done, c * KT + k + 1)
                        nc.vector.tensor_tensor(xT_lo[:, k, :], ps_x[:, k % 2, :], xT_hi[:, k, :].bitcast(F32),
                                                ALU.subtract).then_inc(x_done, 1)
                    for t in range(FT):
                        dve.wait_ge(h_act_done, c * (2 * FT) + 2 * t + 2 + 3)
                        nc.vector.tensor_tensor(h_lo[:, hidden_slot(t), :], h[:, t % 2, :],
                                                h_hi[:, hidden_slot(t), :].bitcast(F32), ALU.subtract).then_inc(h_done, 1)
                    dve.wait_ge(biased, c + 1)
                    dve.wait_ge(h_used, (c + 1) * FT + HR)
                    for r in range(RT):
                        nc.vector.tensor_tensor(y[:, j, r, :], ps_y[:, r, :], y[:, j, r, :], ALU.add).then_inc(y_done, 1)
                    if norm:
                        row_norm.vector(dve, y[:, j], c)

        @block.gpsimd
        def _(pool):
            pool.sem_inc(h_used, HR)
            pool.wait_ge(b2_loaded, 16)
            with pool.Fori(0, B) as b:
                for j in range(CB):
                    c = b * CB + j
                    pool.wait_ge(x_turned, (c + 1) * KT)
                    nc.gpsimd.tensor_tensor(y[:, j], y[:, j], b2_row[:].unsqueeze(1).broadcast_to([P, RT, D]), ALU.add).then_inc(
                        biased, 1)
                    if norm:
                        row_norm.pool(pool, y[:, j], c)
                        pool.wait_ge(row_norm.done, (c + 1) * RT)
                    else:
                        pool.wait_ge(y_done, (c + 1) * RT + RT)
                    pool.dma_start(out[ds(pool.snap(c * CH), CH), :].rearrange("(r p) d -> p r d", p=P), y[:, j]).then_inc(stored[j], 16)
            for j in range(CB):
                pool.wait_ge(stored[j], B * 16)


def prepare_mask(nc, const, tag, mask, neg_out, negT_out, live_out):
    T = SQ // P
    with ExitStack() as stack:
        core = Core(nc, stack, tag)
        m_in = core.sbuf("m_in", [P, T, SQ], I32)
        off = core.sbuf("off", [P, T, SQ], BF16)
        neg = core.sbuf("neg", [P, T, SQ], BF16)
        negT = core.sbuf("negT", [P, T, SQ], BF16)
        all_off = core.sbuf("all_off", [P, T])
        live = core.sbuf("live", [P, T], BF16)
        weight = core.sbuf("weight", [P, T])
        live_row = core.sbuf("live_row", [P, T, P])
        ps_n = core.psum("ps_n", [P, 4, SQ], BF16)
        ps_l = core.psum("ps_l", [P, T, P])
        loaded = core.sem("loaded")
        off_done = core.sem("off_done")
        all_done = core.sem("all_done")
        live_done = core.sem("live_done")
        neg_done = core.sem("neg_done")
        neg_turned = core.sem("neg_turned")
        negT_done = core.sem("negT_done")
        rows_ready = core.sem("rows_ready")
        rows_done = core.sem("rows_done")
        stored = core.sem("stored")
        block = stack.enter_context(nc.Block())

        @block.sync
        def _(sp):
            sp.dma_start(m_in[:], mask.rearrange("(t p) k -> p t k", p=P)).then_inc(loaded, 16)
            sp.wait_ge(neg_done, T)
            sp.dma_start(neg_out, neg[:]).then_inc(stored, 16)
            sp.wait_ge(rows_done, 1)
            sp.dma_start(live_out, live_row[:].rearrange("p t k -> p (t k)")).then_inc(stored, 16)
            sp.wait_ge(negT_done, T + 4)
            sp.dma_start(negT_out, negT[:]).then_inc(stored, 16)
            sp.wait_ge(stored, 48)

        @block.vector
        def _(dve):
            dve.wait_ge(loaded, 16)
            for t in range(T):
                nc.vector.tensor_scalar(off[:, t, :], m_in[:, t, :], 0.0, -1.0, ALU.not_equal, ALU.add).then_inc(off_done, 1)
            for t in range(T):
                dve.wait_ge(off_done, t + 1)
                nc.vector.reduce_max(all_off[:, t:t + 1], off[:, t, :], AX.X).then_inc(all_done, 1)
            dve.wait_ge(all_done, T)
            nc.vector.tensor_scalar(live[:], all_off[:], 1.0, None, ALU.add).then_inc(live_done, 1)
            nc.vector.tensor_scalar(weight[:], all_off[:], 1.0, -NEG, ALU.add, ALU.mult).then_inc(live_done, 1)
            dve.wait_ge(live_done, 2)
            for t in range(T):
                nc.vector.tensor_scalar(neg[:, t, :], off[:, t, :], weight[:, t:t + 1], None, ALU.mult).then_inc(neg_done, 1)

        @block.tensor
        def _(pe):
            pe.wait_ge(live_done, 1)
            for t in range(T):
                mm = nc.tensor.matmul(ps_l[:, t, :], live[:, t:t + 1].broadcast_to([P, P]), const["identb"][:],
                                      start=True, stop=True)
            mm.then_inc(rows_ready, 1)
            pe.wait_ge(neg_done, T)
            for k in range(T):
                pe.wait_ge(negT_done, k + 1)
                for t in range(T):
                    turn = nc.tensor.transpose(ps_n[:, k % 4, t * P:(t + 1) * P], neg[:, t, k * P:(k + 1) * P],
                                               const["identb"][:])
                turn.then_inc(neg_turned, 1)

        @block.scalar
        def _(act):
            act.sem_inc(negT_done, 4)
            act.wait_ge(rows_ready, 1)
            nc.scalar.activation(live_row[:], ps_l[:], ACT.Copy).then_inc(rows_done, 1)
            for k in range(T):
                act.wait_ge(neg_turned, k + 1)
                nc.scalar.activation(negT[:, k, :], ps_n[:, k % 4, :], ACT.Copy).then_inc(negT_done, 1)


_INS = ["x", "ctx_1024", "mask_1x1xSxS_ik0"] + [f"L0_xattn_{n}" for n in
        ("Wq", "bq", "Wk", "bk", "Wv", "bv", "Wo", "bo", "W1", "b1", "W2", "b2")] + [f"L1_xattn_{n}" for n in
        ("sa_qw", "sa_qb", "sa_kw", "sa_kb", "sa_vw", "sa_vb", "sa_ow", "sa_ob", "ca_qw", "ca_qb", "ca_kw", "ca_kb",
         "ca_vw", "ca_vb", "ca_ow", "ca_ob", "w1", "b1", "w2", "b2", "g1", "be1", "g2", "be2", "g3", "be3")]


def build_program(nc, ins, out):
    x = ins["x"].rearrange("b s d -> (b s) d")
    context = ins["ctx_1024"].rearrange("b s d -> (b s) d")
    mask = ins["mask_1x1xSxS_ik0"].rearrange("a b q k -> (a b q) k")
    out_rows = out.rearrange("b s d -> (b s) d")
    p = {n.removeprefix("L0_xattn_"): a for n, a in ins.items() if n.startswith("L0_")}
    t = {n.removeprefix("L1_xattn_"): a for n, a in ins.items() if n.startswith("L1_")}
    SC = ins["ctx_1024"].shape[1]

    def dram(name, shape, dtype=F32):
        return nc.dram_tensor(name, shape, dtype).ap()

    def keys(name, s):
        return dram(f"{name}_hi", (B * D, s)), dram(f"{name}_lo", (B * D, s))

    k0, k2, k1 = keys("k0", SC), keys("k2", SC), keys("k1", SQ)
    q0, q1, q2 = keys("q0", SQ), keys("q1", SQ), keys("q2", SQ)
    v0, v2 = (dram(n, (UNITS, P, SC // P * HD)) for n in ("v0", "v2"))
    v1 = dram("v1", (UNITS, P, SQ // P * HD))
    o0, o1, o2 = (dram(n, (B * D, SQ)) for n in ("o0", "o1", "o2"))
    rows = [dram(f"rows{n}", (B * SQ, D)) for n in range(4)]
    T = SQ // P
    neg, negT = dram("neg", (P, T, SQ), BF16), dram("negT", (P, T, SQ), BF16)
    live = dram("live", (P, SQ))

    with ExitStack() as stack:
        const = {
            "ident": stack.enter_context(nc.sbuf_tensor("ident", [P, P], F32)),
            "identb": stack.enter_context(nc.sbuf_tensor("identb", [P, P], BF16)),
            "ones": stack.enter_context(nc.sbuf_tensor("ones", [P, HD], F32)),
        }
        make_identities(nc, const)
        project(nc, const, "ctx0", context, SC // CH, [("T", p["Wk"], p["bk"], *k0), ("V", p["Wv"], p["bv"], v0)])
        project(nc, const, "ctx2", context, SC // CH, [("T", t["ca_kw"], t["ca_kb"], *k2), ("V", t["ca_vw"], t["ca_vb"], v2)])
        project(nc, const, "query0", x, SQ // CH, [("T", p["Wq"], p["bq"], *q0)])
        attention(nc, const, "attn0", *k0, *q0, v0, o0)
        close_attention(nc, const, "close0", o0, p["Wo"], p["bo"], x, None, rows[0])
        feed_forward(nc, const, "ff0", rows[0], p["W1"], p["b1"], p["W2"], p["b2"], ACT.Gelu_apprx_tanh, None, rows[1])
        prepare_mask(nc, const, "mask", mask, neg, negT, live)
        project(nc, const, "self", rows[1], SQ // CH, [("T", t["sa_qw"], t["sa_qb"], *q1), ("T", t["sa_kw"], t["sa_kb"], *k1),
                                                       ("V", t["sa_vw"], t["sa_vb"], v1)])
        attention(nc, const, "attn1", *k1, *q1, v1, o1, (neg, negT, live))
        close_attention(nc, const, "close1", o1, t["sa_ow"], t["sa_ob"], rows[1], (t["g1"], t["be1"]), rows[2])
        project(nc, const, "query2", rows[2], SQ // CH, [("T", t["ca_qw"], t["ca_qb"], *q2)])
        attention(nc, const, "attn2", *k2, *q2, v2, o2)
        close_attention(nc, const, "close2", o2, t["ca_ow"], t["ca_ob"], rows[2], (t["g2"], t["be2"]), rows[3])
        feed_forward(nc, const, "ff1", rows[3], t["w1"], t["b1"], t["w2"], t["b2"], ACT.Relu, (t["g3"], t["be3"]), out_rows)


def kernel(**inputs):
    import numpy as _np
    import concourse.bacc as _bacc
    from concourse import mybir as _mybir
    from concourse.bass_utils import run_bass_kernel_spmd as _run

    nc = _bacc.Bacc("TRN2", target_bir_lowering=False, num_devices=1)
    arrays, aps = {}, {}
    for name in _INS:
        a = _np.ascontiguousarray(inputs[name])
        arrays[f"in_{name}"] = a
        aps[name] = nc.dram_tensor(f"in_{name}", a.shape, _mybir.dt.from_np(a.dtype), kind="ExternalInput").ap()
    shape = tuple(inputs["x"].shape)
    out = nc.dram_tensor("out_rows", shape, F32, kind="ExternalOutput").ap()
    build_program(nc, aps, out)
    r = _run(nc, [arrays], core_ids=[0])
    return r.results[0]["out_rows"]
```

```python
from contextlib import ExitStack

import concourse.bass as bass
from concourse import mybir

F32 = mybir.dt.float32
F32R = mybir.dt.float32r
BF16 = mybir.dt.bfloat16
I32 = mybir.dt.int32
ALU = mybir.AluOpType
ACT = mybir.ActivationFunctionType
AX = mybir.AxisListType

P = 128
D = 512
KT = D // P
HEADS = 16
HD = D // HEADS
B = 2
SQ = 1024
CH = 512
RT = CH // P
UNITS = B * HEADS
SCALE = float(HD) ** -0.5
EPS = 1e-5
NEG = -1.0e9
LOWEST = -3.0e38


def ds(start, size):
    return bass.ds(start, size)


class Core:

    def __init__(self, nc, stack, tag):
        self.nc, self.stack, self.tag = nc, stack, tag
        self.sems = []
        stack.callback(self.clear)

    def clear(self):
        self.nc.clear_and_free_semaphores(self.sems)
        self.nc.all_engine_barrier()

    def sbuf(self, name, shape, dtype=F32):
        return self.stack.enter_context(self.nc.sbuf_tensor(f"{self.tag}_{name}", shape, dtype))

    def psum(self, name, shape, dtype=F32):
        return self.stack.enter_context(self.nc.psum_tensor(f"{self.tag}_{name}", shape, dtype))

    def sem(self, name):
        self.sems.append(self.nc.alloc_semaphore(f"{self.tag}_{name}"))
        return self.sems[-1]


def row_bias(vector, parts=P):
    return vector.rearrange("(o f) -> o f", o=1).broadcast_to([parts, vector.shape[0]])


def make_identities(nc, const):
    s_memset = nc.alloc_semaphore("id_memset")
    s_identity = nc.alloc_semaphore("id_identity")
    with nc.Block() as block:
        @block.gpsimd
        def _(pool):
            nc.gpsimd.memset(const["ident"][:], 1.0).then_inc(s_memset, 1)
            nc.gpsimd.memset(const["ones"][:], 1.0).then_inc(s_memset, 1)
            pool.wait_ge(s_memset, 1)
            nc.gpsimd.affine_select(out=const["ident"][:], in_=const["ident"][:], compare_op=ALU.is_equal,
                                    fill=0.0, base=0, pattern=[[-1, P]], channel_multiplier=1).then_inc(s_identity, 1)

        @block.vector
        def _(dve):
            dve.wait_ge(s_identity, 1)
            nc.vector.tensor_copy(const["identb"][:], const["ident"][:]).then_inc(s_identity, 1)


def project(nc, const, tag, src, chunks_per_batch, mats):
    CB = chunks_per_batch
    CHUNKS = B * CB
    M = len(mats)
    GROUPS = 4 * M
    T_MATS = [m for m in range(M) if mats[m][0] == "T"]
    V_MATS = [m for m in range(M) if mats[m][0] == "V"]
    TG = 4 * len(T_MATS)
    assert CHUNKS % 2 == 0
    with ExitStack() as stack:
        core = Core(nc, stack, tag)
        w_stage = core.sbuf("w_stage", [P, 2, KT, D])
        w_hi = core.sbuf("w_hi", [P, M, KT, D], F32R)
        w_lo = core.sbuf("w_lo", [P, M, KT, D], F32R)
        b_col = core.sbuf("b_col", [P, M, KT])
        b_row = core.sbuf("b_row", [P, M, D])
        x = core.sbuf("x", [P, 2, RT, D])
        xT_hi = core.sbuf("xT_hi", [P, 2, KT, CH], F32R)
        xT_lo = core.sbuf("xT_lo", [P, 2, KT, CH], F32R)
        t_hi = core.sbuf("t_hi", [P, 4, CH], F32R)
        t_lo = core.sbuf("t_lo", [P, 4, CH], F32R)
        v_out = core.sbuf("v_out", [P, 2, HEADS, RT, HD])
        ps_x = core.psum("ps_x", [P, 2, CH])
        ps_y = core.psum("ps_y", [P, 4, CH])
        w_loaded = [core.sem(f"w_loaded{m}") for m in range(M)]
        x_loaded = [core.sem(f"x_loaded{s}") for s in range(2)]
        w_split = core.sem("w_split")
        w_done = core.sem("w_done")
        x_turned = core.sem("x_turned")
        x_hi_done = core.sem("x_hi_done")
        x_done = core.sem("x_done")
        y_ready = core.sem("y_ready")
        t_hi_done = core.sem("t_hi_done")
        y_done = core.sem("y_done")
        t_stored = [core.sem(f"t_stored{s}") for s in range(4)]
        v_stored = [core.sem(f"v_stored{s}") for s in range(2)]
        block = stack.enter_context(nc.Block())

        def before(i, s, per):
            return i * (2 * per) + s * per

        def all_pairs(engine, chunk):
            with engine.Fori(0, CHUNKS // 2 - 1) as i:
                chunk(i, 0, False)
                chunk(i, 1, False)
            chunk(CHUNKS // 2 - 1, 0, False)
            chunk(CHUNKS // 2 - 1, 1, True)

        @block.sync
        def _(sp):
            def load(c):
                sp.dma_start(x[:, c % 2], src[c * CH:(c + 1) * CH, :].rearrange("(r p) d -> p r d", p=P)).then_inc(
                    x_loaded[c % 2], 16)

            for g in range(4):
                sp.sem_inc(t_stored[g], 16)
            for v in range(len(V_MATS)):
                sp.sem_inc(v_stored[v], 16)
            load(0)
            for m, mat in enumerate(mats):
                if m >= 2:
                    sp.wait_ge(w_done, m - 1)
                sp.dma_start(w_stage[:, m % 2], mat[1].rearrange("(k p) n -> p k n", p=P)).then_inc(w_loaded[m], 16)
                if mat[0] == "T":
                    with nc.allow_non_contiguous_dma(reason="a bias, one element per partition"):
                        sp.dma_start(b_col[:, m, :], mat[2].rearrange("(k p) -> p k", p=P)).then_inc(w_loaded[m], 16)
                else:
                    sp.dma_start(b_row[:, m, :], row_bias(mat[2])).then_inc(w_loaded[m], 16)
                if m == 0:
                    load(1)
            for c in range(CHUNKS):
                b, j = divmod(c, CB)
                if c + 2 < CHUNKS:
                    sp.wait_ge(x_turned, (c + 1) * KT)
                    load(c + 2)
                for m, mat in enumerate(mats):
                    if mat[0] == "T":
                        for g in range(4):
                            sp.wait_ge(y_done, c * GROUPS + m * 4 + g + 1 + 4)
                            for to, part in ((mat[3], t_hi), (mat[4], t_lo)):
                                sp.dma_start(to[b * D + g * P:b * D + (g + 1) * P, j * CH:(j + 1) * CH],
                                             part[:, g, :].bitcast(F32)).then_inc(t_stored[g], 16)
                    else:
                        v = V_MATS.index(m)
                        sp.wait_ge(y_done, c * GROUPS + m * 4 + 4 + 4)
                        sp.dma_start(mat[3][b * HEADS:(b + 1) * HEADS, :, j * RT * HD:(j + 1) * RT * HD].rearrange("h p f -> p h f"),
                                     v_out[:, v].rearrange("p h r d -> p h (r d)")).then_inc(v_stored[v], 16)
            if T_MATS:
                for g in range(4):
                    sp.wait_ge(t_stored[g], 16 + CHUNKS * len(T_MATS) * 32)
            for v in range(len(V_MATS)):
                sp.wait_ge(v_stored[v], 16 + CHUNKS * 16)

        @block.tensor
        def _(pe):
            def turn(i, s):
                slot = s % 2
                pe.wait_ge(x_loaded[slot], i * 16 + 16 * (s // 2 + 1))
                for k in range(KT):
                    pe.wait_ge(x_done, before(i, s, KT) + (k + 1))
                    for r in range(RT):
                        mm = nc.tensor.transpose(ps_x[:, k % 2, r * P:(r + 1) * P],
                                                 x[:, slot, r, k * P:(k + 1) * P], const["ident"][:])
                    mm.then_inc(x_turned, 1)

            def chunk(i, s, last):
                pe.wait_ge(x_done, before(i, s, KT) + (KT + 2))
                for m, mat in enumerate(mats):
                    if m == M - 1 and not last:
                        turn(i, s + 1)
                    pe.wait_ge(w_done, m + 1)
                    for g in range(4):
                        pe.wait_ge(y_done, before(i, s, GROUPS) + (m * 4 + g + 1))
                        cols = slice(g * P, (g + 1) * P)
                        for k in range(KT):
                            if mat[0] == "T":
                                pairs = ((w_hi[:, m, k, cols], xT_hi[:, s, k, :]), (w_lo[:, m, k, cols], xT_hi[:, s, k, :]),
                                         (w_hi[:, m, k, cols], xT_lo[:, s, k, :]))
                            else:
                                pairs = ((xT_hi[:, s, k, cols], w_hi[:, m, k, :]), (xT_hi[:, s, k, cols], w_lo[:, m, k, :]),
                                         (xT_lo[:, s, k, cols], w_hi[:, m, k, :]))
                            for n, (stationary, moving) in enumerate(pairs):
                                mm = nc.tensor.matmul(ps_y[:, g, :], stationary, moving, start=(k == 0 and n == 0),
                                                      stop=(k == KT - 1 and n == 2))
                        mm.then_inc(y_ready, 1)

            turn(0, 0)
            all_pairs(pe, chunk)

        @block.scalar
        def _(act):
            def split_weights(m):
                act.wait_ge(w_loaded[m], 32)
                nc.scalar.activation(w_hi[:, m], w_stage[:, m % 2], ACT.Copy).then_inc(w_split, 1)

            def keep_turned(i, s):
                for k in range(KT):
                    act.wait_ge(x_turned, before(i, s, KT) + (k + 1))
                    nc.scalar.activation(xT_hi[:, s % 2, k, :], ps_x[:, k % 2, :], ACT.Copy).then_inc(x_hi_done, 1)

            def chunk(i, s, last):
                for m in range(M):
                    if m == M - 1 and not last:
                        keep_turned(i, s + 1)
                    if m in T_MATS:
                        t = T_MATS.index(m)
                        for g in range(4):
                            act.wait_ge(y_ready, before(i, s, GROUPS) + (m * 4 + g + 1))
                            act.wait_ge(t_stored[g], before(i, s, len(T_MATS) * 32) + (t * 32 + 16))
                            nc.scalar.activation(t_hi[:, g, :], ps_y[:, g, :], ACT.Identity,
                                                 bias=b_col[:, m, g:g + 1]).then_inc(t_hi_done, 1)

            split_weights(0)
            keep_turned(0, 0)
            for m in range(1, M):
                split_weights(m)
            all_pairs(act, chunk)

        @block.vector
        def _(dve):
            def split_weights(m):
                dve.wait_ge(w_split, m + 1)
                nc.vector.tensor_tensor(w_lo[:, m], w_stage[:, m % 2], w_hi[:, m].bitcast(F32), ALU.subtract).then_inc(w_done, 1)

            def keep_turned(i, s):
                for k in range(KT):
                    dve.wait_ge(x_hi_done, before(i, s, KT) + (k + 1))
                    nc.vector.tensor_tensor(xT_lo[:, s % 2, k, :], ps_x[:, k % 2, :], xT_hi[:, s % 2, k, :].bitcast(F32),
                                            ALU.subtract).then_inc(x_done, 1)

            def chunk(i, s, last):
                for m, mat in enumerate(mats):
                    if m == M - 1 and not last:
                        keep_turned(i, s + 1)
                    for g in range(4):
                        if mat[0] == "T":
                            dve.wait_ge(t_hi_done, before(i, s, TG) + (T_MATS.index(m) * 4 + g + 1))
                            nc.vector.scalar_tensor_tensor(out=t_lo[:, g, :], in0=ps_y[:, g, :], scalar=b_col[:, m, g:g + 1],
                                                           in1=t_hi[:, g, :].bitcast(F32), op0=ALU.add,
                                                           op1=ALU.subtract).then_inc(y_done, 1)
                        else:
                            v = V_MATS.index(m)
                            dve.wait_ge(y_ready, before(i, s, GROUPS) + (m * 4 + g + 1))
                            if g == 0:
                                dve.wait_ge(v_stored[v], before(i, s, 16) + 16)
                            nc.vector.tensor_tensor(v_out[:, v, :, g, :], ps_y[:, g, :].rearrange("p (h d) -> p h d", h=HEADS),
                                                    b_row[:, m, :].rearrange("p (h d) -> p h d", h=HEADS),
                                                    ALU.add).then_inc(y_done, 1)

            dve.sem_inc(x_done, 2)
            dve.sem_inc(y_done, 4)
            split_weights(0)
            keep_turned(0, 0)
            for m in range(1, M):
                split_weights(m)
            all_pairs(dve, chunk)


def attention(nc, const, tag, k_hi, k_lo, q_hi, q_lo, values, outT, sums, mask=None):
    S = k_hi.shape[1]
    KB = S // P
    QB = SQ // P
    HALVES = S // 1024
    NS = QB * HALVES
    SLOTS = 4
    PR = 8
    PAIRS = KB // 2
    PAIR_SLOTS = 4
    BLOCKS = KB // 4
    ROWS = 3 * HD + 3
    LEAD = 5
    FILL = [["tile", "values"], ["tile", "tile"], ["sums", "tile"], ["values"]]
    FILL += [["tile", "values"], ["tile", "tile"], ["values", "tile"], ["sums"]] * (BLOCKS - 1)
    FILL[KB - 4] = ["tile", "turn", "values"]
    assert sum(fill.count("tile") for fill in FILL) == NS and NS == KB
    LOADS = 7 * 16
    LAST = UNITS - 1
    LOOPS = UNITS // SLOTS - 1

    uses, steps, counts = [], [], {"tile": 0, "turn": 0, "values": -1, "sums": -1}
    for fill in FILL:
        steps.append([])
        for kind in fill:
            n = counts[kind]
            steps[-1].append((kind, n, len(uses)))
            counts[kind] += 1
            if kind in ("tile", "turn"):
                uses.append((kind, n))
    assert uses[-2][0] == uses[-1][0] == "tile" and counts["values"] == PAIRS - 1 and counts["sums"] == BLOCKS - 1
    PROLOGUE = NS + 1 + LEAD

    with ExitStack() as stack:
        core = Core(nc, stack, tag)
        k_st = core.sbuf("k_st", [P, SLOTS, S], F32R)
        q_st = core.sbuf("q_st", [P, SLOTS, SQ], F32R)
        v_sb = core.sbuf("v_sb", [P, SLOTS, KB, HD])
        prob = core.sbuf("prob", [P, PR, SQ])
        pair = core.sbuf("pair", [P, PAIR_SLOTS, SQ])
        mx = core.sbuf("mx", [P, 2, NS])
        top = core.sbuf("top", [P, QB])
        rest = core.sbuf("rest", [P, 2, QB])
        parts = core.sbuf("parts", [P, QB, 3], BF16)
        o_odd = core.sbuf("o_odd", [P, CH])
        d_odd = core.sbuf("d_odd", [P, CH])
        o_sb = core.sbuf("o_sb", [P, 2, CH])
        d_sb = core.sbuf("d_sb", [P, 2, CH])
        if mask:
            neg = core.sbuf("neg", [P, QB, S], BF16)
            negT = core.sbuf("negT", [P, KB, SQ], BF16)
            live = core.sbuf("live", [P, SQ])
            junk = core.sbuf("junk", [P, NS, S], BF16)
            pace = core.sbuf("pace", [P, NS])
        ps_s = core.psum("ps_s", [P, 2, 2, CH])
        ps_t = core.psum("ps_t", [P, 2, CH])
        ps_o = core.psum("ps_o", [P, CH])
        ps_d = core.psum("ps_d", [P, CH])
        loaded = [core.sem(f"loaded{s}") for s in range(SLOTS)]
        mask_loaded = core.sem("mask_loaded")
        minus_ones = core.sem("minus_ones")
        q_live = core.sem("q_live")
        s_ready = core.sem("s_ready")
        s_done = core.sem("s_done")
        top_chain = core.sem("top_chain")
        parts_done = core.sem("parts_done")
        row_ready = core.sem("row_ready")
        row_done = core.sem("row_done")
        t_ready = core.sem("t_ready")
        exp_done = core.sem("exp_done")
        pair_done = core.sem("pair_done")
        v_done = core.sem("v_done")
        d_done = core.sem("d_done")
        o_half = core.sem("o_half")
        d_half = core.sem("d_half")
        o_out = core.sem("o_out")
        d_out = core.sem("d_out")
        stored = [core.sem(f"stored{s}") for s in range(2)]
        block = stack.enter_context(nc.Block())

        def stream(i, s, n):
            return i * (SLOTS * NS) + (s * NS + n)

        def exps_before(i, s, k):
            return i * (SLOTS * KB * 2) + (s * KB + k) * 2

        @block.sync
        def _(sp):
            def load(u, row, slot):
                rows = ds(row, HD)
                for part, at in ((k_hi, 0), (k_lo, 1), (k_hi, 2)):
                    sp.dma_start(k_st[at * HD:(at + 1) * HD, slot, :].bitcast(F32), part[rows, :]).then_inc(loaded[slot], 16)
                for part, at in ((q_hi, 0), (q_hi, 1), (q_lo, 2)):
                    sp.dma_start(q_st[at * HD:(at + 1) * HD, slot, :].bitcast(F32), part[rows, :]).then_inc(loaded[slot], 16)
                sp.dma_start(v_sb[:, slot].rearrange("p k d -> p (k d)"),
                             values[ds(u, 1)].rearrange("u p f -> (u p) f")).then_inc(loaded[slot], 16)

            def store(u, row, slot, i, s):
                sp.wait_ge(o_out, i * SLOTS + (s + 1 + 1))
                sp.wait_ge(d_out, i * SLOTS + (s + 1 + 1))
                for half in range(2):
                    queries = slice(half * CH, (half + 1) * CH)
                    sp.dma_start(outT[ds(row, HD), queries], o_sb[half * HD:(half + 1) * HD, slot % 2, :]).then_inc(
                        stored[slot % 2], 16)
                    sp.dma_start(sums[ds(u, 1), queries], d_sb[half * HD:half * HD + 1, slot % 2, :]).then_inc(
                        stored[slot % 2], 16)

            for slot in range(2):
                sp.sem_inc(stored[slot], 64)
            for slot in range(SLOTS):
                load(slot, slot * HD, slot)
                if mask and slot == 0:
                    sp.dma_start(live[:], mask[2]).then_inc(mask_loaded, 16)
                    sp.dma_start(neg[:], mask[0]).then_inc(mask_loaded, 16)
                    sp.dma_start(negT[:], mask[1]).then_inc(mask_loaded, 16)
            with sp.Fori(0, LOOPS) as i:
                for slot in range(SLOTS):
                    u_out, row_out = sp.snap(i * SLOTS + slot), sp.snap((i * SLOTS + slot) * HD)
                    u_in, row_in = sp.snap(i * SLOTS + slot + SLOTS), sp.snap((i * SLOTS + slot + SLOTS) * HD)
                    sp.wait_ge(v_done, i * (SLOTS * PAIRS) + ((slot + 1) * PAIRS + PR // 2))
                    load(u_in, row_in, slot)
                    store(u_out, row_out, slot, i, slot)
            for slot in range(SLOTS):
                u = LOOPS * SLOTS + slot
                store(u, u * HD, slot, LOOPS, slot)
            for slot in range(2):
                sp.wait_ge(stored[slot], 64 + UNITS // 2 * 64)

        @block.gpsimd
        def _(pool):
            def wipe(i, s):
                slot = s % SLOTS
                pool.wait_ge(loaded[slot], (i + s // SLOTS + 1) * LOADS)
                nc.gpsimd.tensor_tensor(q_st[0:3 * HD, slot, :], q_st[0:3 * HD, slot, :].bitcast(F32), live[0:3 * HD, :],
                                        ALU.mult).then_inc(q_live, 1)

            def add_pairs(i, s):
                for p in range(PAIRS):
                    pool.wait_ge(exp_done, exps_before(i, s, 2 * p + 2) + 2)
                    if p % 2 == 0:
                        pool.wait_ge(d_done, i * (SLOTS * BLOCKS) + (s * BLOCKS + p // 2 + 1))
                    nc.gpsimd.tensor_tensor(pair[:, p % PAIR_SLOTS, :], prob[:, 2 * p % PR, :], prob[:, (2 * p + 1) % PR, :],
                                            ALU.add).then_inc(pair_done, 1)

            def unit(i, s):
                if mask and not (isinstance(i, int) and i * SLOTS + s + 2 > LAST):
                    wipe(i, s + 2)
                add_pairs(i, s)

            pool.sem_inc(pair_done, PR // 2)
            if mask:
                pool.wait_ge(mask_loaded, 48)
                wipe(0, 0)
                wipe(0, 1)
            unit(0, 0)
            with pool.Fori(0, LOOPS) as i:
                for s in range(1, SLOTS + 1):
                    unit(i, s)
            for s in range(1, SLOTS):
                unit(LOOPS, s)

        @block.tensor
        def _(pe):
            def first_pass(at, i, s, n):
                slot, qb, half = s % SLOTS, n // HALVES, n % HALVES
                if n == 0:
                    pe.wait_ge(loaded[slot], (i + (s // SLOTS + 1)) * LOADS)
                    if mask:
                        pe.wait_ge(q_live, i * SLOTS + (s + 1))
                for j in range(2):
                    mm = nc.tensor.matmul(ps_s[:, at, j, :], q_st[0:3 * HD, slot, qb * P:(qb + 1) * P],
                                          k_st[0:3 * HD, slot, half * 1024 + j * CH:half * 1024 + (j + 1) * CH],
                                          start=True, stop=True)
                mm.then_inc(s_ready, 1)

            def turn_maxima(at, i, s):
                pe.wait_ge(parts_done, i * SLOTS + (s + 1))
                for q in range(QB):
                    mm = nc.tensor.matmul(ps_s[0:3, at, q // 4, q % 4 * P:(q % 4 + 1) * P], parts[:, q, :],
                                          const["identb"][:], start=True, stop=True)
                mm.then_inc(row_ready, 1)

            def use_tile(i, s, kind, n, x):
                ahead = 1 if kind == "turn" else 1 + (LEAD + n) // NS
                if isinstance(i, int) and i * SLOTS + s + ahead > LAST:
                    return
                before, period = (uses[x - 2], s) if x >= 2 else (uses[x - 2], s - 1)
                if before[0] == "turn":
                    pe.wait_ge(row_done, i * SLOTS + (period + 2))
                else:
                    number = stream(i, period + 1, LEAD + before[1] + 1)
                    pe.wait_ge(s_done, min(number, UNITS * NS) if isinstance(i, int) else number)
                at = (PROLOGUE + s * (NS + 1) + x) % 2
                if kind == "turn":
                    turn_maxima(at, i, s + 1)
                else:
                    first_pass(at, i, s + ahead, (LEAD + n) % NS)

            def second_pass(i, s, k):
                slot = s % SLOTS
                if k == 0:
                    pe.wait_ge(row_done, i * SLOTS + (s + 1))
                for j in range(2):
                    pe.wait_ge(exp_done, exps_before(i, s, k) + (j + 1))
                    mm = nc.tensor.matmul(ps_t[:, j, :], k_st[0:ROWS, slot, k * P:(k + 1) * P],
                                          q_st[0:ROWS, slot, j * CH:(j + 1) * CH], start=True, stop=not mask)
                    if mask:
                        mm = nc.tensor.matmul(ps_t[:, j, :], const["identb"][:], negT[:, k, j * CH:(j + 1) * CH],
                                              start=False, stop=True)
                    mm.then_inc(t_ready, 1)

            def four_at_once(out, operands, first, last, done):
                for tile in range(4):
                    left, right = operands[tile // 2]
                    half = tile % 2
                    mm = nc.tensor.matmul(out[tile * HD:(tile + 1) * HD, :], left, right[:, half * CH:(half + 1) * CH],
                                          start=first, stop=last)
                mm.then_inc(done, 1)

            def weigh_values(i, s, p):
                slot = s % SLOTS
                pe.wait_ge(exp_done, exps_before(i, s, 2 * p + 2) + 2)
                if p == 0:
                    pe.wait_ge(o_out, i * SLOTS + (s + 1))
                four_at_once(ps_o, [(v_sb[:, slot, k, :], prob[:, k % PR, :]) for k in (2 * p, 2 * p + 1)],
                             p == 0, p == PAIRS - 1, v_done)

            def sum_up(i, s, m):
                pe.wait_ge(pair_done, i * (SLOTS * PAIRS) + (s * PAIRS + 2 * m + 2 + PR // 2))
                if m == 0:
                    pe.wait_ge(d_out, i * SLOTS + (s + 1))
                four_at_once(ps_d, [(const["ones"][:], pair[:, p % PAIR_SLOTS, :]) for p in (2 * m, 2 * m + 1)],
                             m == 0, m == BLOCKS - 1, d_done)

            def unit(i, s, first=False):
                for k in range(KB):
                    second_pass(i, s, k)
                    for kind, n, x in steps[k]:
                        if kind in ("tile", "turn"):
                            use_tile(i, s, kind, n, x)
                        elif kind == "values" and (n >= 0 or not first):
                            weigh_values(i, *((s, n) if n >= 0 else (s - 1, PAIRS - 1)))
                        elif kind == "sums" and (n >= 0 or not first):
                            sum_up(i, *((s, n) if n >= 0 else (s - 1, BLOCKS - 1)))

            pe.sem_inc(v_done, PR // 2)
            pe.sem_inc(d_done, PAIR_SLOTS // 2)
            for x in range(PROLOGUE):
                if x == NS:
                    turn_maxima(x % 2, 0, 0)
                else:
                    n = x - (x > NS)
                    if x == NS + 2:
                        pe.wait_ge(row_done, 1)
                    elif x >= 2:
                        pe.wait_ge(s_done, n - 1 if x != NS + 1 else NS)
                    first_pass(x % 2, 0, n // NS, n % NS)
            pe.wait_ge(minus_ones, SLOTS)
            if mask:
                pe.wait_ge(mask_loaded, 48)
            unit(0, 0, first=True)
            with pe.Fori(0, LOOPS) as i:
                for s in range(1, SLOTS + 1):
                    unit(i, s)
            for s in range(1, SLOTS):
                unit(LOOPS, s)
            weigh_values(LOOPS, SLOTS - 1, PAIRS - 1)
            sum_up(LOOPS, SLOTS - 1, BLOCKS - 1)

        @block.scalar
        def _(act):
            def exps(i, s, k):
                if k % 2 == 0:
                    act.wait_ge(v_done, i * (SLOTS * PAIRS) + (s * PAIRS + k // 2 + 1))
                    act.wait_ge(pair_done, i * (SLOTS * PAIRS) + (s * PAIRS + k // 2 + 1))
                for j in range(2):
                    act.wait_ge(t_ready, exps_before(i, s, k) + (j + 1))
                    nc.scalar.activation(prob[:, k % PR, j * CH:(j + 1) * CH], ps_t[:, j, :], ACT.Exp,
                                         scale=SCALE).then_inc(exp_done, 1)

            def maxima(at, i, s):
                act.wait_ge(row_ready, i * SLOTS + (s + 1))
                nc.scalar.activation(q_st[3 * HD:ROWS, s % SLOTS, :], ps_s[0:3, at].rearrange("p a b -> p (a b)"),
                                     ACT.Copy).then_inc(row_done, 1)

            def odd_values(i, s):
                act.wait_ge(v_done, i * (SLOTS * PAIRS) + ((s + 1) * PAIRS + PR // 2))
                act.wait_ge(o_out, i * SLOTS + (s + 1))
                nc.scalar.activation(o_odd[0:2 * HD, :], ps_o[2 * HD:4 * HD, :], ACT.Copy).then_inc(o_half, 1)

            def odd_sums(i, s):
                act.wait_ge(d_done, i * (SLOTS * BLOCKS) + ((s + 1) * BLOCKS + PAIR_SLOTS // 2))
                act.wait_ge(d_out, i * SLOTS + (s + 1))
                nc.scalar.activation(d_odd[0:2 * HD, :], ps_d[2 * HD:4 * HD, :], ACT.Copy).then_inc(d_half, 1)

            def unit(i, s, first=False):
                for k in range(KB):
                    exps(i, s, k)
                    if k == 1 and not first:
                        odd_values(i, s - 1)
                    if k == 3 and not first:
                        odd_sums(i, s - 1)
                    if k == KB - 4 and not (isinstance(i, int) and i * SLOTS + s + 1 > LAST):
                        at = (PROLOGUE + s * (NS + 1) + uses.index(("turn", 0))) % 2
                        maxima(at, i, s + 1)

            act.sem_inc(exp_done, 2)
            maxima(NS % 2, 0, 0)
            unit(0, 0, first=True)
            with act.Fori(0, LOOPS) as i:
                for s in range(1, SLOTS + 1):
                    unit(i, s)
            for s in range(1, SLOTS):
                unit(LOOPS, s)
            odd_values(LOOPS, SLOTS - 1)
            odd_sums(LOOPS, SLOTS - 1)

        @block.vector
        def _(dve):
            CHAIN = 5

            def tile_max(at, i, s, n):
                dve.wait_ge(s_ready, stream(i, s, n + 1))
                tile = ps_s[:, at].rearrange("p a b -> p (a b)")
                to = mx[:, s % 2, n:n + 1]
                if mask:
                    nc.vector.memset(pace[:, n:n + 1], 0.0)
                    nc.vector.tensor_tensor_reduce(out=junk[:, n, :], in0=tile, in1=neg[:, n, :], scale=1.0, scalar=LOWEST,
                                                   op0=ALU.add, op1=ALU.max, accum_out=to).then_inc(s_done, 1)
                else:
                    nc.vector.reduce_max(to, tile, AX.X).then_inc(s_done, 1)

            def split_maxima(i, s):
                at = i * (SLOTS * CHAIN) + s * CHAIN
                dve.wait_ge(s_done, stream(i, s, NS))
                halves = mx[:, s % 2].rearrange("p (q h) -> p q h", h=HALVES)
                nc.vector.tensor_tensor(top[:], halves[:, :, 0], halves[:, :, HALVES - 1], ALU.max).then_inc(top_chain, 1)
                dve.wait_ge(top_chain, at + 1)
                nc.vector.tensor_copy(parts[:, :, 0], top[:]).then_inc(top_chain, 1)
                dve.wait_ge(top_chain, at + 2)
                nc.vector.tensor_tensor(rest[:, 0], top[:], parts[:, :, 0], ALU.subtract).then_inc(top_chain, 1)
                dve.wait_ge(top_chain, at + 3)
                nc.vector.tensor_copy(parts[:, :, 1], rest[:, 0]).then_inc(top_chain, 1)
                dve.wait_ge(top_chain, at + 4)
                nc.vector.tensor_tensor(rest[:, 1], rest[:, 0], parts[:, :, 1], ALU.subtract).then_inc(top_chain, 1)
                dve.wait_ge(top_chain, at + 5)
                nc.vector.tensor_copy(parts[:, :, 2], rest[:, 1]).then_inc(parts_done, 1)

            def outputs(i, s):
                slot = s % 2
                dve.wait_ge(o_half, i * SLOTS + (s + 1))
                dve.wait_ge(stored[slot], i * (SLOTS // 2 * 64) + (s // 2 * 64 + 64))
                nc.vector.tensor_tensor(o_sb[0:2 * HD, slot, :], ps_o[0:2 * HD, :], o_odd[0:2 * HD, :], ALU.add).then_inc(o_out, 1)

            def outputs_sums(i, s):
                dve.wait_ge(d_half, i * SLOTS + (s + 1))
                nc.vector.tensor_tensor(d_sb[0:2 * HD, s % 2, :], ps_d[0:2 * HD, :], d_odd[0:2 * HD, :], ALU.add).then_inc(d_out, 1)

            def use_tile(i, s, n, x):
                ahead = 1 + (LEAD + n) // NS
                if isinstance(i, int) and i * SLOTS + s + ahead > LAST:
                    return
                tile_max((PROLOGUE + s * (NS + 1) + x) % 2, i, s + ahead, (LEAD + n) % NS)
                if (LEAD + n) % NS == NS - 1:
                    split_maxima(i, s + ahead)

            def unit(i, s, first=False):
                for k in range(KB):
                    if k == 2 and not first:
                        outputs(i, s - 1)
                    if k == 4 and not first:
                        outputs_sums(i, s - 1)
                    for kind, n, x in steps[k]:
                        if kind == "tile":
                            use_tile(i, s, n, x)

            dve.sem_inc(o_out, 1)
            dve.sem_inc(d_out, 1)
            for slot in range(SLOTS):
                nc.vector.memset(k_st[3 * HD:ROWS, slot, :].bitcast(F32), -1.0).then_inc(minus_ones, 1)
            if mask:
                dve.wait_ge(mask_loaded, 48)
            for x in range(PROLOGUE):
                n = x - (x > NS)
                if x != NS:
                    tile_max(x % 2, 0, n // NS, n % NS)
                    if n == NS - 1:
                        split_maxima(0, 0)
            unit(0, 0, first=True)
            with dve.Fori(0, LOOPS) as i:
                for s in range(1, SLOTS + 1):
                    unit(i, s)
            for s in range(1, SLOTS):
                unit(LOOPS, s)
            outputs(LOOPS, SLOTS - 1)
            outputs_sums(LOOPS, SLOTS - 1)


class RowNorm:

    def __init__(self, nc, core, gain, shift, rows_ready, per_chunk, credit):
        self.nc, self.gain, self.shift = nc, gain, shift
        self.rows_ready, self.per_chunk, self.credit = rows_ready, per_chunk, credit
        self.g_row = core.sbuf("g_row", [P, D])
        self.s_row = core.sbuf("s_row", [P, D])
        self.stats = core.sbuf("stats", [P, RT, 6])
        self.mv = core.sbuf("mv", [P, RT, 2])
        self.eps = core.sbuf("eps", [P, 1])
        self.pace = core.sbuf("pace", [P, 8])
        self.std = core.sbuf("std", [P, RT])
        self.rstd = core.sbuf("rstd", [P, RT])
        self.loaded = core.sem("norm_loaded")
        self.eps_set = core.sem("norm_eps_set")
        self.stats_done = core.sem("norm_stats")
        self.var_done = core.sem("norm_var")
        self.std_done = core.sem("norm_std")
        self.rstd_done = core.sem("norm_rstd")
        self.centred = core.sem("norm_centred")
        self.gained = core.sem("norm_gained")
        self.done = core.sem("norm_done")

    def sync_start(self, sp):
        sp.dma_start(self.g_row[:], row_bias(self.gain)).then_inc(self.loaded, 16)
        sp.dma_start(self.s_row[:], row_bias(self.shift)).then_inc(self.loaded, 16)

    def vector_start(self, dve):
        self.nc.vector.memset(self.eps[:], EPS).then_inc(self.eps_set, 1)

    def scalar_start(self, act):
        act.wait_ge(self.eps_set, 1)

    def vector(self, dve, y, c):
        nc = self.nc
        for r in range(RT):
            dve.wait_ge(self.rows_ready, c * self.per_chunk + self.credit + self.per_chunk - RT + r + 1)
            nc.vector.bn_stats(self.stats[:, r, :], y[:, r, :]).then_inc(self.stats_done, 1)
        dve.wait_ge(self.stats_done, (c + 1) * RT)
        nc.vector.memset(self.pace[:], 0.0)
        for r in range(RT):
            nc.vector.bn_aggr(self.mv[:, r, :], self.stats[:, r, :]).then_inc(self.var_done, 1)
        dve.wait_ge(self.std_done, c + 1)
        nc.vector.reciprocal(self.rstd[:], self.std[:]).then_inc(self.rstd_done, 1)
        dve.wait_ge(self.rstd_done, c + 1)
        for r in range(RT):
            nc.vector.tensor_scalar(y[:, r, :], y[:, r, :], self.mv[:, r, 0:1], self.rstd[:, r:r + 1], ALU.subtract,
                                    ALU.mult).then_inc(self.centred, 1)

    def scalar(self, act, c):
        act.wait_ge(self.var_done, c * RT + RT)
        self.nc.scalar.activation(self.std[:], self.mv[:, :, 1], ACT.Sqrt, bias=self.eps[:, 0:1]).then_inc(self.std_done, 1)

    def pool(self, pool, y, c):
        pool.wait_ge(self.loaded, 32)
        for r in range(RT):
            pool.wait_ge(self.centred, c * RT + r + 1)
            self.nc.gpsimd.tensor_tensor(y[:, r, :], y[:, r, :], self.g_row[:], ALU.mult).then_inc(self.gained, 1)
            pool.wait_ge(self.gained, c * RT + r + 1)
            self.nc.gpsimd.tensor_tensor(y[:, r, :], y[:, r, :], self.s_row[:], ALU.add).then_inc(self.done, 1)


def close_attention(nc, const, tag, oT, sums, over_sums, w, bias, residual, norm, out):
    CB = SQ // CH
    CHUNKS = B * CB
    with ExitStack() as stack:
        core = Core(nc, stack, tag)
        w_stage = core.sbuf("w_stage", [P, KT, D])
        w_hi = core.sbuf("w_hi", [P, KT, D], F32R)
        w_lo = core.sbuf("w_lo", [P, KT, D], F32R)
        b_row = core.sbuf("b_row", [P, D])
        sums_in = core.sbuf("sums_in", [P, 2, UNITS * SQ // P])
        o_hi = core.sbuf("o_hi", [P, CHUNKS, KT, CH], F32R)
        o_lo = core.sbuf("o_lo", [P, CHUNKS, KT, CH], F32R)
        o = core.sbuf("o", [P, 2, KT, CH])
        y = core.sbuf("y", [P, CHUNKS, RT, D])
        ps_y = core.psum("ps_y", [P, 8, CH])
        w_loaded = core.sem("w_loaded")
        b_loaded = core.sem("b_loaded")
        w_hi_done = core.sem("w_hi_done")
        w_done = core.sem("w_done")
        o_loaded = [core.sem(f"o_loaded{c}") for c in range(CHUNKS)]
        y_loaded = [core.sem(f"y_loaded{c}") for c in range(CHUNKS)]
        over_loaded = [core.sem(f"over_loaded{c}") for c in range(CHUNKS)]
        sums_loaded = core.sem("sums_loaded")
        over_done = core.sem("over_done")
        over_stored = core.sem("over_stored")
        o_divided = core.sem("o_divided")
        o_hi_done = core.sem("o_hi_done")
        o_done = core.sem("o_done")
        biased = core.sem("biased")
        y_ready = core.sem("y_ready")
        y_done = core.sem("y_done")
        stored = core.sem("stored")
        row_norm = RowNorm(nc, core, *norm, y_done, RT, 8) if norm else None
        block = stack.enter_context(nc.Block())

        @block.sync
        def _(sp):
            flat = [a.rearrange("u (a f) -> (u a) f", a=P // UNITS) for a in (sums, over_sums)]

            def load_outputs(c):
                b, j = divmod(c, CB)
                sp.dma_start(o_lo[:, c].bitcast(F32),
                             oT[b * D:(b + 1) * D, j * CH:(j + 1) * CH].rearrange("(k p) q -> p k q", p=P)).then_inc(o_loaded[c], 16)

            sp.dma_start(sums_in[:, 0, :], flat[0]).then_inc(sums_loaded, 16)
            load_outputs(0)
            sp.dma_start(w_stage[:], w.rearrange("(k p) n -> p k n", p=P)).then_inc(w_loaded, 16)
            sp.wait_ge(over_done, 1)
            sp.dma_start(flat[1], sums_in[:, 1, :]).then_inc(over_stored, 16)
            sp.dma_start(b_row[:], row_bias(bias)).then_inc(b_loaded, 16)
            if norm:
                row_norm.sync_start(sp)
            sp.wait_ge(over_stored, 16)
            for c in range(CHUNKS):
                b, j = divmod(c, CB)
                if c > 0:
                    load_outputs(c)
                by_head = over_sums[b * HEADS:(b + 1) * HEADS, j * CH:(j + 1) * CH].rearrange("(k h) q -> h k q", h=P // HD)
                for h in range(P // HD):
                    sp.dma_start(o_hi[h * HD:(h + 1) * HD, c].bitcast(F32),
                                 by_head[h:h + 1].broadcast_to([HD, KT, CH])).then_inc(over_loaded[c], 16)
                sp.dma_start(y[:, c], residual[c * CH:(c + 1) * CH, :].rearrange("(r p) d -> p r d", p=P)).then_inc(
                    y_loaded[c], 16)

        @block.tensor
        def _(pe):
            pe.wait_ge(w_done, 1)
            for c in range(CHUNKS):
                pe.wait_ge(o_done, c + 1)
                for r in range(RT):
                    pe.wait_ge(y_done, c * RT + r + 1)
                    rows = slice(r * P, (r + 1) * P)
                    for k in range(KT):
                        for i, (stationary, moving) in enumerate(((o_hi[:, c, k, rows], w_hi[:, k, :]),
                                                                  (o_hi[:, c, k, rows], w_lo[:, k, :]),
                                                                  (o_lo[:, c, k, rows], w_hi[:, k, :]))):
                            mm = nc.tensor.matmul(ps_y[:, c % 2 * RT + r, :], stationary, moving, start=(k == 0 and i == 0),
                                                  stop=(k == KT - 1 and i == 2))
                    mm.then_inc(y_ready, 1)

        @block.scalar
        def _(act):
            act.wait_ge(w_loaded, 16)
            nc.scalar.activation(w_hi[:], w_stage[:], ACT.Copy).then_inc(w_hi_done, 1)
            if norm:
                row_norm.scalar_start(act)
            for c in range(CHUNKS + 2):
                if c < CHUNKS:
                    act.wait_ge(o_divided, c + 1)
                    nc.scalar.activation(o_hi[:, c], o[:, c % 2], ACT.Copy).then_inc(o_hi_done, 1)
                if norm and 2 <= c < CHUNKS + 2:
                    row_norm.scalar(act, c - 2)

        @block.vector
        def _(dve):
            dve.sem_inc(y_done, 8)
            if norm:
                row_norm.vector_start(dve)
            dve.wait_ge(sums_loaded, 16)
            nc.vector.reciprocal(sums_in[:, 1, :], sums_in[:, 0, :]).then_inc(over_done, 1)
            dve.wait_ge(w_hi_done, 1)
            nc.vector.tensor_tensor(w_lo[:], w_stage[:], w_hi[:].bitcast(F32), ALU.subtract).then_inc(w_done, 1)
            for c in range(CHUNKS + 2):
                if c < CHUNKS:
                    dve.wait_ge(o_loaded[c], 16)
                    dve.wait_ge(over_loaded[c], 16 * (P // HD))
                    if c >= 2:
                        dve.wait_ge(o_done, c - 1)
                    nc.vector.tensor_tensor(o[:, c % 2], o_lo[:, c].bitcast(F32), o_hi[:, c].bitcast(F32),
                                            ALU.mult).then_inc(o_divided, 1)
                if 1 <= c <= CHUNKS:
                    dve.wait_ge(o_hi_done, c)
                    nc.vector.tensor_tensor(o_lo[:, c - 1], o[:, (c - 1) % 2], o_hi[:, c - 1].bitcast(F32),
                                            ALU.subtract).then_inc(o_done, 1)
                if c >= 2:
                    dve.wait_ge(biased, c - 1)
                    for r in range(RT):
                        dve.wait_ge(y_ready, (c - 2) * RT + r + 1)
                        nc.vector.tensor_tensor(y[:, c - 2, r, :], ps_y[:, c % 2 * RT + r, :], y[:, c - 2, r, :],
                                                ALU.add).then_inc(y_done, 1)
                    if norm:
                        row_norm.vector(dve, y[:, c - 2], c - 2)

        @block.gpsimd
        def _(pool):
            pool.wait_ge(b_loaded, 16)
            for c in range(CHUNKS):
                pool.wait_ge(y_loaded[c], 16)
                nc.gpsimd.tensor_tensor(y[:, c], y[:, c], b_row[:].unsqueeze(1).broadcast_to([P, RT, D]), ALU.add).then_inc(
                    biased, 1)
            for c in range(CHUNKS):
                if norm:
                    row_norm.pool(pool, y[:, c], c)
                    pool.wait_ge(row_norm.done, (c + 1) * RT)
                else:
                    pool.wait_ge(y_done, (c + 1) * RT + 8)
                pool.dma_start(out[c * CH:(c + 1) * CH, :].rearrange("(r p) d -> p r d", p=P), y[:, c]).then_inc(stored, 16)
            pool.wait_ge(stored, CHUNKS * 16)


def feed_forward(nc, const, tag, src, w1, b1, w2, b2, function, norm, out):
    CB = SQ // CH
    F = w1.shape[1]
    FT = F // P
    WP = 8
    STAGES = 4
    PIECE = F * KT // WP
    HR = 3
    with ExitStack() as stack:
        core = Core(nc, stack, tag)
        w_stage = core.sbuf("w_stage", [P, STAGES, PIECE])
        w1_hi = core.sbuf("w1_hi", [P, KT, F], F32R)
        w1_lo = core.sbuf("w1_lo", [P, KT, F], F32R)
        w2_hi = core.sbuf("w2_hi", [P, FT, D], F32R)
        w2_lo = core.sbuf("w2_lo", [P, FT, D], F32R)
        b1_col = core.sbuf("b1_col", [P, FT])
        b2_row = core.sbuf("b2_row", [P, D])
        y = core.sbuf("y", [P, 2, RT, D])
        xT_hi = core.sbuf("xT_hi", [P, KT, CH], F32R)
        xT_lo = core.sbuf("xT_lo", [P, KT, CH], F32R)
        h = core.sbuf("h", [P, 2, CH])
        h_hi = core.sbuf("h_hi", [P, HR, CH], F32R)
        h_lo = core.sbuf("h_lo", [P, HR, CH], F32R)
        ps_x = core.psum("ps_x", [P, 2, CH])
        ps_h = core.psum("ps_h", [P, 2, CH])
        ps_y = core.psum("ps_y", [P, RT, D])
        w_loaded = [core.sem(f"w_loaded{n}") for n in range(STAGES)]
        b1_loaded = core.sem("b1_loaded")
        b2_loaded = core.sem("b2_loaded")
        w1_hi_done = core.sem("w1_hi_done")
        w1_done = core.sem("w1_done")
        w2_hi_done = core.sem("w2_hi_done")
        w2_done = core.sem("w2_done")
        x_loaded = [core.sem(f"x_loaded{s}") for s in range(2)]
        x_turned = core.sem("x_turned")
        x_hi_done = core.sem("x_hi_done")
        x_done = core.sem("x_done")
        biased = core.sem("biased")
        h_ready = core.sem("h_ready")
        h_act_done = core.sem("h_act_done")
        h_done = core.sem("h_done")
        h_used = core.sem("h_used")
        y_done = core.sem("y_done")
        stored = [core.sem(f"stored{s}") for s in range(2)]
        row_norm = RowNorm(nc, core, *norm, y_done, RT, RT) if norm else None
        block = stack.enter_context(nc.Block())
        NP = 2 * WP

        def piece(n):
            if n < WP:
                k, part = n * KT // WP, n % (WP // KT)
                cols = slice(part * PIECE, (part + 1) * PIECE)
                return w1[k * P:(k + 1) * P, cols], w1_hi[:, k, cols], w1_lo[:, k, cols]
            n -= WP
            per = FT // WP
            return (w2[n * per * P:(n + 1) * per * P, :].rearrange("(k p) d -> p k d", p=P),
                    w2_hi[:, n * per:(n + 1) * per, :].rearrange("p k d -> p (k d)"),
                    w2_lo[:, n * per:(n + 1) * per, :].rearrange("p k d -> p (k d)"))

        def hidden_slot(t):
            return t % HR

        @block.sync
        def _(sp):
            with nc.allow_non_contiguous_dma(reason="a bias, one element per partition"):
                sp.dma_start(b1_col[:], b1.rearrange("(t p) -> p t", p=P)).then_inc(b1_loaded, 16)
            sp.dma_start(b2_row[:], row_bias(b2)).then_inc(b2_loaded, 16)
            if norm:
                row_norm.sync_start(sp)

            def load_rows(b, j):
                row = (b * CB + j) * CH
                sp.dma_start(y[:, j], src[row:row + CH, :].rearrange("(r p) d -> p r d", p=P)).then_inc(
                    x_loaded[j], 16)

            load_rows(0, 0)
            for n in range(NP):
                if n == WP:
                    load_rows(0, 1)
                if n >= STAGES:
                    before = n - STAGES + 1
                    sp.wait_ge(*((w1_done, before) if before <= WP else (w2_done, before - WP)))
                to = w_stage[:, n % STAGES]
                sp.dma_start(to if n < WP else to.rearrange("p (k d) -> p k d", d=D), piece(n)[0]).then_inc(
                    w_loaded[n % STAGES], 16)
            for b in range(1, B):
                for j in range(CB):
                    sp.wait_ge(stored[j], b * 16)
                    load_rows(b, j)

        @block.tensor
        def _(pe):
            with pe.Fori(0, B) as b:
                for j in range(CB):
                    c = b * CB + j
                    pe.wait_ge(x_loaded[j], (b + 1) * 16)
                    for k in range(KT):
                        pe.wait_ge(x_done, c * KT + k + 1)
                        for r in range(RT):
                            turn = nc.tensor.transpose(ps_x[:, k % 2, r * P:(r + 1) * P], y[:, j, r, k * P:(k + 1) * P],
                                                       const["ident"][:])
                        turn.then_inc(x_turned, 1)
                    pe.wait_ge(x_done, (c + 1) * KT + 2)

                    def hidden(t):
                        pe.wait_ge(w1_done, WP)
                        pe.wait_ge(h_act_done, c * (2 * FT) + 2 * t + 1)
                        cols = slice(t * P, (t + 1) * P)
                        for k in range(KT):
                            for i, (stationary, moving) in enumerate(((w1_hi[:, k, cols], xT_hi[:, k, :]),
                                                                      (w1_lo[:, k, cols], xT_hi[:, k, :]),
                                                                      (w1_hi[:, k, cols], xT_lo[:, k, :]))):
                                mm = nc.tensor.matmul(ps_h[:, t % 2, :], stationary, moving, start=(k == 0 and i == 0),
                                                      stop=(k == KT - 1 and i == 2))
                        mm.then_inc(h_ready, 1)

                    def output(t):
                        pe.wait_ge(h_done, c * FT + t + 1 + 2)
                        s = hidden_slot(t)
                        pe.wait_ge(w2_done, t // (FT // WP) + 1)
                        for r in range(RT):
                            if t == 0:
                                pe.wait_ge(y_done, c * RT + r + 1)
                            rows = slice(r * P, (r + 1) * P)
                            for i, (stationary, moving) in enumerate(((h_hi[:, s, rows], w2_hi[:, t, :]),
                                                                      (h_hi[:, s, rows], w2_lo[:, t, :]),
                                                                      (h_lo[:, s, rows], w2_hi[:, t, :]))):
                                mm = nc.tensor.matmul(ps_y[:, r, :], stationary, moving, start=(t == 0 and i == 0),
                                                      stop=(t == FT - 1 and i == 2))
                        mm.then_inc(h_used, 1)

                    for t in range(FT):
                        hidden(t)
                        if t > 0:
                            output(t - 1)
                    output(FT - 1)

        @block.scalar
        def _(act):
            act.sem_inc(h_act_done, 3)
            for n in range(WP):
                act.wait_ge(w_loaded[n % STAGES], (n // STAGES + 1) * 16)
                nc.scalar.activation(piece(n)[1], w_stage[:, n % STAGES], ACT.Copy).then_inc(w1_hi_done, 1)
            act.wait_ge(b1_loaded, 16)
            if norm:
                row_norm.scalar_start(act)
            with act.Fori(0, B) as b:
                for j in range(CB):
                    c = b * CB + j
                    for k in range(KT):
                        act.wait_ge(x_turned, c * KT + k + 1)
                        nc.scalar.activation(xT_hi[:, k, :], ps_x[:, k % 2, :], ACT.Copy).then_inc(x_hi_done, 1)
                    for t in range(FT):
                        s = hidden_slot(t)
                        act.wait_ge(h_ready, c * FT + t + 1)
                        act.wait_ge(h_used, c * FT + t + 1)
                        nc.scalar.activation(h_hi[:, s, :], ps_h[:, t % 2, :], function, bias=b1_col[:, t:t + 1]).then_inc(
                            h_act_done, 1)
                        act.wait_ge(h_done, c * FT + t + 1)
                        nc.scalar.activation(h[:, t % 2, :], ps_h[:, t % 2, :], function, bias=b1_col[:, t:t + 1]).then_inc(
                            h_act_done, 1)
                    if norm:
                        row_norm.scalar(act, c)

        @block.vector
        def _(dve):
            dve.sem_inc(x_done, 2)
            dve.sem_inc(y_done, RT)
            dve.sem_inc(h_done, 2)
            if norm:
                row_norm.vector_start(dve)
            for n in range(WP):
                dve.wait_ge(w1_hi_done, n + 1)
                _, hi, lo = piece(n)
                nc.vector.tensor_tensor(lo, w_stage[:, n % STAGES], hi.bitcast(F32), ALU.subtract).then_inc(w1_done, 1)
            with dve.Fori(0, B) as b:
                for j in range(CB):
                    c = b * CB + j
                    for k in range(KT):
                        dve.wait_ge(x_hi_done, c * KT + k + 1)
                        nc.vector.tensor_tensor(xT_lo[:, k, :], ps_x[:, k % 2, :], xT_hi[:, k, :].bitcast(F32),
                                                ALU.subtract).then_inc(x_done, 1)
                    for t in range(FT):
                        dve.wait_ge(h_act_done, c * (2 * FT) + 2 * t + 2 + 3)
                        nc.vector.tensor_tensor(h_lo[:, hidden_slot(t), :], h[:, t % 2, :],
                                                h_hi[:, hidden_slot(t), :].bitcast(F32), ALU.subtract).then_inc(h_done, 1)
                    dve.wait_ge(biased, c + 1)
                    dve.wait_ge(h_used, (c + 1) * FT + HR)
                    for r in range(RT):
                        nc.vector.tensor_tensor(y[:, j, r, :], ps_y[:, r, :], y[:, j, r, :], ALU.add).then_inc(y_done, 1)
                    if norm:
                        row_norm.vector(dve, y[:, j], c)

        @block.gpsimd
        def _(pool):
            pool.sem_inc(h_used, HR)
            for n in range(WP, NP):
                _, hi, lo = piece(n)
                pool.wait_ge(w_loaded[n % STAGES], (n // STAGES + 1) * 16)
                nc.gpsimd.tensor_copy(hi, w_stage[:, n % STAGES]).then_inc(w2_hi_done, 1)
                pool.wait_ge(w2_hi_done, n - WP + 1)
                nc.gpsimd.tensor_tensor(lo, w_stage[:, n % STAGES], hi.bitcast(F32), ALU.subtract).then_inc(w2_done, 1)
            pool.wait_ge(b2_loaded, 16)
            with pool.Fori(0, B) as b:
                for j in range(CB):
                    c = b * CB + j
                    pool.wait_ge(x_turned, (c + 1) * KT)
                    nc.gpsimd.tensor_tensor(y[:, j], y[:, j], b2_row[:].unsqueeze(1).broadcast_to([P, RT, D]), ALU.add).then_inc(
                        biased, 1)
                    if norm:
                        row_norm.pool(pool, y[:, j], c)
                        pool.wait_ge(row_norm.done, (c + 1) * RT)
                    else:
                        pool.wait_ge(y_done, (c + 1) * RT + RT)
                    pool.dma_start(out[ds(pool.snap(c * CH), CH), :].rearrange("(r p) d -> p r d", p=P), y[:, j]).then_inc(stored[j], 16)
            for j in range(CB):
                pool.wait_ge(stored[j], B * 16)


def prepare_mask(nc, const, tag, mask, neg_out, negT_out, live_out):
    T = SQ // P
    with ExitStack() as stack:
        core = Core(nc, stack, tag)
        m_in = core.sbuf("m_in", [P, T, SQ], I32)
        off = core.sbuf("off", [P, T, SQ], BF16)
        neg = core.sbuf("neg", [P, T, SQ], BF16)
        negT = core.sbuf("negT", [P, T, SQ], BF16)
        all_off = core.sbuf("all_off", [P, T])
        live = core.sbuf("live", [P, T], BF16)
        weight = core.sbuf("weight", [P, T])
        live_row = core.sbuf("live_row", [P, T, P])
        ps_n = core.psum("ps_n", [P, 4, SQ], BF16)
        ps_l = core.psum("ps_l", [P, T, P])
        loaded = core.sem("loaded")
        off_done = core.sem("off_done")
        all_done = core.sem("all_done")
        live_done = core.sem("live_done")
        neg_done = core.sem("neg_done")
        neg_turned = core.sem("neg_turned")
        negT_done = core.sem("negT_done")
        rows_ready = core.sem("rows_ready")
        rows_done = core.sem("rows_done")
        stored = core.sem("stored")
        block = stack.enter_context(nc.Block())

        @block.sync
        def _(sp):
            sp.dma_start(m_in[:], mask.rearrange("(t p) k -> p t k", p=P)).then_inc(loaded, 16)
            sp.wait_ge(neg_done, T)
            sp.dma_start(neg_out, neg[:]).then_inc(stored, 16)
            sp.wait_ge(rows_done, 1)
            sp.dma_start(live_out, live_row[:].rearrange("p t k -> p (t k)")).then_inc(stored, 16)
            sp.wait_ge(negT_done, T + 4)
            sp.dma_start(negT_out, negT[:]).then_inc(stored, 16)
            sp.wait_ge(stored, 48)

        @block.vector
        def _(dve):
            dve.wait_ge(loaded, 16)
            for t in range(T):
                nc.vector.tensor_scalar(off[:, t, :], m_in[:, t, :], 0.0, -1.0, ALU.not_equal, ALU.add).then_inc(off_done, 1)
            for t in range(T):
                dve.wait_ge(off_done, t + 1)
                nc.vector.reduce_max(all_off[:, t:t + 1], off[:, t, :], AX.X).then_inc(all_done, 1)
            dve.wait_ge(all_done, T)
            nc.vector.tensor_scalar(live[:], all_off[:], 1.0, None, ALU.add).then_inc(live_done, 1)
            nc.vector.tensor_scalar(weight[:], all_off[:], 1.0, -NEG, ALU.add, ALU.mult).then_inc(live_done, 1)
            dve.wait_ge(live_done, 2)
            for t in range(T):
                nc.vector.tensor_scalar(neg[:, t, :], off[:, t, :], weight[:, t:t + 1], None, ALU.mult).then_inc(neg_done, 1)

        @block.tensor
        def _(pe):
            pe.wait_ge(live_done, 1)
            for t in range(T):
                mm = nc.tensor.matmul(ps_l[:, t, :], live[:, t:t + 1].broadcast_to([P, P]), const["identb"][:],
                                      start=True, stop=True)
            mm.then_inc(rows_ready, 1)
            pe.wait_ge(neg_done, T)
            for k in range(T):
                pe.wait_ge(negT_done, k + 1)
                for t in range(T):
                    turn = nc.tensor.transpose(ps_n[:, k % 4, t * P:(t + 1) * P], neg[:, t, k * P:(k + 1) * P],
                                               const["identb"][:])
                turn.then_inc(neg_turned, 1)

        @block.scalar
        def _(act):
            act.sem_inc(negT_done, 4)
            act.wait_ge(rows_ready, 1)
            nc.scalar.activation(live_row[:], ps_l[:], ACT.Copy).then_inc(rows_done, 1)
            for k in range(T):
                act.wait_ge(neg_turned, k + 1)
                nc.scalar.activation(negT[:, k, :], ps_n[:, k % 4, :], ACT.Copy).then_inc(negT_done, 1)


_INS = ["x", "ctx_1024", "mask_1x1xSxS_ik0"] + [f"L0_xattn_{n}" for n in
        ("Wq", "bq", "Wk", "bk", "Wv", "bv", "Wo", "bo", "W1", "b1", "W2", "b2")] + [f"L1_xattn_{n}" for n in
        ("sa_qw", "sa_qb", "sa_kw", "sa_kb", "sa_vw", "sa_vb", "sa_ow", "sa_ob", "ca_qw", "ca_qb", "ca_kw", "ca_kb",
         "ca_vw", "ca_vb", "ca_ow", "ca_ob", "w1", "b1", "w2", "b2", "g1", "be1", "g2", "be2", "g3", "be3")]


def build_program(nc, ins, out):
    x = ins["x"].rearrange("b s d -> (b s) d")
    context = ins["ctx_1024"].rearrange("b s d -> (b s) d")
    mask = ins["mask_1x1xSxS_ik0"].rearrange("a b q k -> (a b q) k")
    out_rows = out.rearrange("b s d -> (b s) d")
    p = {n.removeprefix("L0_xattn_"): a for n, a in ins.items() if n.startswith("L0_")}
    t = {n.removeprefix("L1_xattn_"): a for n, a in ins.items() if n.startswith("L1_")}
    SC = ins["ctx_1024"].shape[1]

    def dram(name, shape, dtype=F32):
        return nc.dram_tensor(name, shape, dtype).ap()

    def keys(name, s):
        return dram(f"{name}_hi", (B * D, s)), dram(f"{name}_lo", (B * D, s))

    k0, k2, k1 = keys("k0", SC), keys("k2", SC), keys("k1", SQ)
    q0, q1, q2 = keys("q0", SQ), keys("q1", SQ), keys("q2", SQ)
    v0, v2 = (dram(n, (UNITS, P, SC // P * HD)) for n in ("v0", "v2"))
    v1 = dram("v1", (UNITS, P, SQ // P * HD))
    o0, o1, o2 = ((dram(n, (B * D, SQ)), dram(f"{n}_sums", (UNITS, SQ))) for n in ("o0", "o1", "o2"))
    over = [dram(f"over_sums{n}", (UNITS, SQ)) for n in range(3)]
    rows = [dram(f"rows{n}", (B * SQ, D)) for n in range(4)]
    T = SQ // P
    neg, negT = dram("neg", (P, T, SQ), BF16), dram("negT", (P, T, SQ), BF16)
    live = dram("live", (P, SQ))

    with ExitStack() as stack:
        const = {
            "ident": stack.enter_context(nc.sbuf_tensor("ident", [P, P], F32)),
            "identb": stack.enter_context(nc.sbuf_tensor("identb", [P, P], BF16)),
            "ones": stack.enter_context(nc.sbuf_tensor("ones", [P, HD], F32)),
        }
        make_identities(nc, const)
        project(nc, const, "ctx0", context, SC // CH, [
            ("T", p["Wk"], p["bk"], *k0), ("V", p["Wv"], p["bv"], v0),
            ("T", t["ca_kw"], t["ca_kb"], *k2), ("V", t["ca_vw"], t["ca_vb"], v2)])
        project(nc, const, "query0", x, SQ // CH, [("T", p["Wq"], p["bq"], *q0)])
        attention(nc, const, "attn0", *k0, *q0, v0, *o0)
        close_attention(nc, const, "close0", *o0, over[0], p["Wo"], p["bo"], x, None, rows[0])
        feed_forward(nc, const, "ff0", rows[0], p["W1"], p["b1"], p["W2"], p["b2"], ACT.Gelu_apprx_tanh, None, rows[1])
        prepare_mask(nc, const, "mask", mask, neg, negT, live)
        project(nc, const, "self", rows[1], SQ // CH, [("T", t["sa_qw"], t["sa_qb"], *q1), ("T", t["sa_kw"], t["sa_kb"], *k1),
                                                       ("V", t["sa_vw"], t["sa_vb"], v1)])
        attention(nc, const, "attn1", *k1, *q1, v1, *o1, (neg, negT, live))
        close_attention(nc, const, "close1", *o1, over[1], t["sa_ow"], t["sa_ob"], rows[1], (t["g1"], t["be1"]), rows[2])
        project(nc, const, "query2", rows[2], SQ // CH, [("T", t["ca_qw"], t["ca_qb"], *q2)])
        attention(nc, const, "attn2", *k2, *q2, v2, *o2)
        close_attention(nc, const, "close2", *o2, over[2], t["ca_ow"], t["ca_ob"], rows[2], (t["g2"], t["be2"]), rows[3])
        feed_forward(nc, const, "ff1", rows[3], t["w1"], t["b1"], t["w2"], t["b2"], ACT.Relu, (t["g3"], t["be3"]), out_rows)


def kernel(**inputs):
    import numpy as _np
    import concourse.bacc as _bacc
    from concourse import mybir as _mybir
    from concourse.bass_utils import run_bass_kernel_spmd as _run

    nc = _bacc.Bacc("TRN2", target_bir_lowering=False, num_devices=1)
    arrays, aps = {}, {}
    for name in _INS:
        a = _np.ascontiguousarray(inputs[name])
        arrays[f"in_{name}"] = a
        aps[name] = nc.dram_tensor(f"in_{name}", a.shape, _mybir.dt.from_np(a.dtype), kind="ExternalInput").ap()
    shape = tuple(inputs["x"].shape)
    out = nc.dram_tensor("out_rows", shape, F32, kind="ExternalOutput").ap()
    build_program(nc, aps, out)
    r = _run(nc, [arrays], core_ids=[0])
    return r.results[0]["out_rows"]
```

```python
from contextlib import ExitStack

import concourse.bass as bass
from concourse import mybir

F32 = mybir.dt.float32
F32R = mybir.dt.float32r
BF16 = mybir.dt.bfloat16
I32 = mybir.dt.int32
ALU = mybir.AluOpType
ACT = mybir.ActivationFunctionType
AX = mybir.AxisListType

P = 128
D = 512
KT = D // P
HEADS = 16
HD = D // HEADS
B = 2
SQ = 1024
CH = 512
RT = CH // P
UNITS = B * HEADS
SCALE = float(HD) ** -0.5
EPS = 1e-5
NEG = -1.0e9
LOWEST = -3.0e38


def ds(start, size):
    return bass.ds(start, size)


class Core:

    def __init__(self, nc, stack, tag):
        self.nc, self.stack, self.tag = nc, stack, tag
        self.sems = []
        stack.callback(self.clear)

    def clear(self):
        self.nc.clear_and_free_semaphores(self.sems)
        self.nc.all_engine_barrier()

    def sbuf(self, name, shape, dtype=F32):
        return self.stack.enter_context(self.nc.sbuf_tensor(f"{self.tag}_{name}", shape, dtype))

    def psum(self, name, shape, dtype=F32):
        return self.stack.enter_context(self.nc.psum_tensor(f"{self.tag}_{name}", shape, dtype))

    def sem(self, name):
        self.sems.append(self.nc.alloc_semaphore(f"{self.tag}_{name}"))
        return self.sems[-1]


def row_bias(vector, parts=P):
    return vector.rearrange("(o f) -> o f", o=1).broadcast_to([parts, vector.shape[0]])


def make_identities(nc, const):
    s_memset = nc.alloc_semaphore("id_memset")
    s_identity = nc.alloc_semaphore("id_identity")
    with nc.Block() as block:
        @block.gpsimd
        def _(pool):
            nc.gpsimd.memset(const["ident"][:], 1.0).then_inc(s_memset, 1)
            nc.gpsimd.memset(const["ones"][:], 1.0).then_inc(s_memset, 1)
            pool.wait_ge(s_memset, 1)
            nc.gpsimd.affine_select(out=const["ident"][:], in_=const["ident"][:], compare_op=ALU.is_equal,
                                    fill=0.0, base=0, pattern=[[-1, P]], channel_multiplier=1).then_inc(s_identity, 1)

        @block.vector
        def _(dve):
            dve.wait_ge(s_identity, 1)
            nc.vector.tensor_copy(const["identb"][:], const["ident"][:]).then_inc(s_identity, 1)


class MaskTiles:
    TILES = SQ // P

    def __init__(self, nc, core, mask, neg_out, negT_out, live_out):
        T = self.TILES
        self.nc, self.mask, self.neg_out, self.negT_out, self.live_out = nc, mask, neg_out, negT_out, live_out
        self.m_in = core.sbuf("m_in", [P, 2, SQ], I32)
        self.off = core.sbuf("m_off", [P, 2, SQ], BF16)
        self.neg = core.sbuf("m_neg", [P, 2, SQ], BF16)
        self.negT = core.sbuf("m_negT", [P, 2, T, P], BF16)
        self.all_off = core.sbuf("m_all_off", [P, 2])
        self.live = core.sbuf("m_live", [P, 2], BF16)
        self.weight = core.sbuf("m_weight", [P, 2])
        self.live_row = core.sbuf("m_live_row", [P, 2, P])
        self.pace = core.sbuf("m_pace", [P, 2, 4])
        self.ps_n = core.psum("m_ps_n", [P, T, P], BF16)
        self.ps_l = core.psum("m_ps_l", [P, P])
        self.loaded = [core.sem(f"m_loaded{s}") for s in range(2)]
        self.off_done = core.sem("m_off_done")
        self.all_done = core.sem("m_all_done")
        self.live_done = core.sem("m_live_done")
        self.neg_done = core.sem("m_neg_done")
        self.live_turned = core.sem("m_live_turned")
        self.neg_turned = core.sem("m_neg_turned")
        self.live_kept = core.sem("m_live_kept")
        self.negT_kept = core.sem("m_negT_kept")
        self.stored = [core.sem(f"m_stored{s}") for s in range(2)]

    def sync_start(self, sp):
        for s in range(2):
            sp.sem_inc(self.stored[s], 48)
            self.load(sp, s)

    def load(self, sp, t):
        if t >= 2:
            sp.wait_ge(self.off_done, t - 1)
        sp.dma_start(self.m_in[:, t % 2, :], self.mask[t * P:(t + 1) * P, :]).then_inc(self.loaded[t % 2], 16)

    def sync(self, sp, t):
        if 2 <= t + 1 < self.TILES:
            self.load(sp, t + 1)
        rows = slice(t * P, (t + 1) * P)
        sp.wait_ge(self.neg_done, t + 1)
        sp.dma_start(self.neg_out[:, t, :], self.neg[:, t % 2, :]).then_inc(self.stored[t % 2], 16)
        sp.wait_ge(self.live_kept, t + 1)
        sp.dma_start(self.live_out[:, rows], self.live_row[:, t % 2, :]).then_inc(self.stored[t % 2], 16)
        sp.wait_ge(self.negT_kept, t + 1 + 1)
        with self.nc.allow_non_contiguous_dma(reason="a tile's rows are columns here"):
            sp.dma_start(self.negT_out[:, :, rows], self.negT[:, t % 2]).then_inc(self.stored[t % 2], 16)

    def sync_finish(self, sp):
        for s in range(2):
            sp.wait_ge(self.stored[s], 48 + self.TILES // 2 * 48)

    def vector(self, dve, i, s):
        nc, t = self.nc, i * 2 + s
        dve.wait_ge(self.loaded[s], i * 16 + 16)
        nc.vector.memset(self.pace[:, s, 0:1], 0.0)
        nc.vector.tensor_scalar(self.off[:, s, :], self.m_in[:, s, :], 0.0, -1.0, ALU.not_equal, ALU.add).then_inc(self.off_done, 1)
        dve.wait_ge(self.off_done, t + 1)
        nc.vector.reduce_max(self.all_off[:, s:s + 1], self.off[:, s, :], AX.X).then_inc(self.all_done, 1)
        dve.wait_ge(self.all_done, t + 1)
        nc.vector.memset(self.pace[:, s, 1:2], 0.0)
        nc.vector.tensor_scalar(self.live[:, s:s + 1], self.all_off[:, s:s + 1], 1.0, None, ALU.add).then_inc(self.live_done, 1)
        nc.vector.tensor_scalar(self.weight[:, s:s + 1], self.all_off[:, s:s + 1], 1.0, -NEG, ALU.add, ALU.mult).then_inc(
            self.live_done, 1)
        dve.wait_ge(self.live_done, i * 4 + (s * 2 + 2))
        nc.vector.memset(self.pace[:, s, 2:3], 0.0)
        dve.wait_ge(self.stored[s], i * 48 + 48)
        nc.vector.memset(self.pace[:, s, 3:4], 0.0)
        nc.vector.tensor_scalar(self.neg[:, s, :], self.off[:, s, :], self.weight[:, s:s + 1], None, ALU.mult).then_inc(
            self.neg_done, 1)

    def tensor(self, pe, const, i, s):
        nc, t = self.nc, i * 2 + s
        pe.wait_ge(self.live_done, i * 4 + (s * 2 + 1))
        pe.wait_ge(self.negT_kept, t + 1)
        nc.tensor.matmul(self.ps_l[:], self.live[:, s:s + 1].broadcast_to([P, P]), const["identb"][:],
                         start=True, stop=True).then_inc(self.live_turned, 1)
        pe.wait_ge(self.neg_done, t + 1)
        for k in range(self.TILES):
            mm = nc.tensor.transpose(self.ps_n[:, k, :], self.neg[:, s, k * P:(k + 1) * P], const["identb"][:])
        mm.then_inc(self.neg_turned, 1)

    def scalar_start(self, act):
        act.sem_inc(self.negT_kept, 1)

    def scalar(self, act, i, s):
        nc, t = self.nc, i * 2 + s
        act.wait_ge(self.live_turned, t + 1)
        act.wait_ge(self.stored[s], i * 48 + 48)
        nc.scalar.activation(self.live_row[:, s, :], self.ps_l[:], ACT.Copy).then_inc(self.live_kept, 1)
        act.wait_ge(self.neg_turned, t + 1)
        nc.scalar.activation(self.negT[:, s].rearrange("p k q -> p (k q)"), self.ps_n[:].rearrange("p k q -> p (k q)"),
                             ACT.Copy).then_inc(self.negT_kept, 1)


def project(nc, const, tag, src, chunks_per_batch, mats, mask=None):
    CB = chunks_per_batch
    CHUNKS = B * CB
    M = len(mats)
    GROUPS = 4 * M
    T_MATS = [m for m in range(M) if mats[m][0] == "T"]
    V_MATS = [m for m in range(M) if mats[m][0] == "V"]
    TG = 4 * len(T_MATS)
    assert CHUNKS % 2 == 0 and KT == 4
    with ExitStack() as stack:
        core = Core(nc, stack, tag)
        w_stage = core.sbuf("w_stage", [P, 2, KT, D])
        w_hi = core.sbuf("w_hi", [P, M, KT, D], F32R)
        w_lo = core.sbuf("w_lo", [P, M, KT, D], F32R)
        b_col = core.sbuf("b_col", [P, M, KT])
        b_row = core.sbuf("b_row", [P, M, D])
        x = core.sbuf("x", [P, 2, RT, D])
        xT_hi = core.sbuf("xT_hi", [P, 2, KT, CH], F32R)
        xT_lo = core.sbuf("xT_lo", [P, 2, KT, CH], F32R)
        t_hi = core.sbuf("t_hi", [P, 4, CH], F32R)
        t_lo = core.sbuf("t_lo", [P, 4, CH], F32R)
        v_out = core.sbuf("v_out", [P, 2, HEADS, RT, HD])
        ps_x = core.psum("ps_x", [P, 2, CH])
        ps_y = core.psum("ps_y", [P, 4, CH])
        w_loaded = [core.sem(f"w_loaded{m}") for m in range(M)]
        x_loaded = [core.sem(f"x_loaded{s}") for s in range(2)]
        w_split = core.sem("w_split")
        w_done = core.sem("w_done")
        x_turned = core.sem("x_turned")
        x_hi_done = core.sem("x_hi_done")
        x_done = core.sem("x_done")
        y_ready = core.sem("y_ready")
        t_hi_done = core.sem("t_hi_done")
        y_done = core.sem("y_done")
        t_stored = [core.sem(f"t_stored{s}") for s in range(4)]
        v_stored = [core.sem(f"v_stored{s}") for s in range(2)]
        mask_tiles = MaskTiles(nc, core, *mask) if mask else None
        assert not mask or CHUNKS == MaskTiles.TILES and M == 4
        block = stack.enter_context(nc.Block())

        def before(i, s, per):
            return i * (2 * per) + s * per

        def all_pairs(engine, chunk):
            with engine.Fori(0, CHUNKS // 2 - 1) as i:
                chunk(i, 0, False)
                chunk(i, 1, False)
            chunk(CHUNKS // 2 - 1, 0, False)
            chunk(CHUNKS // 2 - 1, 1, True)

        @block.sync
        def _(sp):
            def load(c):
                sp.dma_start(x[:, c % 2], src[c * CH:(c + 1) * CH, :].rearrange("(r p) d -> p r d", p=P)).then_inc(
                    x_loaded[c % 2], 16)

            for g in range(4):
                sp.sem_inc(t_stored[g], 16)
            for v in range(len(V_MATS)):
                sp.sem_inc(v_stored[v], 16)
            load(0)
            for m, mat in enumerate(mats):
                if m >= 2:
                    sp.wait_ge(w_done, m - 1)
                sp.dma_start(w_stage[:, m % 2], mat[1].rearrange("(k p) n -> p k n", p=P)).then_inc(w_loaded[m], 16)
                if mat[0] == "T":
                    with nc.allow_non_contiguous_dma(reason="a bias, one element per partition"):
                        sp.dma_start(b_col[:, m, :], mat[2].rearrange("(k p) -> p k", p=P)).then_inc(w_loaded[m], 16)
                else:
                    sp.dma_start(b_row[:, m, :], row_bias(mat[2])).then_inc(w_loaded[m], 16)
                if m == 0:
                    load(1)
            if mask:
                mask_tiles.sync_start(sp)
            for c in range(CHUNKS):
                b, j = divmod(c, CB)
                if c + 2 < CHUNKS:
                    sp.wait_ge(x_turned, (c + 1) * KT)
                    load(c + 2)
                for m, mat in enumerate(mats):
                    if mask and m == 3:
                        mask_tiles.sync(sp, c)
                    if mat[0] == "T":
                        for g in range(4):
                            sp.wait_ge(y_done, c * GROUPS + m * 4 + g + 1 + 4)
                            for to, part in ((mat[3], t_hi), (mat[4], t_lo)):
                                sp.dma_start(to[b * D + g * P:b * D + (g + 1) * P, j * CH:(j + 1) * CH],
                                             part[:, g, :].bitcast(F32)).then_inc(t_stored[g], 16)
                    else:
                        v = V_MATS.index(m)
                        sp.wait_ge(y_done, c * GROUPS + m * 4 + 4 + 4)
                        sp.dma_start(mat[3][b * HEADS:(b + 1) * HEADS, :, j * RT * HD:(j + 1) * RT * HD].rearrange("h p f -> p h f"),
                                     v_out[:, v].rearrange("p h r d -> p h (r d)")).then_inc(v_stored[v], 16)
            if T_MATS:
                for g in range(4):
                    sp.wait_ge(t_stored[g], 16 + CHUNKS * len(T_MATS) * 32)
            for v in range(len(V_MATS)):
                sp.wait_ge(v_stored[v], 16 + CHUNKS * 16)
            if mask:
                mask_tiles.sync_finish(sp)

        @block.tensor
        def _(pe):
            def turn(i, s, k):
                slot = s % 2
                if k == 0:
                    pe.wait_ge(x_loaded[slot], i * 16 + 16 * (s // 2 + 1))
                pe.wait_ge(x_done, before(i, s, KT) + (k + 1))
                for r in range(RT):
                    mm = nc.tensor.transpose(ps_x[:, k % 2, r * P:(r + 1) * P],
                                             x[:, slot, r, k * P:(k + 1) * P], const["ident"][:])
                mm.then_inc(x_turned, 1)

            def chunk(i, s, last):
                pe.wait_ge(x_done, before(i, s, KT) + (KT + 2))
                for m, mat in enumerate(mats):
                    if mask and m == 2:
                        mask_tiles.tensor(pe, const, i, s)
                    pe.wait_ge(w_done, m + 1)
                    for g in range(4):
                        if m == M - 1 and not last:
                            turn(i, s + 1, g)
                        pe.wait_ge(y_done, before(i, s, GROUPS) + (m * 4 + g + 1))
                        cols = slice(g * P, (g + 1) * P)
                        for k in range(KT):
                            if mat[0] == "T":
                                pairs = ((w_hi[:, m, k, cols], xT_hi[:, s, k, :]), (w_lo[:, m, k, cols], xT_hi[:, s, k, :]),
                                         (w_hi[:, m, k, cols], xT_lo[:, s, k, :]))
                            else:
                                pairs = ((xT_hi[:, s, k, cols], w_hi[:, m, k, :]), (xT_hi[:, s, k, cols], w_lo[:, m, k, :]),
                                         (xT_lo[:, s, k, cols], w_hi[:, m, k, :]))
                            for n, (stationary, moving) in enumerate(pairs):
                                mm = nc.tensor.matmul(ps_y[:, g, :], stationary, moving, start=(k == 0 and n == 0),
                                                      stop=(k == KT - 1 and n == 2))
                        mm.then_inc(y_ready, 1)

            for k in range(KT):
                turn(0, 0, k)
            all_pairs(pe, chunk)

        @block.scalar
        def _(act):
            def split_weights(m):
                act.wait_ge(w_loaded[m], 32)
                nc.scalar.activation(w_hi[:, m], w_stage[:, m % 2], ACT.Copy).then_inc(w_split, 1)

            def keep_turned(i, s, k):
                act.wait_ge(x_turned, before(i, s, KT) + (k + 1))
                nc.scalar.activation(xT_hi[:, s % 2, k, :], ps_x[:, k % 2, :], ACT.Copy).then_inc(x_hi_done, 1)

            def chunk(i, s, last):
                for m in range(M):
                    if mask and m == 2:
                        mask_tiles.scalar(act, i, s)
                    for g in range(4):
                        if m == M - 1 and not last:
                            keep_turned(i, s + 1, g)
                        if m in T_MATS:
                            t = T_MATS.index(m)
                            act.wait_ge(y_ready, before(i, s, GROUPS) + (m * 4 + g + 1))
                            act.wait_ge(t_stored[g], before(i, s, len(T_MATS) * 32) + (t * 32 + 16))
                            nc.scalar.activation(t_hi[:, g, :], ps_y[:, g, :], ACT.Identity,
                                                 bias=b_col[:, m, g:g + 1]).then_inc(t_hi_done, 1)

            split_weights(0)
            for k in range(KT):
                keep_turned(0, 0, k)
            for m in range(1, M):
                split_weights(m)
            if mask:
                mask_tiles.scalar_start(act)
            all_pairs(act, chunk)

        @block.vector
        def _(dve):
            def split_weights(m):
                dve.wait_ge(w_split, m + 1)
                nc.vector.tensor_tensor(w_lo[:, m], w_stage[:, m % 2], w_hi[:, m].bitcast(F32), ALU.subtract).then_inc(w_done, 1)

            def keep_turned(i, s, k):
                dve.wait_ge(x_hi_done, before(i, s, KT) + (k + 1))
                nc.vector.tensor_tensor(xT_lo[:, s % 2, k, :], ps_x[:, k % 2, :], xT_hi[:, s % 2, k, :].bitcast(F32),
                                        ALU.subtract).then_inc(x_done, 1)

            def chunk(i, s, last):
                for m, mat in enumerate(mats):
                    if mask and m == 1:
                        mask_tiles.vector(dve, i, s)
                    for g in range(4):
                        if m == M - 1 and not last:
                            keep_turned(i, s + 1, g)
                        if mat[0] == "T":
                            dve.wait_ge(t_hi_done, before(i, s, TG) + (T_MATS.index(m) * 4 + g + 1))
                            nc.vector.scalar_tensor_tensor(out=t_lo[:, g, :], in0=ps_y[:, g, :], scalar=b_col[:, m, g:g + 1],
                                                           in1=t_hi[:, g, :].bitcast(F32), op0=ALU.add,
                                                           op1=ALU.subtract).then_inc(y_done, 1)
                        else:
                            v = V_MATS.index(m)
                            dve.wait_ge(y_ready, before(i, s, GROUPS) + (m * 4 + g + 1))
                            if g == 0:
                                dve.wait_ge(v_stored[v], before(i, s, 16) + 16)
                            nc.vector.tensor_tensor(v_out[:, v, :, g, :], ps_y[:, g, :].rearrange("p (h d) -> p h d", h=HEADS),
                                                    b_row[:, m, :].rearrange("p (h d) -> p h d", h=HEADS),
                                                    ALU.add).then_inc(y_done, 1)

            dve.sem_inc(x_done, 2)
            dve.sem_inc(y_done, 4)
            split_weights(0)
            for k in range(KT):
                keep_turned(0, 0, k)
            for m in range(1, M):
                split_weights(m)
            all_pairs(dve, chunk)


def attention(nc, const, tag, k_hi, k_lo, q_hi, q_lo, values, outT, sums, over_sums, mask=None):
    S = k_hi.shape[1]
    KB = S // P
    QB = SQ // P
    HALVES = S // 1024
    NS = QB * HALVES
    SLOTS = 4
    PR = 8
    PAIRS = KB // 2
    PAIR_SLOTS = 4
    BLOCKS = KB // 4
    ROWS = 3 * HD + 3
    LEAD = 5
    FILL = [["tile", "values"], ["tile", "tile"], ["sums", "tile"], ["values"]]
    FILL += [["tile", "values"], ["tile", "tile"], ["values", "tile"], ["sums"]] * (BLOCKS - 1)
    quads = mask is not None
    SUMS = BLOCKS // 2 if quads else BLOCKS
    SUMS_FREE = 1 if quads else PAIR_SLOTS // 2
    if quads:
        assert BLOCKS == 2
        FILL = [["tile", "values"], ["tile", "tile"], ["tile"], ["values"], [], ["tile", "tile"], ["values", "tile"], ["values"]]
    SUMS_STEP = 4 if quads else 2
    FILL[KB - 4] = ["tile", "turn", "sums" if quads else "values"]
    assert sum(fill.count("tile") for fill in FILL) == NS and NS == KB
    LOADS = 7 * 16
    LAST = UNITS - 1
    LOOPS = UNITS // SLOTS - 1

    uses, steps, counts = [], [], {"tile": 0, "turn": 0, "values": -1, "sums": -1}
    for fill in FILL:
        steps.append([])
        for kind in fill:
            n = counts[kind]
            steps[-1].append((kind, n, len(uses)))
            counts[kind] += 1
            if kind in ("tile", "turn"):
                uses.append((kind, n))
    assert uses[-2][0] == uses[-1][0] == "tile" and counts["values"] == PAIRS - 1 and counts["sums"] == SUMS - 1
    PROLOGUE = NS + 1 + LEAD

    with ExitStack() as stack:
        core = Core(nc, stack, tag)
        k_st = core.sbuf("k_st", [P, SLOTS, S], F32R)
        q_st = core.sbuf("q_st", [P, SLOTS, SQ], F32R)
        v_sb = core.sbuf("v_sb", [P, SLOTS, KB, HD])
        prob = core.sbuf("prob", [P, PR, SQ])
        pair = core.sbuf("pair", [P, PAIR_SLOTS, SQ])
        mx = core.sbuf("mx", [P, 2, NS])
        top = core.sbuf("top", [P, QB])
        rest = core.sbuf("rest", [P, 2, QB])
        parts = core.sbuf("parts", [P, QB, 3], BF16)
        o_odd = core.sbuf("o_odd", [P, CH])
        d_odd = core.sbuf("d_odd", [P, CH])
        o_sb = core.sbuf("o_sb", [P, 2, CH])
        d_sb = core.sbuf("d_sb", [P, 2, CH])
        sums_in = core.sbuf("sums_in", [P, 2, UNITS * SQ // P])
        if mask:
            neg = core.sbuf("neg", [P, QB, S], BF16)
            negT = core.sbuf("negT", [P, KB, SQ], BF16)
            live = core.sbuf("live", [P, SQ])
            junk = core.sbuf("junk", [P, NS, S], BF16)
            quad = core.sbuf("quad", [P, 2, SQ])
            pace = core.sbuf("pace", [P, NS])
        ps_s = core.psum("ps_s", [P, 2, 2, CH])
        ps_t = core.psum("ps_t", [P, 2, CH])
        ps_o = core.psum("ps_o", [P, CH])
        ps_d = core.psum("ps_d", [P, CH])
        loaded = [core.sem(f"loaded{s}") for s in range(SLOTS)]
        mask_loaded = core.sem("mask_loaded")
        minus_ones = core.sem("minus_ones")
        q_live = core.sem("q_live")
        s_ready = core.sem("s_ready")
        s_done = core.sem("s_done")
        top_chain = core.sem("top_chain")
        parts_done = core.sem("parts_done")
        row_ready = core.sem("row_ready")
        row_done = core.sem("row_done")
        t_ready = core.sem("t_ready")
        exp_done = core.sem("exp_done")
        pair_done = core.sem("pair_done")
        v_done = core.sem("v_done")
        quad_done = core.sem("quad_done")
        d_done = core.sem("d_done")
        o_half = core.sem("o_half")
        d_half = core.sem("d_half")
        o_out = core.sem("o_out")
        d_out = core.sem("d_out")
        sums_loaded = core.sem("sums_loaded")
        over_done = core.sem("over_done")
        over_stored = core.sem("over_stored")
        stored = [core.sem(f"stored{s}") for s in range(2)]
        block = stack.enter_context(nc.Block())

        def stream(i, s, n):
            return i * (SLOTS * NS) + (s * NS + n)

        EARLY = (UNITS - HEADS) * P // UNITS

        def early_sums(a):
            return a[0:UNITS - HEADS].rearrange("u (a f) -> (u a) f", a=P // UNITS)

        def exps_before(i, s, k):
            return i * (SLOTS * KB * 2) + (s * KB + k) * 2

        @block.sync
        def _(sp):
            def load(u, row, slot):
                rows = ds(row, HD)
                for part, at in ((k_hi, 0), (k_lo, 1), (k_hi, 2)):
                    sp.dma_start(k_st[at * HD:(at + 1) * HD, slot, :].bitcast(F32), part[rows, :]).then_inc(loaded[slot], 16)
                for part, at in ((q_hi, 0), (q_hi, 1), (q_lo, 2)):
                    sp.dma_start(q_st[at * HD:(at + 1) * HD, slot, :].bitcast(F32), part[rows, :]).then_inc(loaded[slot], 16)
                sp.dma_start(v_sb[:, slot].rearrange("p k d -> p (k d)"),
                             values[ds(u, 1)].rearrange("u p f -> (u p) f")).then_inc(loaded[slot], 16)

            def store(u, row, slot, i, s):
                sp.wait_ge(o_out, i * SLOTS + (s + 1 + 1))
                sp.wait_ge(d_out, i * SLOTS + (s + 1 + 1))
                for half in range(2):
                    queries = slice(half * CH, (half + 1) * CH)
                    sp.dma_start(outT[ds(row, HD), queries], o_sb[half * HD:(half + 1) * HD, slot % 2, :]).then_inc(
                        stored[slot % 2], 16)
                    sp.dma_start(sums[ds(u, 1), queries], d_sb[half * HD:half * HD + 1, slot % 2, :]).then_inc(
                        stored[slot % 2], 16)

            for slot in range(2):
                sp.sem_inc(stored[slot], 64)
            for slot in range(SLOTS):
                load(slot, slot * HD, slot)
                if mask and slot == 0:
                    sp.dma_start(live[:], mask[2]).then_inc(mask_loaded, 16)
                    sp.dma_start(neg[:], mask[0]).then_inc(mask_loaded, 16)
                    sp.dma_start(negT[:], mask[1]).then_inc(mask_loaded, 16)
            with sp.Fori(0, LOOPS) as i:
                for slot in range(SLOTS):
                    u_out, row_out = sp.snap(i * SLOTS + slot), sp.snap((i * SLOTS + slot) * HD)
                    u_in, row_in = sp.snap(i * SLOTS + slot + SLOTS), sp.snap((i * SLOTS + slot + SLOTS) * HD)
                    sp.wait_ge(v_done, i * (SLOTS * PAIRS) + ((slot + 1) * PAIRS + PR // 2))
                    load(u_in, row_in, slot)
                    store(u_out, row_out, slot, i, slot)
            flat = [early_sums(a) for a in (sums, over_sums)]
            for slot in range(2):
                sp.wait_ge(stored[slot], 64 + (UNITS - HEADS) // 2 * 64)
            sp.dma_start(sums_in[0:EARLY, 0, :], flat[0]).then_inc(sums_loaded, 16)
            for slot in range(SLOTS):
                u = LOOPS * SLOTS + slot
                store(u, u * HD, slot, LOOPS, slot)
                if slot == 1:
                    sp.wait_ge(over_done, 1)
                    sp.dma_start(flat[1], sums_in[0:EARLY, 1, :]).then_inc(over_stored, 16)
            sp.wait_ge(over_stored, 16)
            for slot in range(2):
                sp.wait_ge(stored[slot], 64 + UNITS // 2 * 64)

        @block.gpsimd
        def _(pool):
            def wipe(i, s):
                slot = s % SLOTS
                pool.wait_ge(loaded[slot], (i + s // SLOTS + 1) * LOADS)
                nc.gpsimd.tensor_tensor(q_st[0:3 * HD, slot, :], q_st[0:3 * HD, slot, :].bitcast(F32), live[0:3 * HD, :],
                                        ALU.mult).then_inc(q_live, 1)

            def add_pairs(i, s):
                for p in range(PAIRS):
                    pool.wait_ge(exp_done, exps_before(i, s, 2 * p + 2) + 2)
                    if p % 2 == 0:
                        pool.wait_ge(quad_done if quads else d_done, i * (SLOTS * BLOCKS) + (s * BLOCKS + p // 2 + 1))
                    nc.gpsimd.tensor_tensor(pair[:, p % PAIR_SLOTS, :], prob[:, 2 * p % PR, :], prob[:, (2 * p + 1) % PR, :],
                                            ALU.add).then_inc(pair_done, 1)

            def unit(i, s):
                if mask and not (isinstance(i, int) and i * SLOTS + s + 2 > LAST):
                    wipe(i, s + 2)
                add_pairs(i, s)

            pool.sem_inc(pair_done, PR // 2)
            if mask:
                pool.wait_ge(mask_loaded, 48)
                wipe(0, 0)
                wipe(0, 1)
            unit(0, 0)
            with pool.Fori(0, LOOPS) as i:
                for s in range(1, SLOTS + 1):
                    unit(i, s)
            for s in range(1, SLOTS):
                unit(LOOPS, s)

        @block.tensor
        def _(pe):
            def first_pass(at, i, s, n):
                slot, qb, half = s % SLOTS, n // HALVES, n % HALVES
                if n == 0:
                    pe.wait_ge(loaded[slot], (i + (s // SLOTS + 1)) * LOADS)
                    if mask:
                        pe.wait_ge(q_live, i * SLOTS + (s + 1))
                for j in range(2):
                    mm = nc.tensor.matmul(ps_s[:, at, j, :], q_st[0:3 * HD, slot, qb * P:(qb + 1) * P],
                                          k_st[0:3 * HD, slot, half * 1024 + j * CH:half * 1024 + (j + 1) * CH],
                                          start=True, stop=True)
                mm.then_inc(s_ready, 1)

            def turn_maxima(at, i, s):
                pe.wait_ge(parts_done, i * SLOTS + (s + 1))
                for q in range(QB):
                    mm = nc.tensor.matmul(ps_s[0:3, at, q // 4, q % 4 * P:(q % 4 + 1) * P], parts[:, q, :],
                                          const["identb"][:], start=True, stop=True)
                mm.then_inc(row_ready, 1)

            def use_tile(i, s, kind, n, x):
                ahead = 1 if kind == "turn" else 1 + (LEAD + n) // NS
                if isinstance(i, int) and i * SLOTS + s + ahead > LAST:
                    return
                before, period = (uses[x - 2], s) if x >= 2 else (uses[x - 2], s - 1)
                if before[0] == "turn":
                    pe.wait_ge(row_done, i * SLOTS + (period + 2))
                else:
                    number = stream(i, period + 1, LEAD + before[1] + 1)
                    pe.wait_ge(s_done, min(number, UNITS * NS) if isinstance(i, int) else number)
                at = (PROLOGUE + s * (NS + 1) + x) % 2
                if kind == "turn":
                    turn_maxima(at, i, s + 1)
                else:
                    first_pass(at, i, s + ahead, (LEAD + n) % NS)

            def second_pass(i, s, k):
                slot = s % SLOTS
                if k == 0:
                    pe.wait_ge(row_done, i * SLOTS + (s + 1))
                for j in range(2):
                    pe.wait_ge(exp_done, exps_before(i, s, k) + (j + 1))
                    mm = nc.tensor.matmul(ps_t[:, j, :], k_st[0:ROWS, slot, k * P:(k + 1) * P],
                                          q_st[0:ROWS, slot, j * CH:(j + 1) * CH], start=True, stop=not mask)
                    if mask:
                        mm = nc.tensor.matmul(ps_t[:, j, :], const["identb"][:], negT[:, k, j * CH:(j + 1) * CH],
                                              start=False, stop=True)
                    mm.then_inc(t_ready, 1)

            def four_at_once(out, operands, first, last, done):
                for tile in range(4):
                    left, right = operands[tile // 2]
                    half = tile % 2
                    mm = nc.tensor.matmul(out[tile * HD:(tile + 1) * HD, :], left, right[:, half * CH:(half + 1) * CH],
                                          start=first, stop=last)
                mm.then_inc(done, 1)

            def weigh_values(i, s, p):
                slot = s % SLOTS
                pe.wait_ge(exp_done, exps_before(i, s, 2 * p + 2) + 2)
                if p == 0:
                    pe.wait_ge(o_out, i * SLOTS + (s + 1))
                four_at_once(ps_o, [(v_sb[:, slot, k, :], prob[:, k % PR, :]) for k in (2 * p, 2 * p + 1)],
                             p == 0, p == PAIRS - 1, v_done)

            def sum_up(i, s, m):
                if quads:
                    pe.wait_ge(quad_done, i * (SLOTS * BLOCKS) + ((s + 1) * BLOCKS + PAIR_SLOTS // 2))
                    operands = [(const["ones"][:], quad[:, q, :]) for q in range(2)]
                else:
                    pe.wait_ge(pair_done, i * (SLOTS * PAIRS) + (s * PAIRS + 2 * m + 2 + PR // 2))
                    operands = [(const["ones"][:], pair[:, p % PAIR_SLOTS, :]) for p in (2 * m, 2 * m + 1)]
                if m == 0:
                    pe.wait_ge(d_out, i * SLOTS + (s + 1))
                four_at_once(ps_d, operands, m == 0, m == SUMS - 1, d_done)

            def unit(i, s, first=False):
                for k in range(KB):
                    second_pass(i, s, k)
                    for kind, n, x in steps[k]:
                        if kind in ("tile", "turn"):
                            use_tile(i, s, kind, n, x)
                        elif kind == "values" and (n >= 0 or not first):
                            weigh_values(i, *((s, n) if n >= 0 else (s - 1, PAIRS - 1)))
                        elif kind == "sums" and (n >= 0 or not first):
                            sum_up(i, *((s, n) if n >= 0 else (s - 1, SUMS - 1)))

            pe.sem_inc(v_done, PR // 2)
            pe.sem_inc(d_done, SUMS_FREE)
            for x in range(PROLOGUE):
                if x == NS:
                    turn_maxima(x % 2, 0, 0)
                else:
                    n = x - (x > NS)
                    if x == NS + 2:
                        pe.wait_ge(row_done, 1)
                    elif x >= 2:
                        pe.wait_ge(s_done, n - 1 if x != NS + 1 else NS)
                    first_pass(x % 2, 0, n // NS, n % NS)
            pe.wait_ge(minus_ones, SLOTS)
            if mask:
                pe.wait_ge(mask_loaded, 48)
            unit(0, 0, first=True)
            with pe.Fori(0, LOOPS) as i:
                for s in range(1, SLOTS + 1):
                    unit(i, s)
            for s in range(1, SLOTS):
                unit(LOOPS, s)
            weigh_values(LOOPS, SLOTS - 1, PAIRS - 1)
            sum_up(LOOPS, SLOTS - 1, SUMS - 1)

        @block.scalar
        def _(act):
            def exps(i, s, k):
                if k % 2 == 0:
                    act.wait_ge(v_done, i * (SLOTS * PAIRS) + (s * PAIRS + k // 2 + 1))
                    act.wait_ge(pair_done, i * (SLOTS * PAIRS) + (s * PAIRS + k // 2 + 1))
                for j in range(2):
                    act.wait_ge(t_ready, exps_before(i, s, k) + (j + 1))
                    nc.scalar.activation(prob[:, k % PR, j * CH:(j + 1) * CH], ps_t[:, j, :], ACT.Exp,
                                         scale=SCALE).then_inc(exp_done, 1)

            def maxima(at, i, s):
                act.wait_ge(row_ready, i * SLOTS + (s + 1))
                nc.scalar.activation(q_st[3 * HD:ROWS, s % SLOTS, :], ps_s[0:3, at].rearrange("p a b -> p (a b)"),
                                     ACT.Copy).then_inc(row_done, 1)

            def odd_values(i, s):
                act.wait_ge(v_done, i * (SLOTS * PAIRS) + ((s + 1) * PAIRS + PR // 2))
                act.wait_ge(o_out, i * SLOTS + (s + 1))
                nc.scalar.activation(o_odd[0:2 * HD, :], ps_o[2 * HD:4 * HD, :], ACT.Copy).then_inc(o_half, 1)

            def odd_sums(i, s):
                act.wait_ge(d_done, i * (SLOTS * SUMS) + ((s + 1) * SUMS + SUMS_FREE))
                act.wait_ge(d_out, i * SLOTS + (s + 1))
                nc.scalar.activation(d_odd[0:2 * HD, :], ps_d[2 * HD:4 * HD, :], ACT.Copy).then_inc(d_half, 1)

            def unit(i, s, first=False):
                for k in range(KB):
                    if k == 1 and not first:
                        odd_values(i, s - 1)
                    exps(i, s, k)
                    if k == SUMS_STEP + 1 and not first:
                        odd_sums(i, s - 1)
                    if k == KB - 4 and not (isinstance(i, int) and i * SLOTS + s + 1 > LAST):
                        at = (PROLOGUE + s * (NS + 1) + uses.index(("turn", 0))) % 2
                        maxima(at, i, s + 1)

            act.sem_inc(exp_done, 2)
            maxima(NS % 2, 0, 0)
            unit(0, 0, first=True)
            with act.Fori(0, LOOPS) as i:
                for s in range(1, SLOTS + 1):
                    unit(i, s)
            for s in range(1, SLOTS):
                unit(LOOPS, s)
            odd_values(LOOPS, SLOTS - 1)
            odd_sums(LOOPS, SLOTS - 1)

        @block.vector
        def _(dve):
            CHAIN = 5

            def tile_max(at, i, s, n):
                dve.wait_ge(s_ready, stream(i, s, n + 1))
                tile = ps_s[:, at].rearrange("p a b -> p (a b)")
                to = mx[:, s % 2, n:n + 1]
                if mask:
                    nc.vector.memset(pace[:, n:n + 1], 0.0)
                    nc.vector.tensor_tensor_reduce(out=junk[:, n, :], in0=tile, in1=neg[:, n, :], scale=1.0, scalar=LOWEST,
                                                   op0=ALU.add, op1=ALU.max, accum_out=to).then_inc(s_done, 1)
                else:
                    nc.vector.reduce_max(to, tile, AX.X).then_inc(s_done, 1)

            def split_maxima(i, s):
                at = i * (SLOTS * CHAIN) + s * CHAIN
                dve.wait_ge(s_done, stream(i, s, NS))
                halves = mx[:, s % 2].rearrange("p (q h) -> p q h", h=HALVES)
                nc.vector.tensor_tensor(top[:], halves[:, :, 0], halves[:, :, HALVES - 1], ALU.max).then_inc(top_chain, 1)
                dve.wait_ge(top_chain, at + 1)
                nc.vector.tensor_copy(parts[:, :, 0], top[:]).then_inc(top_chain, 1)
                dve.wait_ge(top_chain, at + 2)
                nc.vector.tensor_tensor(rest[:, 0], top[:], parts[:, :, 0], ALU.subtract).then_inc(top_chain, 1)
                dve.wait_ge(top_chain, at + 3)
                nc.vector.tensor_copy(parts[:, :, 1], rest[:, 0]).then_inc(top_chain, 1)
                dve.wait_ge(top_chain, at + 4)
                nc.vector.tensor_tensor(rest[:, 1], rest[:, 0], parts[:, :, 1], ALU.subtract).then_inc(top_chain, 1)
                dve.wait_ge(top_chain, at + 5)
                nc.vector.tensor_copy(parts[:, :, 2], rest[:, 1]).then_inc(parts_done, 1)

            def outputs(i, s):
                slot = s % 2
                dve.wait_ge(o_half, i * SLOTS + (s + 1))
                dve.wait_ge(stored[slot], i * (SLOTS // 2 * 64) + (s // 2 * 64 + 64))
                nc.vector.tensor_tensor(o_sb[0:2 * HD, slot, :], ps_o[0:2 * HD, :], o_odd[0:2 * HD, :], ALU.add).then_inc(o_out, 1)

            def outputs_sums(i, s):
                dve.wait_ge(d_half, i * SLOTS + (s + 1))
                nc.vector.tensor_tensor(d_sb[0:2 * HD, s % 2, :], ps_d[0:2 * HD, :], d_odd[0:2 * HD, :], ALU.add).then_inc(d_out, 1)

            def add_quad(i, s, m):
                dve.wait_ge(pair_done, i * (SLOTS * PAIRS) + (s * PAIRS + 2 * m + 2 + PR // 2))
                if m == 0:
                    dve.wait_ge(d_done, i * SLOTS + (s + 1))
                nc.vector.tensor_tensor(quad[:, m, :], pair[:, 2 * m, :], pair[:, 2 * m + 1, :], ALU.add).then_inc(quad_done, 1)

            def use_tile(i, s, n, x):
                ahead = 1 + (LEAD + n) // NS
                if isinstance(i, int) and i * SLOTS + s + ahead > LAST:
                    return
                tile_max((PROLOGUE + s * (NS + 1) + x) % 2, i, s + ahead, (LEAD + n) % NS)
                if (LEAD + n) % NS == NS - 1:
                    split_maxima(i, s + ahead)

            def unit(i, s, first=False):
                for k in range(KB):
                    if quads and k == 3 and not first:
                        add_quad(i, s - 1, 1)
                    if k == SUMS_STEP + 2 and not first:
                        outputs_sums(i, s - 1)
                    if quads and k == KB - 1:
                        add_quad(i, s, 0)
                    for kind, n, x in steps[k]:
                        if kind == "tile":
                            use_tile(i, s, n, x)
                        if k == 1 and x == steps[k][0][2] and not first:
                            outputs(i, s - 1)

            dve.sem_inc(o_out, 1)
            dve.sem_inc(d_out, 1)
            if quads:
                dve.sem_inc(quad_done, PAIR_SLOTS // 2)
            for slot in range(SLOTS):
                nc.vector.memset(k_st[3 * HD:ROWS, slot, :].bitcast(F32), -1.0).then_inc(minus_ones, 1)
            if mask:
                dve.wait_ge(mask_loaded, 48)
            for x in range(PROLOGUE):
                n = x - (x > NS)
                if x != NS:
                    tile_max(x % 2, 0, n // NS, n % NS)
                    if n == NS - 1:
                        split_maxima(0, 0)
            unit(0, 0, first=True)
            with dve.Fori(0, LOOPS) as i:
                for s in range(1, SLOTS + 1):
                    unit(i, s)
            for s in range(1, SLOTS):
                unit(LOOPS, s)
                if s == 1:
                    dve.wait_ge(sums_loaded, 16)
                    nc.vector.reciprocal(sums_in[0:EARLY, 1, :], sums_in[0:EARLY, 0, :]).then_inc(over_done, 1)
            outputs(LOOPS, SLOTS - 1)
            if quads:
                add_quad(LOOPS, SLOTS - 1, 1)
            outputs_sums(LOOPS, SLOTS - 1)


class RowNorm:

    def __init__(self, nc, core, gain, shift, rows_ready, per_chunk, credit, vector_rows):
        self.nc, self.gain, self.shift = nc, gain, shift
        self.rows_ready, self.per_chunk, self.credit = rows_ready, per_chunk, credit
        self.vector_rows = vector_rows
        self.g_row = core.sbuf("g_row", [P, D])
        self.s_row = core.sbuf("s_row", [P, D])
        self.stats = core.sbuf("stats", [P, RT, 6])
        self.mv = core.sbuf("mv", [P, RT, 2])
        self.eps = core.sbuf("eps", [P, 1])
        self.pace = core.sbuf("pace", [P, 8])
        self.std = core.sbuf("std", [P, RT])
        self.rstd = core.sbuf("rstd", [P, RT])
        self.loaded = core.sem("norm_loaded")
        self.eps_set = core.sem("norm_eps_set")
        self.stats_done = core.sem("norm_stats")
        self.var_done = core.sem("norm_var")
        self.std_done = core.sem("norm_std")
        self.rstd_done = core.sem("norm_rstd")
        self.centred = core.sem("norm_centred")
        self.gained = core.sem("norm_gained")
        self.done = core.sem("norm_done")
        self.v_gained = core.sem("norm_v_gained")
        self.v_done = core.sem("norm_v_done")

    def sync_start(self, sp):
        sp.dma_start(self.g_row[:], row_bias(self.gain)).then_inc(self.loaded, 16)
        sp.dma_start(self.s_row[:], row_bias(self.shift)).then_inc(self.loaded, 16)

    def vector_start(self, dve):
        if self.vector_rows:
            dve.wait_ge(self.loaded, 32)
        self.nc.vector.memset(self.eps[:], EPS).then_inc(self.eps_set, 1)

    def scalar_start(self, act):
        act.wait_ge(self.eps_set, 1)

    def row_stats(self, dve, y, c, r):
        dve.wait_ge(self.rows_ready, c * self.per_chunk + (self.credit + self.per_chunk - RT + r + 1))
        self.nc.vector.bn_stats(self.stats[:, r, :], y[:, r, :]).then_inc(self.stats_done, 1)

    def vector(self, dve, y, c):
        nc = self.nc
        dve.wait_ge(self.stats_done, (c + 1) * RT)
        nc.vector.memset(self.pace[:], 0.0)
        for r in range(RT):
            nc.vector.bn_aggr(self.mv[:, r, :], self.stats[:, r, :]).then_inc(self.var_done, 1)
        dve.wait_ge(self.std_done, c + 1)
        nc.vector.reciprocal(self.rstd[:], self.std[:]).then_inc(self.rstd_done, 1)
        dve.wait_ge(self.rstd_done, c + 1)
        for r in range(RT):
            nc.vector.tensor_scalar(y[:, r, :], y[:, r, :], self.mv[:, r, 0:1], self.rstd[:, r:r + 1], ALU.subtract,
                                    ALU.mult).then_inc(self.centred, 1)
        for r in range(RT - self.vector_rows, RT):
            dve.wait_ge(self.centred, c * RT + (r + 1))
            nc.vector.tensor_tensor(y[:, r, :], y[:, r, :], self.g_row[:], ALU.mult).then_inc(self.v_gained, 1)
        for r in range(self.vector_rows):
            dve.wait_ge(self.v_gained, c * self.vector_rows + (r + 1))
            row = RT - self.vector_rows + r
            nc.vector.tensor_tensor(y[:, row, :], y[:, row, :], self.s_row[:], ALU.add).then_inc(self.v_done, 1)

    def scalar(self, act, c):
        act.wait_ge(self.var_done, c * RT + RT)
        self.nc.scalar.activation(self.std[:], self.mv[:, :, 1], ACT.Sqrt, bias=self.eps[:, 0:1]).then_inc(self.std_done, 1)

    def pool(self, pool, y, c):
        rows = RT - self.vector_rows
        pool.wait_ge(self.loaded, 32)
        for r in range(rows):
            pool.wait_ge(self.centred, c * RT + r + 1)
            self.nc.gpsimd.tensor_tensor(y[:, r, :], y[:, r, :], self.g_row[:], ALU.mult).then_inc(self.gained, 1)
            pool.wait_ge(self.gained, c * rows + (r + 1))
            self.nc.gpsimd.tensor_tensor(y[:, r, :], y[:, r, :], self.s_row[:], ALU.add).then_inc(self.done, 1)

    def wait_done(self, engine, c):
        engine.wait_ge(self.done, (c + 1) * (RT - self.vector_rows))
        if self.vector_rows:
            engine.wait_ge(self.v_done, (c + 1) * self.vector_rows)


def close_attention(nc, const, tag, oT, sums, over_sums, w, bias, residual, norm, out):
    CB = SQ // CH
    CHUNKS = B * CB
    LATE = HEADS * P // UNITS
    with ExitStack() as stack:
        core = Core(nc, stack, tag)
        w_stage = core.sbuf("w_stage", [P, KT, D])
        w_hi = core.sbuf("w_hi", [P, KT, D], F32R)
        w_lo = core.sbuf("w_lo", [P, KT, D], F32R)
        b_row = core.sbuf("b_row", [P, D])
        sums_in = core.sbuf("sums_in", [P, 2, UNITS * SQ // P])
        o_hi = core.sbuf("o_hi", [P, CHUNKS, KT, CH], F32R)
        o_lo = core.sbuf("o_lo", [P, CHUNKS, KT, CH], F32R)
        o = core.sbuf("o", [P, 2, KT, CH])
        y = core.sbuf("y", [P, CHUNKS, RT, D])
        ps_y = core.psum("ps_y", [P, 8, CH])
        w_loaded = core.sem("w_loaded")
        b_loaded = core.sem("b_loaded")
        w_hi_done = core.sem("w_hi_done")
        w_done = core.sem("w_done")
        o_loaded = [core.sem(f"o_loaded{c}") for c in range(CHUNKS)]
        y_loaded = [core.sem(f"y_loaded{c}") for c in range(CHUNKS)]
        over_loaded = [core.sem(f"over_loaded{c}") for c in range(CHUNKS)]
        sums_loaded = core.sem("sums_loaded")
        over_done = core.sem("over_done")
        over_stored = core.sem("over_stored")
        o_divided = core.sem("o_divided")
        o_hi_done = core.sem("o_hi_done")
        o_done = core.sem("o_done")
        biased = core.sem("biased")
        y_ready = core.sem("y_ready")
        y_done = core.sem("y_done")
        stored = core.sem("stored")
        row_norm = RowNorm(nc, core, *norm, y_done, RT, 8, 2) if norm else None
        block = stack.enter_context(nc.Block())

        @block.sync
        def _(sp):
            flat = [a[UNITS - HEADS:UNITS].rearrange("u (a f) -> (u a) f", a=P // UNITS) for a in (sums, over_sums)]

            def load_outputs(c):
                b, j = divmod(c, CB)
                sp.dma_start(o_lo[:, c].bitcast(F32),
                             oT[b * D:(b + 1) * D, j * CH:(j + 1) * CH].rearrange("(k p) q -> p k q", p=P)).then_inc(o_loaded[c], 16)

            def load_over(c):
                b, j = divmod(c, CB)
                by_head = over_sums[b * HEADS:(b + 1) * HEADS, j * CH:(j + 1) * CH].rearrange("(k h) q -> h k q", h=P // HD)
                for h in range(P // HD):
                    sp.dma_start(o_hi[h * HD:(h + 1) * HD, c].bitcast(F32),
                                 by_head[h:h + 1].broadcast_to([HD, KT, CH])).then_inc(over_loaded[c], 16)

            sp.dma_start(w_stage[:], w.rearrange("(k p) n -> p k n", p=P)).then_inc(w_loaded, 16)
            load_outputs(0)
            load_over(0)
            sp.dma_start(sums_in[0:LATE, 0, :], flat[0]).then_inc(sums_loaded, 16)
            sp.dma_start(b_row[:], row_bias(bias)).then_inc(b_loaded, 16)
            for c in range(CHUNKS):
                if c == 1:
                    sp.wait_ge(over_done, 1)
                    sp.dma_start(flat[1], sums_in[0:LATE, 1, :]).then_inc(over_stored, 16)
                    if norm:
                        row_norm.sync_start(sp)
                if c > 0:
                    load_outputs(c)
                    if c == CHUNKS - CB:
                        sp.wait_ge(over_stored, 16)
                    load_over(c)
                sp.dma_start(y[:, c], residual[c * CH:(c + 1) * CH, :].rearrange("(r p) d -> p r d", p=P)).then_inc(
                    y_loaded[c], 16)

        @block.tensor
        def _(pe):
            pe.wait_ge(w_done, 1)
            for c in range(CHUNKS):
                pe.wait_ge(o_done, c + 1)
                for r in range(RT):
                    pe.wait_ge(y_done, c * RT + r + 1)
                    rows = slice(r * P, (r + 1) * P)
                    for k in range(KT):
                        for i, (stationary, moving) in enumerate(((o_hi[:, c, k, rows], w_hi[:, k, :]),
                                                                  (o_hi[:, c, k, rows], w_lo[:, k, :]),
                                                                  (o_lo[:, c, k, rows], w_hi[:, k, :]))):
                            mm = nc.tensor.matmul(ps_y[:, c % 2 * RT + r, :], stationary, moving, start=(k == 0 and i == 0),
                                                  stop=(k == KT - 1 and i == 2))
                    mm.then_inc(y_ready, 1)

        @block.scalar
        def _(act):
            act.wait_ge(w_loaded, 16)
            nc.scalar.activation(w_hi[:], w_stage[:], ACT.Copy).then_inc(w_hi_done, 1)
            for c in range(CHUNKS + 2):
                if c < CHUNKS:
                    act.wait_ge(o_divided, c + 1)
                    nc.scalar.activation(o_hi[:, c], o[:, c % 2], ACT.Copy).then_inc(o_hi_done, 1)
                if norm and c == 1:
                    row_norm.scalar_start(act)
                if norm and c >= 2:
                    row_norm.scalar(act, c - 2)

        @block.vector
        def _(dve):
            def divide(c):
                dve.wait_ge(o_loaded[c], 16)
                dve.wait_ge(over_loaded[c], 16 * (P // HD))
                if c >= 2:
                    dve.wait_ge(o_done, c - 1)
                nc.vector.tensor_tensor(o[:, c % 2], o_lo[:, c].bitcast(F32), o_hi[:, c].bitcast(F32),
                                        ALU.mult).then_inc(o_divided, 1)

            def low_part(c):
                dve.wait_ge(o_hi_done, c + 1)
                nc.vector.tensor_tensor(o_lo[:, c], o[:, c % 2], o_hi[:, c].bitcast(F32), ALU.subtract).then_inc(o_done, 1)

            def add_residual(c):
                dve.wait_ge(biased, c + 1)
                for r in range(RT):
                    dve.wait_ge(y_ready, c * RT + r + 1)
                    nc.vector.tensor_tensor(y[:, c, r, :], ps_y[:, c % 2 * RT + r, :], y[:, c, r, :], ALU.add).then_inc(y_done, 1)
                    if norm:
                        row_norm.row_stats(dve, y[:, c], c, r)

            def normalise(c):
                if norm:
                    row_norm.vector(dve, y[:, c], c)

            dve.sem_inc(y_done, 8)
            dve.wait_ge(w_hi_done, 1)
            nc.vector.tensor_tensor(w_lo[:], w_stage[:], w_hi[:].bitcast(F32), ALU.subtract).then_inc(w_done, 1)
            divide(0)
            dve.wait_ge(sums_loaded, 16)
            nc.vector.reciprocal(sums_in[0:LATE, 1, :], sums_in[0:LATE, 0, :]).then_inc(over_done, 1)
            low_part(0)
            divide(1)
            if norm:
                row_norm.vector_start(dve)
            low_part(1)
            for c in range(2, CHUNKS):
                divide(c)
                add_residual(c - 2)
                low_part(c)
                normalise(c - 2)
            for c in range(CHUNKS - 2, CHUNKS):
                add_residual(c)
                normalise(c)

        @block.gpsimd
        def _(pool):
            pool.wait_ge(b_loaded, 16)
            for c in range(CHUNKS):
                pool.wait_ge(y_loaded[c], 16)
                nc.gpsimd.tensor_tensor(y[:, c], y[:, c], b_row[:].unsqueeze(1).broadcast_to([P, RT, D]), ALU.add).then_inc(
                    biased, 1)
            for c in range(CHUNKS):
                if norm:
                    row_norm.pool(pool, y[:, c], c)
                    row_norm.wait_done(pool, c)
                else:
                    pool.wait_ge(y_done, (c + 1) * RT + 8)
                pool.dma_start(out[c * CH:(c + 1) * CH, :].rearrange("(r p) d -> p r d", p=P), y[:, c]).then_inc(stored, 16)
            pool.wait_ge(stored, CHUNKS * 16)


def feed_forward(nc, const, tag, src, w1, b1, w2, b2, function, norm, out):
    CB = SQ // CH
    F = w1.shape[1]
    FT = F // P
    WP = 8
    STAGES = 4
    PIECE = F * KT // WP
    HR = 3
    with ExitStack() as stack:
        core = Core(nc, stack, tag)
        w_stage = core.sbuf("w_stage", [P, STAGES, PIECE])
        w1_hi = core.sbuf("w1_hi", [P, KT, F], F32R)
        w1_lo = core.sbuf("w1_lo", [P, KT, F], F32R)
        w2_hi = core.sbuf("w2_hi", [P, FT, D], F32R)
        w2_lo = core.sbuf("w2_lo", [P, FT, D], F32R)
        b1_col = core.sbuf("b1_col", [P, FT])
        b2_row = core.sbuf("b2_row", [P, D])
        y = core.sbuf("y", [P, 2, RT, D])
        xT_hi = core.sbuf("xT_hi", [P, KT, CH], F32R)
        xT_lo = core.sbuf("xT_lo", [P, KT, CH], F32R)
        h = core.sbuf("h", [P, 2, CH])
        h_hi = core.sbuf("h_hi", [P, HR, CH], F32R)
        h_lo = core.sbuf("h_lo", [P, HR, CH], F32R)
        ps_x = core.psum("ps_x", [P, 2, CH])
        ps_h = core.psum("ps_h", [P, 2, CH])
        ps_y = core.psum("ps_y", [P, RT, D])
        w_loaded = [core.sem(f"w_loaded{n}") for n in range(STAGES)]
        b1_loaded = core.sem("b1_loaded")
        b2_loaded = core.sem("b2_loaded")
        w1_hi_done = core.sem("w1_hi_done")
        w1_done = core.sem("w1_done")
        w2_hi_done = core.sem("w2_hi_done")
        w2_done = core.sem("w2_done")
        x_loaded = [core.sem(f"x_loaded{s}") for s in range(2)]
        x_turned = core.sem("x_turned")
        x_hi_done = core.sem("x_hi_done")
        x_done = core.sem("x_done")
        biased = core.sem("biased")
        h_ready = core.sem("h_ready")
        h_act_done = core.sem("h_act_done")
        h_done = core.sem("h_done")
        h_used = core.sem("h_used")
        y_done = core.sem("y_done")
        stored = [core.sem(f"stored{s}") for s in range(2)]
        row_norm = RowNorm(nc, core, *norm, y_done, RT, RT, 0) if norm else None
        block = stack.enter_context(nc.Block())
        NP = 2 * WP

        def piece(n):
            if n < WP:
                k, part = n * KT // WP, n % (WP // KT)
                cols = slice(part * PIECE, (part + 1) * PIECE)
                return w1[k * P:(k + 1) * P, cols], w1_hi[:, k, cols], w1_lo[:, k, cols]
            n -= WP
            per = FT // WP
            return (w2[n * per * P:(n + 1) * per * P, :].rearrange("(k p) d -> p k d", p=P),
                    w2_hi[:, n * per:(n + 1) * per, :].rearrange("p k d -> p (k d)"),
                    w2_lo[:, n * per:(n + 1) * per, :].rearrange("p k d -> p (k d)"))

        def hidden_slot(t):
            return t % HR

        @block.sync
        def _(sp):
            with nc.allow_non_contiguous_dma(reason="a bias, one element per partition"):
                sp.dma_start(b1_col[:], b1.rearrange("(t p) -> p t", p=P)).then_inc(b1_loaded, 16)
            sp.dma_start(b2_row[:], row_bias(b2)).then_inc(b2_loaded, 16)
            if norm:
                row_norm.sync_start(sp)

            def load_rows(b, j):
                row = (b * CB + j) * CH
                sp.dma_start(y[:, j], src[row:row + CH, :].rearrange("(r p) d -> p r d", p=P)).then_inc(
                    x_loaded[j], 16)

            load_rows(0, 0)
            for n in range(NP):
                if n == WP:
                    load_rows(0, 1)
                if n >= STAGES:
                    before = n - STAGES + 1
                    sp.wait_ge(*((w1_done, before) if before <= WP else (w2_done, before - WP)))
                to = w_stage[:, n % STAGES]
                sp.dma_start(to if n < WP else to.rearrange("p (k d) -> p k d", d=D), piece(n)[0]).then_inc(
                    w_loaded[n % STAGES], 16)
            for b in range(1, B):
                for j in range(CB):
                    sp.wait_ge(stored[j], b * 16)
                    load_rows(b, j)

        def before(b, j, per):
            return b * (CB * per) + j * per

        def all_chunks(engine, chunk):
            with engine.Fori(0, B - 1) as b:
                for j in range(CB):
                    chunk(b, j, False)
            for j in range(CB):
                chunk(B - 1, j, j == CB - 1)

        @block.tensor
        def _(pe):
            def turn(b, j, k):
                if k == 0:
                    pe.wait_ge(x_loaded[j % CB], (b + (j // CB + 1)) * 16)
                pe.wait_ge(x_done, before(b, j, KT) + (k + 1))
                for r in range(RT):
                    mm = nc.tensor.transpose(ps_x[:, k % 2, r * P:(r + 1) * P], y[:, j % CB, r, k * P:(k + 1) * P],
                                             const["ident"][:])
                mm.then_inc(x_turned, 1)

            def chunk(b, j, last):
                pe.wait_ge(x_done, before(b, j, KT) + (KT + 2))

                def hidden(t):
                    pe.wait_ge(w1_done, WP)
                    pe.wait_ge(h_act_done, before(b, j, 2 * FT) + (2 * t + 1))
                    cols = slice(t * P, (t + 1) * P)
                    for k in range(KT):
                        for i, (stationary, moving) in enumerate(((w1_hi[:, k, cols], xT_hi[:, k, :]),
                                                                  (w1_lo[:, k, cols], xT_hi[:, k, :]),
                                                                  (w1_hi[:, k, cols], xT_lo[:, k, :]))):
                            mm = nc.tensor.matmul(ps_h[:, t % 2, :], stationary, moving, start=(k == 0 and i == 0),
                                                  stop=(k == KT - 1 and i == 2))
                    mm.then_inc(h_ready, 1)

                def output(t):
                    pe.wait_ge(h_done, before(b, j, FT) + (t + 1 + 2))
                    s = hidden_slot(t)
                    pe.wait_ge(w2_done, t // (FT // WP) + 1)
                    for r in range(RT):
                        if t == 0:
                            pe.wait_ge(y_done, before(b, j, RT) + (r + 1))
                        rows = slice(r * P, (r + 1) * P)
                        for i, (stationary, moving) in enumerate(((h_hi[:, s, rows], w2_hi[:, t, :]),
                                                                  (h_hi[:, s, rows], w2_lo[:, t, :]),
                                                                  (h_lo[:, s, rows], w2_hi[:, t, :]))):
                            mm = nc.tensor.matmul(ps_y[:, r, :], stationary, moving, start=(t == 0 and i == 0),
                                                  stop=(t == FT - 1 and i == 2))
                    mm.then_inc(h_used, 1)

                for t in range(FT):
                    hidden(t)
                    if t == FT - 1 and not last:
                        turn(b, j + 1, 0)
                        turn(b, j + 1, 1)
                    if t > 0:
                        output(t - 1)
                if not last:
                    turn(b, j + 1, 2)
                    turn(b, j + 1, 3)
                output(FT - 1)

            for k in range(KT):
                turn(0, 0, k)
            all_chunks(pe, chunk)

        @block.scalar
        def _(act):
            act.sem_inc(h_act_done, 3)
            for n in range(WP):
                act.wait_ge(w_loaded[n % STAGES], (n // STAGES + 1) * 16)
                nc.scalar.activation(piece(n)[1], w_stage[:, n % STAGES], ACT.Copy).then_inc(w1_hi_done, 1)
            act.wait_ge(b1_loaded, 16)
            if norm:
                row_norm.scalar_start(act)

            def keep_turned(b, j):
                for k in range(KT):
                    act.wait_ge(x_turned, before(b, j, KT) + (k + 1))
                    nc.scalar.activation(xT_hi[:, k, :], ps_x[:, k % 2, :], ACT.Copy).then_inc(x_hi_done, 1)

            def chunk(b, j, last):
                for t in range(FT):
                    s = hidden_slot(t)
                    act.wait_ge(h_ready, before(b, j, FT) + (t + 1))
                    act.wait_ge(h_used, before(b, j, FT) + (t + 1))
                    nc.scalar.activation(h_hi[:, s, :], ps_h[:, t % 2, :], function, bias=b1_col[:, t:t + 1]).then_inc(
                        h_act_done, 1)
                    act.wait_ge(h_done, before(b, j, FT) + (t + 1))
                    nc.scalar.activation(h[:, t % 2, :], ps_h[:, t % 2, :], function, bias=b1_col[:, t:t + 1]).then_inc(
                        h_act_done, 1)
                if not last:
                    keep_turned(b, j + 1)
                if norm:
                    row_norm.scalar(act, before(b, j, 1))

            keep_turned(0, 0)
            all_chunks(act, chunk)

        @block.vector
        def _(dve):
            dve.sem_inc(x_done, 2)
            dve.sem_inc(y_done, RT)
            dve.sem_inc(h_done, 2)
            if norm:
                row_norm.vector_start(dve)
            for n in range(WP):
                dve.wait_ge(w1_hi_done, n + 1)
                _, hi, lo = piece(n)
                nc.vector.tensor_tensor(lo, w_stage[:, n % STAGES], hi.bitcast(F32), ALU.subtract).then_inc(w1_done, 1)

            def keep_turned(b, j):
                for k in range(KT):
                    dve.wait_ge(x_hi_done, before(b, j, KT) + (k + 1))
                    nc.vector.tensor_tensor(xT_lo[:, k, :], ps_x[:, k % 2, :], xT_hi[:, k, :].bitcast(F32),
                                            ALU.subtract).then_inc(x_done, 1)

            def chunk(b, j, last):
                for t in range(FT):
                    dve.wait_ge(h_act_done, before(b, j, 2 * FT) + (2 * t + 2 + 3))
                    nc.vector.tensor_tensor(h_lo[:, hidden_slot(t), :], h[:, t % 2, :],
                                            h_hi[:, hidden_slot(t), :].bitcast(F32), ALU.subtract).then_inc(h_done, 1)
                if not last:
                    keep_turned(b, j + 1)
                dve.wait_ge(biased, before(b, j, 1) + 1)
                dve.wait_ge(h_used, before(b, j, FT) + (FT + HR))
                for r in range(RT):
                    nc.vector.tensor_tensor(y[:, j, r, :], ps_y[:, r, :], y[:, j, r, :], ALU.add).then_inc(y_done, 1)
                if norm:
                    for r in range(RT):
                        row_norm.row_stats(dve, y[:, j], before(b, j, 1), r)
                    row_norm.vector(dve, y[:, j], before(b, j, 1))

            keep_turned(0, 0)
            all_chunks(dve, chunk)

        @block.gpsimd
        def _(pool):
            pool.sem_inc(h_used, HR)
            for n in range(WP, NP):
                _, hi, lo = piece(n)
                pool.wait_ge(w_loaded[n % STAGES], (n // STAGES + 1) * 16)
                nc.gpsimd.tensor_copy(hi, w_stage[:, n % STAGES]).then_inc(w2_hi_done, 1)
                pool.wait_ge(w2_hi_done, n - WP + 1)
                nc.gpsimd.tensor_tensor(lo, w_stage[:, n % STAGES], hi.bitcast(F32), ALU.subtract).then_inc(w2_done, 1)
            pool.wait_ge(b2_loaded, 16)
            with pool.Fori(0, B) as b:
                for j in range(CB):
                    c = b * CB + j
                    pool.wait_ge(x_turned, (c + 1) * KT)
                    nc.gpsimd.tensor_tensor(y[:, j], y[:, j], b2_row[:].unsqueeze(1).broadcast_to([P, RT, D]), ALU.add).then_inc(
                        biased, 1)
                    if norm:
                        row_norm.pool(pool, y[:, j], c)
                        row_norm.wait_done(pool, c)
                    else:
                        pool.wait_ge(y_done, (c + 1) * RT + RT)
                    pool.dma_start(out[ds(pool.snap(c * CH), CH), :].rearrange("(r p) d -> p r d", p=P), y[:, j]).then_inc(stored[j], 16)
            for j in range(CB):
                pool.wait_ge(stored[j], B * 16)


_INS = ["x", "ctx_1024", "mask_1x1xSxS_ik0"] + [f"L0_xattn_{n}" for n in
        ("Wq", "bq", "Wk", "bk", "Wv", "bv", "Wo", "bo", "W1", "b1", "W2", "b2")] + [f"L1_xattn_{n}" for n in
        ("sa_qw", "sa_qb", "sa_kw", "sa_kb", "sa_vw", "sa_vb", "sa_ow", "sa_ob", "ca_qw", "ca_qb", "ca_kw", "ca_kb",
         "ca_vw", "ca_vb", "ca_ow", "ca_ob", "w1", "b1", "w2", "b2", "g1", "be1", "g2", "be2", "g3", "be3")]


def build_program(nc, ins, out):
    x = ins["x"].rearrange("b s d -> (b s) d")
    context = ins["ctx_1024"].rearrange("b s d -> (b s) d")
    mask = ins["mask_1x1xSxS_ik0"].rearrange("a b q k -> (a b q) k")
    out_rows = out.rearrange("b s d -> (b s) d")
    p = {n.removeprefix("L0_xattn_"): a for n, a in ins.items() if n.startswith("L0_")}
    t = {n.removeprefix("L1_xattn_"): a for n, a in ins.items() if n.startswith("L1_")}
    SC = ins["ctx_1024"].shape[1]

    def dram(name, shape, dtype=F32):
        return nc.dram_tensor(name, shape, dtype).ap()

    def keys(name, s):
        return dram(f"{name}_hi", (B * D, s)), dram(f"{name}_lo", (B * D, s))

    k0, k2, k1 = keys("k0", SC), keys("k2", SC), keys("k1", SQ)
    q0, q1, q2 = keys("q0", SQ), keys("q1", SQ), keys("q2", SQ)
    v0, v2 = (dram(n, (UNITS, P, SC // P * HD)) for n in ("v0", "v2"))
    v1 = dram("v1", (UNITS, P, SQ // P * HD))
    o0, o1, o2 = ((dram(n, (B * D, SQ)), dram(f"{n}_sums", (UNITS, SQ))) for n in ("o0", "o1", "o2"))
    over = [dram(f"over_sums{n}", (UNITS, SQ)) for n in range(3)]
    rows = [dram(f"rows{n}", (B * SQ, D)) for n in range(4)]
    T = SQ // P
    neg, negT = dram("neg", (P, T, SQ), BF16), dram("negT", (P, T, SQ), BF16)
    live = dram("live", (P, SQ))

    with ExitStack() as stack:
        const = {
            "ident": stack.enter_context(nc.sbuf_tensor("ident", [P, P], F32)),
            "identb": stack.enter_context(nc.sbuf_tensor("identb", [P, P], BF16)),
            "ones": stack.enter_context(nc.sbuf_tensor("ones", [P, HD], F32)),
        }
        make_identities(nc, const)
        project(nc, const, "ctx0", context, SC // CH, [
            ("T", p["Wk"], p["bk"], *k0), ("V", p["Wv"], p["bv"], v0),
            ("T", t["ca_kw"], t["ca_kb"], *k2), ("V", t["ca_vw"], t["ca_vb"], v2)], (mask, neg, negT, live))
        project(nc, const, "query0", x, SQ // CH, [("T", p["Wq"], p["bq"], *q0)])
        attention(nc, const, "attn0", *k0, *q0, v0, *o0, over[0])
        close_attention(nc, const, "close0", *o0, over[0], p["Wo"], p["bo"], x, None, rows[0])
        feed_forward(nc, const, "ff0", rows[0], p["W1"], p["b1"], p["W2"], p["b2"], ACT.Gelu_apprx_tanh, None, rows[1])
        project(nc, const, "self", rows[1], SQ // CH, [("T", t["sa_qw"], t["sa_qb"], *q1), ("T", t["sa_kw"], t["sa_kb"], *k1),
                                                       ("V", t["sa_vw"], t["sa_vb"], v1)])
        attention(nc, const, "attn1", *k1, *q1, v1, *o1, over[1], (neg, negT, live))
        close_attention(nc, const, "close1", *o1, over[1], t["sa_ow"], t["sa_ob"], rows[1], (t["g1"], t["be1"]), rows[2])
        project(nc, const, "query2", rows[2], SQ // CH, [("T", t["ca_qw"], t["ca_qb"], *q2)])
        attention(nc, const, "attn2", *k2, *q2, v2, *o2, over[2])
        close_attention(nc, const, "close2", *o2, over[2], t["ca_ow"], t["ca_ob"], rows[2], (t["g2"], t["be2"]), rows[3])
        feed_forward(nc, const, "ff1", rows[3], t["w1"], t["b1"], t["w2"], t["b2"], ACT.Relu, (t["g3"], t["be3"]), out_rows)


def kernel(**inputs):
    import numpy as _np
    import concourse.bacc as _bacc
    from concourse import mybir as _mybir
    from concourse.bass_utils import run_bass_kernel_spmd as _run

    nc = _bacc.Bacc("TRN2", target_bir_lowering=False, num_devices=1)
    arrays, aps = {}, {}
    for name in _INS:
        a = _np.ascontiguousarray(inputs[name])
        arrays[f"in_{name}"] = a
        aps[name] = nc.dram_tensor(f"in_{name}", a.shape, _mybir.dt.from_np(a.dtype), kind="ExternalInput").ap()
    shape = tuple(inputs["x"].shape)
    out = nc.dram_tensor("out_rows", shape, F32, kind="ExternalOutput").ap()
    build_program(nc, aps, out)
    r = _run(nc, [arrays], core_ids=[0])
    return r.results[0]["out_rows"]
```
